# Optimizing a Trainium2 kernel written in Bass

```python
import numpy as np
import jax
import jax.numpy as jnp

def _softmax(x, axis=-1):
    return jax.nn.softmax(x, axis=axis)

def _gelu(x):
    return jax.nn.gelu(x, approximate=True)

def _silu(x):
    return jax.nn.silu(x)

def _sigmoid(x):
    return jax.nn.sigmoid(x)

def _layernorm(x, axis=-1, eps=1e-05):
    m = jnp.mean(x, axis=axis, keepdims=True)
    v = jnp.var(x, axis=axis, keepdims=True)
    return (x - m) / jnp.sqrt(v + eps)

def _scatter_add(tgt, idx, src, axis=0):
    return tgt.at[idx].add(src)

def _segment_sum(src, seg, n):
    return jax.ops.segment_sum(src, seg, n)
kernel_name = 'mk_gnn_preln_d4_gnn_r8_76a19a'

def setup_inputs(seed: int=0):
    np.random.seed(seed)
    _w = jnp.asarray

    def _rec_inputs():
        import jax
        import jax.numpy as jnp
        _gk = jax.random.key(seed)
        x = -0.0003713 + 1 * jax.random.normal(jax.random.fold_in(_gk, 1), (12500, 128), jnp.float32)
        _s = jax.random.randint(jax.random.fold_in(_gk, 2), (100000,), 0, 12500, jnp.int32)
        _d = jax.random.randint(jax.random.fold_in(_gk, 3), (100000,), 0, 12500, jnp.int32)
        _loop = jnp.arange(12500, dtype=jnp.int32)
        src = jnp.concatenate([_s, _d, _loop])
        dst = jnp.concatenate([_d, _s, _loop])
        _o = jnp.argsort(dst, stable=True)
        src = src[_o]
        dst = dst[_o]
        edge_attr_128 = -8.16379e-05 + 0.999858 * jax.random.normal(jax.random.fold_in(_gk, 12), (212500, 128), jnp.float32)
        edge_weight = jax.random.uniform(jax.random.fold_in(_gk, 15), (212500,), jnp.float32, 0.0, 1)
        return (x, src, dst, edge_attr_128, edge_weight)
    x, src, dst, edge_attr_128, edge_weight = _rec_inputs()

    def _L0_gnn_setup():
        import jax, jax.numpy as jnp
        import numpy as np
        N = 12500
        E = 400000
        D_IN = 128
        D_OUT = 128
        key = jax.random.key(seed)
        k1, k2, k3, k4, k5, k6 = jax.random.split(key, 6)
        x = jax.random.normal(k1, (N, D_IN), dtype=jnp.float32)
        edge_row = jax.random.randint(k2, (E,), 0, N)
        edge_col = jax.random.randint(k3, (E,), 0, N)
        edge_val = jax.random.uniform(k4, (E,), dtype=jnp.float32)
        stdv = 1.0 / np.sqrt(D_OUT)
        weight = jax.random.uniform(k5, (D_IN, D_OUT), dtype=jnp.float32, minval=-stdv, maxval=stdv)
        bias = jax.random.uniform(k6, (D_OUT,), dtype=jnp.float32, minval=-stdv, maxval=stdv)
        return {'x': x, 'edge_row': edge_row, 'edge_col': edge_col, 'edge_val': edge_val, 'weight': weight, 'bias': bias}
    _L0_gnn_all = _L0_gnn_setup()
    _L0_gnn_in = {k: v for k, v in _L0_gnn_all.items() if k in ('weight', 'bias')}
    del _L0_gnn_all

    def _L1_gnn_setup():
        import jax, jax.numpy as jnp
        import numpy as np
        N_NODES = 6250
        N_EDGES = 100000
        IN_DIM = 128
        HID = 32
        HEADS = 3
        OUT_DIM = 128
        NEG_SLOPE = 0.2
        EPS = 1e-16

        def _gat_layer(x, src, dst, W, a_s, a_d, b, concat):
            n = x.shape[0]
            heads, c = a_s.shape
            h = (x @ W).reshape(n, heads, c)
            alpha_src = jnp.sum(h * a_s[None], axis=-1)
            alpha_dst = jnp.sum(h * a_d[None], axis=-1)
            e = jax.nn.leaky_relu(alpha_src[src] + alpha_dst[dst], NEG_SLOPE)
            m = jax.ops.segment_max(e, dst, num_segments=n)
            e = jnp.exp(e - m[dst])
            denom = jax.ops.segment_sum(e, dst, num_segments=n)
            alpha = e / (denom[dst] + EPS)
            out = jax.ops.segment_sum(alpha[:, :, None] * h[src], dst, num_segments=n)
            out = out.reshape(n, heads * c) if concat else out.mean(axis=1)
            return out + b
        key = jax.random.key(seed)
        ks = jax.random.split(key, 16)
        x = jax.random.normal(ks[0], (N_NODES, IN_DIM), jnp.float32)
        edge_index = jax.random.randint(ks[1], (2, N_EDGES), 0, N_NODES, dtype=jnp.int32)
        s = 0.1
        return {'x': x, 'edge_index': edge_index, 'W1': jax.random.normal(ks[2], (IN_DIM, HEADS * HID), jnp.float32) * s, 'as1': jax.random.normal(ks[3], (HEADS, HID), jnp.float32) * s, 'ad1': jax.random.normal(ks[4], (HEADS, HID), jnp.float32) * s, 'b1': jnp.zeros((HEADS * HID,), jnp.float32), 'W2': jax.random.normal(ks[5], (HEADS * HID, HEADS * HID), jnp.float32) * s, 'as2': jax.random.normal(ks[6], (HEADS, HID), jnp.float32) * s, 'ad2': jax.random.normal(ks[7], (HEADS, HID), jnp.float32) * s, 'b2': jnp.zeros((HEADS * HID,), jnp.float32), 'W3': jax.random.normal(ks[8], (HEADS * HID, OUT_DIM), jnp.float32) * s, 'as3': jax.random.normal(ks[9], (1, OUT_DIM), jnp.float32) * s, 'ad3': jax.random.normal(ks[10], (1, OUT_DIM), jnp.float32) * s, 'b3': jnp.zeros((OUT_DIM,), jnp.float32)}
    _L1_gnn_all = _L1_gnn_setup()
    _L1_gnn_in = {k: v for k, v in _L1_gnn_all.items() if k in ('W1', 'as1', 'ad1', 'b1', 'W2', 'as2', 'ad2', 'b2', 'W3', 'as3', 'ad3', 'b3')}
    del _L1_gnn_all

    def _L2_gnn_setup():
        import jax, jax.numpy as jnp
        import numpy as np
        N_NODES = 6250
        N_EDGES = 100000
        D = 128
        BN_EPS = 0.001
        key = jax.random.key(seed)
        ks = jax.random.split(key, 13)
        s = 1.0 / np.sqrt(D)
        return {'node_features': jax.random.normal(ks[0], (N_NODES, D), jnp.float32), 'edge_features': jax.random.normal(ks[1], (N_EDGES, D), jnp.float32), 'W_node': jax.random.normal(ks[2], (D, D), jnp.float32) * s, 'b_node': jax.random.normal(ks[3], (D,), jnp.float32) * 0.01, 'W_gate': jax.random.normal(ks[4], (D, D), jnp.float32) * s, 'b_gate': jax.random.normal(ks[5], (D,), jnp.float32) * 0.01, 'W_filt': jax.random.normal(ks[6], (D, D), jnp.float32) * s, 'b_filt': jax.random.normal(ks[7], (D,), jnp.float32) * 0.01, 'bn_gamma': jax.random.uniform(ks[8], (D,), jnp.float32, 0.5, 1.5), 'bn_beta': jax.random.normal(ks[9], (D,), jnp.float32) * 0.1, 'bn_mean': jax.random.normal(ks[10], (D,), jnp.float32) * 0.1, 'bn_var': jax.random.uniform(ks[11], (D,), jnp.float32, 0.5, 1.5), 'edge_indices': jax.random.randint(ks[12], (N_EDGES, 2), 0, N_NODES, jnp.int32)}
    _L2_gnn_all = _L2_gnn_setup()
    _L2_gnn_in = {k: v for k, v in _L2_gnn_all.items() if k in ('W_node', 'b_node', 'W_gate', 'b_gate', 'W_filt', 'b_filt', 'bn_gamma', 'bn_beta', 'bn_mean', 'bn_var')}
    del _L2_gnn_all

    def _L3_gnn_setup():
        import jax, jax.numpy as jnp
        import numpy as np
        N_NODES = 6250
        N_EDGES = 100000
        HID = 128
        key = jax.random.key(seed)
        ks = jax.random.split(key, 10)
        s_msg = 1.0 / np.sqrt(2 * HID + 1)
        s_u1 = 1.0 / np.sqrt(2 * HID)
        s_u2 = 1.0 / np.sqrt(HID)
        return {'z': jax.random.normal(ks[0], (N_NODES, HID), dtype=jnp.float32), 'edge_weight': jax.random.uniform(ks[1], (N_EDGES,), dtype=jnp.float32), 'edge_src': jax.random.randint(ks[2], (N_EDGES,), 0, N_NODES), 'edge_dst': jax.random.randint(ks[3], (N_EDGES,), 0, N_NODES), 'Wm': jax.random.normal(ks[4], (2 * HID + 1, HID), dtype=jnp.float32) * s_msg, 'bm': jax.random.normal(ks[5], (HID,), dtype=jnp.float32) * s_msg, 'W1': jax.random.normal(ks[6], (2 * HID, HID), dtype=jnp.float32) * s_u1, 'b1': jax.random.normal(ks[7], (HID,), dtype=jnp.float32) * s_u1, 'W2': jax.random.normal(ks[8], (HID, HID), dtype=jnp.float32) * s_u2, 'b2': jax.random.normal(ks[9], (HID,), dtype=jnp.float32) * s_u2}
    _L3_gnn_all = _L3_gnn_setup()
    _L3_gnn_in = {k: v for k, v in _L3_gnn_all.items() if k in ('Wm', 'bm', 'W1', 'b1', 'W2', 'b2')}
    del _L3_gnn_all
    return {'x': x, 'src': src, 'dst': dst, 'edge_attr_128': edge_attr_128, 'edge_weight': edge_weight, 'L0_gnn_weight': _L0_gnn_in['weight'], 'L0_gnn_bias': _L0_gnn_in['bias'], 'L1_gnn_W1': _L1_gnn_in['W1'], 'L1_gnn_as1': _L1_gnn_in['as1'], 'L1_gnn_ad1': _L1_gnn_in['ad1'], 'L1_gnn_b1': _L1_gnn_in['b1'], 'L1_gnn_W2': _L1_gnn_in['W2'], 'L1_gnn_as2': _L1_gnn_in['as2'], 'L1_gnn_ad2': _L1_gnn_in['ad2'], 'L1_gnn_b2': _L1_gnn_in['b2'], 'L1_gnn_W3': _L1_gnn_in['W3'], 'L1_gnn_as3': _L1_gnn_in['as3'], 'L1_gnn_ad3': _L1_gnn_in['ad3'], 'L1_gnn_b3': _L1_gnn_in['b3'], 'L2_gnn_W_node': _L2_gnn_in['W_node'], 'L2_gnn_b_node': _L2_gnn_in['b_node'], 'L2_gnn_W_gate': _L2_gnn_in['W_gate'], 'L2_gnn_b_gate': _L2_gnn_in['b_gate'], 'L2_gnn_W_filt': _L2_gnn_in['W_filt'], 'L2_gnn_b_filt': _L2_gnn_in['b_filt'], 'L2_gnn_bn_gamma': _L2_gnn_in['bn_gamma'], 'L2_gnn_bn_beta': _L2_gnn_in['bn_beta'], 'L2_gnn_bn_mean': _L2_gnn_in['bn_mean'], 'L2_gnn_bn_var': _L2_gnn_in['bn_var'], 'L3_gnn_Wm': _L3_gnn_in['Wm'], 'L3_gnn_bm': _L3_gnn_in['bm'], 'L3_gnn_W1': _L3_gnn_in['W1'], 'L3_gnn_b1': _L3_gnn_in['b1'], 'L3_gnn_W2': _L3_gnn_in['W2'], 'L3_gnn_b2': _L3_gnn_in['b2']}

def reference(x, src, dst, edge_attr_128, edge_weight, L0_gnn_weight, L0_gnn_bias, L1_gnn_W1, L1_gnn_as1, L1_gnn_ad1, L1_gnn_b1, L1_gnn_W2, L1_gnn_as2, L1_gnn_ad2, L1_gnn_b2, L1_gnn_W3, L1_gnn_as3, L1_gnn_ad3, L1_gnn_b3, L2_gnn_W_node, L2_gnn_b_node, L2_gnn_W_gate, L2_gnn_b_gate, L2_gnn_W_filt, L2_gnn_b_filt, L2_gnn_bn_gamma, L2_gnn_bn_beta, L2_gnn_bn_mean, L2_gnn_bn_var, L3_gnn_Wm, L3_gnn_bm, L3_gnn_W1, L3_gnn_b1, L3_gnn_W2, L3_gnn_b2):
    import jax
    import jax.numpy as jnp

    def _L0_gnn_ref(x, edge_row, edge_col, edge_val, weight, bias):
        import jax, jax.numpy as jnp
        import numpy as np
        N = 12500
        E = 400000
        D_IN = 128
        D_OUT = 128
        support = x @ weight
        msgs = support[edge_col] * edge_val[:, None]
        out = jax.ops.segment_sum(msgs, edge_row, num_segments=N)
        return out + bias

    def _L1_gnn_ref(x, edge_index, W1, as1, ad1, b1, W2, as2, ad2, b2, W3, as3, ad3, b3):
        import jax, jax.numpy as jnp
        import numpy as np
        N_NODES = 6250
        N_EDGES = 100000
        IN_DIM = 128
        HID = 32
        HEADS = 3
        OUT_DIM = 128
        NEG_SLOPE = 0.2
        EPS = 1e-16

        def _gat_layer(x, src, dst, W, a_s, a_d, b, concat):
            n = x.shape[0]
            heads, c = a_s.shape
            h = (x @ W).reshape(n, heads, c)
            alpha_src = jnp.sum(h * a_s[None], axis=-1)
            alpha_dst = jnp.sum(h * a_d[None], axis=-1)
            e = jax.nn.leaky_relu(alpha_src[src] + alpha_dst[dst], NEG_SLOPE)
            m = jax.ops.segment_max(e, dst, num_segments=n)
            e = jnp.exp(e - m[dst])
            denom = jax.ops.segment_sum(e, dst, num_segments=n)
            alpha = e / (denom[dst] + EPS)
            out = jax.ops.segment_sum(alpha[:, :, None] * h[src], dst, num_segments=n)
            out = out.reshape(n, heads * c) if concat else out.mean(axis=1)
            return out + b
        n = x.shape[0]
        loops = jnp.arange(n, dtype=edge_index.dtype)
        src = jnp.concatenate([edge_index[0], loops])
        dst = jnp.concatenate([edge_index[1], loops])
        h = _gat_layer(x, src, dst, W1, as1, ad1, b1, concat=True)
        h = jax.nn.elu(h)
        h = _gat_layer(h, src, dst, W2, as2, ad2, b2, concat=True)
        h = jax.nn.elu(h)
        out = _gat_layer(h, src, dst, W3, as3, ad3, b3, concat=False)
        return out

    def _L2_gnn_ref(node_features, edge_features, W_node, b_node, W_gate, b_gate, W_filt, b_filt, bn_gamma, bn_beta, bn_mean, bn_var, edge_indices):
        import jax, jax.numpy as jnp
        import numpy as np
        N_NODES = 6250
        N_EDGES = 100000
        D = 128
        BN_EPS = 0.001
        n = node_features.shape[0]
        node_hidden = node_features @ W_node + b_node
        gate = jax.nn.sigmoid(edge_features @ W_gate + b_gate)
        filt = edge_features @ W_filt + b_filt
        neighbors = jnp.take(node_hidden, edge_indices[:, 1], axis=0)
        messages = gate * filt * neighbors
        seg = edge_indices[:, 0]
        sums = jax.ops.segment_sum(messages, seg, num_segments=n)
        counts = jax.ops.segment_sum(jnp.ones((seg.shape[0],), jnp.float32), seg, num_segments=n)[:, None]
        aggregated = jnp.where(counts > 0, sums / jnp.maximum(counts, 1.0), 0.0)
        out = node_hidden + aggregated
        out = (out - bn_mean) * jax.lax.rsqrt(bn_var + BN_EPS) * bn_gamma + bn_beta
        return jax.nn.relu(out)

    def _L3_gnn_ref(z, edge_weight, edge_src, edge_dst, Wm, bm, W1, b1, W2, b2):
        import jax, jax.numpy as jnp
        import numpy as np
        N_NODES = 6250
        N_EDGES = 100000
        HID = 128
        n, H = z.shape
        Wd, Ws, ww = (Wm[:H], Wm[H:2 * H], Wm[2 * H])
        msgs = z[edge_dst] @ Wd + z[edge_src] @ Ws + edge_weight[:, None] * ww[None, :] + bm
        agg = jax.ops.segment_max(msgs, edge_dst, num_segments=n)
        deg = jax.ops.segment_sum(jnp.ones_like(edge_weight), edge_dst, num_segments=n)
        agg = jnp.where(deg[:, None] > 0, agg, jnp.zeros((), dtype=z.dtype))
        W1a, W1b = (W1[:H], W1[H:])
        hidden = jax.nn.relu(z @ W1a + agg @ W1b + b1)
        return hidden @ W2 + b2
    edge_index = jnp.stack([src, dst])
    edge_index_t = jnp.stack([src, dst], axis=1)
    h = jnp.maximum(_layernorm(x, axis=-1), 0.0)
    x = x + _L0_gnn_ref(h, src, dst, edge_weight, L0_gnn_weight, L0_gnn_bias)
    h = jnp.maximum(_layernorm(x, axis=-1), 0.0)
    x = x + _L1_gnn_ref(h, edge_index, L1_gnn_W1, L1_gnn_as1, L1_gnn_ad1, L1_gnn_b1, L1_gnn_W2, L1_gnn_as2, L1_gnn_ad2, L1_gnn_b2, L1_gnn_W3, L1_gnn_as3, L1_gnn_ad3, L1_gnn_b3)
    h = jnp.maximum(_layernorm(x, axis=-1), 0.0)
    x = x + _L2_gnn_ref(h, edge_attr_128, L2_gnn_W_node, L2_gnn_b_node, L2_gnn_W_gate, L2_gnn_b_gate, L2_gnn_W_filt, L2_gnn_b_filt, L2_gnn_bn_gamma, L2_gnn_bn_beta, L2_gnn_bn_mean, L2_gnn_bn_var, edge_index_t)
    h = jnp.maximum(_layernorm(x, axis=-1), 0.0)
    x = x + _L3_gnn_ref(h, edge_weight, src, dst, L3_gnn_Wm, L3_gnn_bm, L3_gnn_W1, L3_gnn_b1, L3_gnn_W2, L3_gnn_b2)
    return x

_drawn_inputs = setup_inputs


def setup_inputs(seed=0):
    import zlib

    import numpy as np

    out = dict(_drawn_inputs(seed))
    spreads = {'L1_gnn_b1': (0.0, 0.315), 'L1_gnn_b2': (0.0, 0.1), 'L1_gnn_b3': (0.0, 0.1)}
    factors = {'L1_gnn_as1': 8.0,
     'L1_gnn_ad1': 64.0,
     'L1_gnn_as2': 61.302,
     'L1_gnn_ad2': 64.0,
     'L1_gnn_as3': 64.0,
     'L1_gnn_ad3': 64.0,
     'L2_gnn_b_node': 8.0,
     'L2_gnn_W_gate': 5.32,
     'L2_gnn_b_gate': 64.0,
     'L2_gnn_b_filt': 64.0,
     'L3_gnn_bm': 3.733,
     'L3_gnn_b1': 2.965}
    for name, (base, spread) in spreads.items():
        noise = np.random.default_rng([zlib.crc32(name.encode()), seed]).standard_normal(out[name].shape)
        drawn = base * np.exp(spread * noise) if base else spread * noise
        out[name] = jnp.asarray(drawn.astype(out[name].dtype))
    for name, factor in factors.items():
        out[name] = (out[name] * factor).astype(out[name].dtype)
    return out
```

```python
import concourse.bass as bass
from concourse import mybir
from contextlib import ExitStack

F32 = mybir.dt.float32
BF16 = mybir.dt.bfloat16
I32 = mybir.dt.int32
U32 = mybir.dt.uint32
ALU = mybir.AluOpType
ACT = mybir.ActivationFunctionType

P = 128
N = 12500
E = 212500
D = 128
NB = -(-N // P)
NP = NB * P
COLS = 2048
ROWS = -(-E // COLS)
EP = ROWS * COLS
TPR = COLS // P
PAIRS = TPR // 2
WIN = 2 * P
FULL = E // COLS
LAST = E - FULL * COLS
PAD_NODE = NP - 1
ORD = 12800
ZERO_ROW = ORD - 1
HEADS = 3
HID = 32
BIG = 1.0e38
assert ROWS <= P and N < PAD_NODE and N + WIN < ZERO_ROW and ORD % 512 == 0


class Chain:

    def __init__(self, eng, sem, base=0):
        self.eng, self.sem, self.base, self.n = eng, sem, base, 0

    def step(self, ins):
        self.n += 1
        ins.then_inc(self.sem, 1)
        self.eng.wait_ge(self.sem, self.base + self.n)


def make_constants(nc, sb, psum, sem, k):
    made = sem("constants_made")
    with nc.Block() as block:
        @block.gpsimd
        def _(pool):
            c = Chain(pool, made)
            nc.gpsimd.iota(k.iota[:, :], [[1, WIN]], base=0, channel_multiplier=0,
                           allow_small_or_imprecise_dtypes=True)
            nc.gpsimd.iota(k.spare[:, :], [[1, 1]], base=EP, channel_multiplier=1,
                           allow_small_or_imprecise_dtypes=True)
            nc.gpsimd.iota(k.eid[:, :], [[1, COLS]], base=0, channel_multiplier=COLS,
                           allow_small_or_imprecise_dtypes=True)
            c.step(nc.gpsimd.memset(k.ones[:, :], 1.0))
            c.step(nc.gpsimd.memset(k.ident[:, :], 0.0))
            nc.gpsimd.affine_select(out=k.ident[:, :], in_=k.ident[:, :], compare_op=ALU.not_equal, fill=1.0,
                                    base=0, pattern=[[-1, P]], channel_multiplier=1)
            nc.gpsimd.affine_select(out=k.before[:, :], in_=k.ones[:, :], compare_op=ALU.is_gt, fill=0.0,
                                    base=0, pattern=[[1, P]], channel_multiplier=-1)
            c.step(nc.gpsimd.affine_select(out=k.after[:, :], in_=k.ones[:, :], compare_op=ALU.is_gt, fill=0.0,
                                           base=0, pattern=[[-1, P]], channel_multiplier=1))


def to_tile_columns(nc, pe, dve, side, fields, ps, packed, ident, turned, evacuated):
    for f, (src, dtype) in enumerate(fields):
        for b in range(TPR // 4):
            n = f * (TPR // 4) + b
            if side == "pe":
                if n >= 2:
                    pe.wait_ge(evacuated, n - 1)
                for j in range(4):
                    t = 4 * b + j
                    last = nc.tensor.transpose(ps[n % 2][:, j * ROWS:(j + 1) * ROWS],
                                               src[:, t * P:(t + 1) * P], ident[0:ROWS, 0:ROWS])
                last.then_inc(turned, 1)
            else:
                dve.wait_ge(turned, n + 1)
                c0 = f * TPR + 4 * b
                out = packed[:, :, c0:c0 + 4]
                if dtype is not F32:
                    out = packed[:, :, :].bitcast(dtype)[:, :, c0:c0 + 4]
                nc.vector.tensor_copy(out.rearrange("p g j -> p j g"),
                                      ps[n % 2][:, 0:4 * ROWS].rearrange("p (j g) -> p j g", j=4)
                                      ).then_inc(evacuated, 1)


def stage_edges(nc, sb, psum, sem, k, src, dst, weight, sort_meta):
    loaded, filled, turned, evacuated, stored, cut = (
        sem(f"edges_{x}") for x in ("loaded", "filled", "turned", "evacuated", "stored", "cut"))
    src_i, dst_i = sb("src_i", [ROWS, COLS], I32), sb("dst_i", [ROWS, COLS], I32)
    part = sb("part", [ROWS, COLS], I32)
    src_f, dst_f, w_f = (sb(x, [ROWS, COLS], F32) for x in ("src_f", "dst_f", "w_f"))
    halves = [sb(f"half{i}", [ROWS, COLS], F32) for i in range(4)]
    packed = sb("packed", [P, ROWS, 8 * TPR], F32)
    ps = [psum(f"ps_turn{i}", [P, 512], F32) for i in range(2)]
    fields = [(x, F32) for x in (*halves, src_f, dst_f, w_f, k.eid)]
    with nc.Block() as block:
        @block.sync
        def _(sp):
            sp.wait_ge(filled, 1)
            for to, of in ((src_i, src), (dst_i, dst), (w_f, weight)):
                sp.dma_start(to[0:FULL, :], of[0:FULL * COLS].rearrange("(g c) -> g c", c=COLS)).then_inc(loaded, 16)
                sp.dma_start(to[FULL:ROWS, 0:LAST], of[FULL * COLS:E].rearrange("(g c) -> g c", g=1)).then_inc(loaded, 16)
            sp.wait_ge(evacuated, 8 * TPR // 4)
            sp.dma_start(sort_meta.rearrange("g p c -> p g c"), packed[:, :, :]).then_inc(stored, 16)
            sp.wait_ge(stored, 16)

        @block.vector
        def _(dve):
            nc.vector.memset(src_i[:, :], PAD_NODE)
            nc.vector.memset(dst_i[:, :], PAD_NODE)
            nc.vector.memset(w_f[:, :], 0.0).then_inc(filled, 1)
            dve.wait_ge(loaded, 6 * 16)
            c = Chain(dve, cut)
            nc.vector.tensor_copy(src_f[:, :], src_i[:, :])
            nc.vector.tensor_copy(dst_f[:, :], dst_i[:, :])
            for i, key in enumerate((src_i, dst_i)):
                for j, (op, by) in enumerate(((ALU.bitwise_and, P - 1), (ALU.logical_shift_right, 7))):
                    c.step(nc.vector.tensor_scalar(part[:, :], key[:, :], by, None, op))
                    c.step(nc.vector.tensor_copy(halves[2 * i + j][:, :], part[:, :]))
            to_tile_columns(nc, None, dve, "dve", fields, ps, packed, k.ident, turned, evacuated)

        @block.tensor
        def _(pe):
            pe.wait_ge(cut, 8)
            to_tile_columns(nc, pe, None, "pe", fields, ps, packed, k.ident, turned, evacuated)


def count_keys(nc, sb, psum, sem, k, key, sort_meta, cnt):
    meta = [sb(f"meta{h}", [P, 2 * TPR], F32) for h in range(2)]
    hot = [sb(f"hot{h}", [P, TPR, 2, P], BF16) for h in range(2)]
    total = psum("ps_count", [P, P], F32)
    iota = sb("iota16", [P, P], BF16)
    loaded = [sem(f"count_{key}_loaded{h}") for h in range(2)]
    hots = [sem(f"count_{key}_hot{h}") for h in range(2)]
    used = [sem(f"count_{key}_used{h}") for h in range(2)]
    ready, copied = sem(f"count_{key}_iota"), sem(f"count_{key}_copied")
    c0 = 0 if key == "src" else 2 * TPR
    with nc.Block() as block:
        @block.sync
        def _(sp):
            with sp.Fori(0, ROWS // 2) as it:
                for h in range(2):
                    sp.wait_ge(hots[h], it)
                    sp.dma_start(meta[h][:, :], sort_meta[it * 2 + h, :, c0:c0 + 2 * TPR]).then_inc(loaded[h], 16)

        @block.vector
        def _(dve):
            nc.vector.tensor_copy(iota[:, :], k.iota[:, 0:P]).then_inc(ready, 1)
            dve.wait_ge(ready, 1)
            with dve.Fori(0, ROWS // 2) as it:
                for h in range(2):
                    dve.wait_ge(loaded[h], it * 16 + 16)
                    dve.wait_ge(used[h], it)
                    for t in range(TPR):
                        for half in range(2):
                            last = nc.vector.tensor_scalar(hot[h][:, t, half, :], iota[:, :],
                                                           meta[h][:, half * TPR + t:half * TPR + t + 1], None,
                                                           ALU.is_equal)
                    last.then_inc(hots[h], 1)
            for h in range(2):
                dve.wait_ge(used[h], ROWS // 2)
            nc.vector.tensor_copy(cnt[:, :], total[:, 0:NB]).then_inc(copied, 1)

        @block.tensor
        def _(pe):
            def group(h, n, first):
                pe.wait_ge(hots[h], n)
                for t in range(TPR):
                    last = nc.tensor.matmul(total[:, :], hot[h][:, t, 0, :], hot[h][:, t, 1, :],
                                            start=first and t == 0, stop=True, skip_group_check=True)
                last.then_inc(used[h], 1)
            group(0, 1, True)
            group(1, 1, False)
            with pe.Fori(1, ROWS // 2) as it:
                for h in range(2):
                    group(h, it + 1, False)


def node_offsets(nc, sb, psum, sem, k, key, cnt, start, row_of, spot):
    has, col, run, tmp = (sb(x, [P, NB], F32) for x in ("has", "col", "run", "tmp"))
    ordf = sb("ordf", [P, NB], F32)
    ps = psum("ps_sums", [P, 2, 2, P], F32)
    d, summed = sem(f"offsets_{key}_steps"), sem(f"offsets_{key}_summed")
    with nc.Block() as block:
        @block.tensor
        def _(pe):
            pe.wait_ge(d, 1)
            for i, x in enumerate((cnt, has)):
                nc.tensor.matmul(ps[:, i, 0, 0:NB], k.ones[:, 0:P], x[:, :], start=True, stop=True)
                last = nc.tensor.matmul(ps[:, i, 1, 0:NB], k.before[:, :], x[:, :], start=True, stop=True)
            last.then_inc(summed, 1)

        @block.vector
        def _(dve):
            c = Chain(dve, d)
            c.step(nc.vector.tensor_scalar(has[:, :], cnt[:, :], 0.0, None, ALU.is_gt))
            dve.wait_ge(summed, 1)
            for i, out in enumerate((start, ordf)):
                c.step(nc.vector.tensor_copy(col[:, :], ps[:, i, 0, 0:NB]))
                c.step(nc.vector.tensor_tensor_scan(run[:, :], k.ones[:, 0:NB], col[:, :], 0.0, ALU.mult, ALU.add))
                c.step(nc.vector.tensor_tensor(tmp[:, :], run[:, :], col[:, :], ALU.subtract))
                c.step(nc.vector.tensor_tensor(out[:, :], tmp[:, :], ps[:, i, 1, 0:NB], ALU.add))
            c.step(nc.vector.scalar_tensor_tensor(tmp[:, :], ordf[:, :], -float(ZERO_ROW), has[:, :], ALU.add, ALU.mult))
            c.step(nc.vector.tensor_scalar(row_of[:, :], tmp[:, :], float(ZERO_ROW), None, ALU.add))
            c.step(nc.vector.scalar_tensor_tensor(tmp[:, :], start[:, :], k.spare[:, :], has[:, :], ALU.subtract, ALU.mult))
            c.step(nc.vector.tensor_scalar(spot[:, :], tmp[:, :], k.spare[:, :], None, ALU.add))


def sort_edges(nc, sb, psum, sem, k, key, sort_meta, start, ordered):
    c0 = 0 if key == "src" else 2 * TPR
    meta = [sb(f"meta{h}", [P, 2 * TPR], F32) for h in range(2)]
    values = [sb(f"values{h}", [P, 4 * TPR], F32) for h in range(2)]
    moved = [sb(f"moved{h}", [P, TPR, 4], F32) for h in range(2)]
    hot = [sb(f"hot{i}", [P, 2, P], F32) for i in range(4)]
    hot_t = [sb(f"hot_t{i}", [P, 2, P], F32) for i in range(2)]
    table = [sb(f"table{i}", [P, NB], F32) for i in range(2)]
    junk = [sb(f"junk{i}", [P, 2, P], F32) for i in range(2)]
    parts = [sb(f"parts{h}", [P, 2, TPR], F32) for h in range(2)]
    place = [sb(f"place{h}", [P, TPR], U32) for h in range(2)]
    ps_t = [psum(f"ps_t{i}", [P, 2, P], F32) for i in range(2)]
    ps_q = [psum(f"ps_q{i}", [P, 2, P], F32) for i in range(2)]
    ps_c = psum("ps_c", [P, NB], F32)
    s = {x: sem(f"sort_{key}_{x}") for x in ("seeded", "hots", "turned", "turned_copied", "asked", "answered",
                                            "table_grown", "table_copied")}
    scattered, g0 = k.pool_dma.take(ROWS // 2 * 16 * TPR)
    loaded, placed = ([sem(f"sort_{key}_{x}{h}") for h in range(2)] for x in ("loaded", "placed"))
    with nc.Block() as block:
        @block.sync
        def _(sp):
            with sp.Fori(0, ROWS // 2) as it:
                for h in range(2):
                    sp.wait_ge(placed[h], it)
                    sp.dma_start(meta[h][:, :], sort_meta[it * 2 + h, :, c0:c0 + 2 * TPR]).then_inc(loaded[h], 16)
                    sp.dma_start(values[h][:, :], sort_meta[it * 2 + h, :, 4 * TPR:8 * TPR]).then_inc(loaded[h], 16)

        @block.vector
        def _(dve):
            with dve.Fori(0, ROWS // 2) as it:
                for h in range(2):
                    q = it * 2 + h
                    dve.wait_ge(loaded[h], it * 32 + 32)

                    def make_hot(t):
                        for half in range(2):
                            last = nc.vector.tensor_scalar(hot[t % 4][:, half, :], k.iota[:, 0:P],
                                                           meta[h][:, half * TPR + t:half * TPR + t + 1], None,
                                                           ALU.is_equal)
                        last.then_inc(s["hots"], 1)

                    def read_answer(t):
                        dve.wait_ge(s["asked"], q * TPR + t + 1)
                        if t >= 2:
                            dve.wait_ge(s["answered"], q * TPR + t - 1)
                        nc.vector.scalar_tensor_tensor(junk[t % 2][:, 0, :], ps_q[t % 2][:, 0, :], 1.5, k.after[:, :],
                                                       ALU.is_gt, ALU.mult, accum_out=parts[h][:, 0, t:t + 1])
                        nc.vector.scalar_tensor_tensor(junk[t % 2][:, 1, 0:NB], ps_q[t % 2][:, 1, 0:NB], 1.0,
                                                       hot[t % 4][:, 1, 0:NB], ALU.mult, ALU.mult,
                                                       accum_out=parts[h][:, 1, t:t + 1]).then_inc(s["answered"], 1)
                    dve.wait_ge(scattered[h], it * (16 * TPR) + g0[h])
                    dve.wait_ge(s["answered"], q * TPR)
                    make_hot(0)
                    make_hot(1)
                    for t in range(TPR):
                        if t + 2 < TPR:
                            if t >= 2:
                                dve.wait_ge(s["table_grown"], q * TPR + t - 1)
                                dve.wait_ge(s["answered"], q * TPR + t - 1)
                            make_hot(t + 2)
                        read_answer(t)
                    dve.wait_ge(s["table_grown"], q * TPR + TPR)
                    dve.wait_ge(s["answered"], q * TPR + TPR)
                    nc.vector.tensor_copy(moved[h][:, :, :].rearrange("p t c -> p c t"),
                                          values[h][:, :].rearrange("p (c t) -> p c t", c=4))
                    nc.vector.tensor_tensor(place[h][:, :], parts[h][:, 0, :], parts[h][:, 1, :],
                                            ALU.add).then_inc(placed[h], 1)

        @block.tensor
        def _(pe):
            nc.tensor.matmul(ps_c[:, :], k.ident[:, :], start[:, :], start=True, stop=True,
                             skip_group_check=True).then_inc(s["seeded"], 1)
            with pe.Fori(0, ROWS // 2) as it:
                for h in range(2):
                    for t in range(TPR):
                        n = (it * 2 + h) * TPR + t
                        pe.wait_ge(s["hots"], n + 1)
                        for half in range(2):
                            last = nc.tensor.transpose(ps_t[t % 2][:, half, :], hot[t % 4][:, half, :], k.ident[:, :])
                        last.then_inc(s["turned"], 1)
                        pe.wait_ge(s["turned_copied"], n + 1)
                        pe.wait_ge(s["table_copied"], n + 1)
                        if t >= 2:
                            pe.wait_ge(s["answered"], n - 1)
                        nc.tensor.matmul(ps_q[t % 2][:, 0, :], hot_t[t % 2][:, 0, :], hot_t[t % 2][:, 0, :],
                                         start=True, stop=False, skip_group_check=True)
                        nc.tensor.matmul(ps_q[t % 2][:, 0, :], hot_t[t % 2][:, 1, :], hot_t[t % 2][:, 1, :],
                                         start=False, stop=True, skip_group_check=True)
                        nc.tensor.matmul(ps_q[t % 2][:, 1, 0:NB], hot_t[t % 2][:, 0, :], table[t % 2][:, :],
                                         start=True, stop=True, skip_group_check=True).then_inc(s["asked"], 1)
                        nc.tensor.matmul(ps_c[:, :], hot[t % 4][:, 0, :], hot[t % 4][:, 1, 0:NB], start=False,
                                         stop=True, skip_group_check=True).then_inc(s["table_grown"], 1)

        @block.scalar
        def _(act):
            act.wait_ge(s["seeded"], 1)
            nc.scalar.copy(table[0][:, :], ps_c[:, :]).then_inc(s["table_copied"], 1)
            with act.Fori(0, ROWS // 2) as it:
                for h in range(2):
                    for t in range(TPR):
                        n = (it * 2 + h) * TPR + t
                        act.wait_ge(s["turned"], n + 1)
                        nc.scalar.copy(hot_t[t % 2][:, :, :], ps_t[t % 2][:, :, :]).then_inc(s["turned_copied"], 1)
                        act.wait_ge(s["table_grown"], n + 1)
                        nc.scalar.copy(table[(t + 1) % 2][:, :], ps_c[:, :]).then_inc(s["table_copied"], 1)

        @block.gpsimd
        def _(pool):
            with pool.Fori(0, ROWS // 2) as it:
                for h in range(2):
                    pool.wait_ge(placed[h], it + 1)
                    pool.sem_inc(k.turns, 1)
                    for t in range(TPR):
                        pool.indirect_dma_start(
                            out=ordered, out_offset=bass.IndirectOffsetOnAxis(ap=place[h][:, t:t + 1], axis=0),
                            in_=moved[h][:, t, :], in_offset=None).then_inc(scattered[h], 16)
            for h in range(2):
                pool.wait_ge(scattered[h], ROWS // 2 * 16 * TPR + g0[h])
def lay_out_segments(nc, sb, psum, sem, k, key, ordered, edge_meta, bases, flags):
    own, other = (0, 1) if key == "src" else (1, 0)
    rows = sb("rows", [ROWS, COLS, 4], F32)
    near = sb("near", [ROWS, 2], F32)
    first, end, ordn, rel = (sb(x, [ROWS, COLS], F32) for x in ("first", "end", "ordn", "rel"))
    cols = [sb(f"cols{i}", [ROWS, COLS], F32) for i in range(3)]
    low = sb("low", [ROWS, 1], F32)
    base_i = sb("base_i", [ROWS, PAIRS], I32)
    packed = sb("packed", [P, ROWS, 4 * TPR], F32)
    ps = [psum(f"ps_turn{i}", [P, 512], F32) for i in range(2)]
    ps_low = psum("ps_low", [P, 1], F32)
    names = ("loaded", "near", "next", "steps", "summed", "turned", "evacuated", "stored")
    s = {x: sem(f"segments_{key}_{x}") for x in names}
    last_field = cols[2] if key == "src" else end
    last_type = U32 if key == "src" else F32
    fields = [(cols[0], U32), (cols[1], F32), (rel, F32), (last_field, last_type)]
    with nc.Block() as block:
        @block.sync
        def _(sp):
            sp.dma_start(rows[:, :, :], ordered.rearrange("(g c) f -> g c f", c=COLS)).then_inc(s["loaded"], 16)
            sp.wait_ge(s["loaded"], 16)
            sp.wait_ge(s["steps"], 1)
            sp.dma_start(near[1:ROWS, 0:1], rows[0:ROWS - 1, COLS - 1, own:own + 1]).then_inc(s["near"], 16)
            sp.wait_ge(s["steps"], 3)
            sp.dma_start(near[0:ROWS - 1, 1:2], first[1:ROWS, 0:1]).then_inc(s["next"], 16)
            sp.wait_ge(s["evacuated"], 4 * TPR // 4)
            sp.dma_start(edge_meta.rearrange("g p c -> p g c"), packed[:, :, :]).then_inc(s["stored"], 16)
            sp.dma_start(bases.rearrange("a (g c) -> (a g) c", c=PAIRS), base_i[:, :]).then_inc(s["stored"], 16)
            sp.dma_start(flags[0], first[:, :]).then_inc(s["stored"], 16)
            sp.dma_start(flags[1], end[:, :]).then_inc(s["stored"], 16)
            sp.wait_ge(s["stored"], 64)

        @block.vector
        def _(dve):
            c = Chain(dve, s["steps"])
            nc.vector.memset(near[:, 0:1], -1.0)
            c.step(nc.vector.memset(near[:, 1:2], 1.0))
            dve.wait_ge(s["loaded"], 16)
            c.step(nc.vector.tensor_tensor(first[:, 1:COLS], rows[:, 1:COLS, own], rows[:, 0:COLS - 1, own], ALU.not_equal))
            dve.wait_ge(s["near"], 16)
            c.step(nc.vector.tensor_tensor(first[:, 0:1], rows[:, 0:1, own], near[:, 0:1], ALU.not_equal))
            c.step(nc.vector.tensor_copy(end[:, 0:COLS - 1], first[:, 1:COLS]))
            nc.vector.tensor_copy(cols[0][:, :], rows[:, :, other])
            nc.vector.tensor_copy(cols[1][:, :], rows[:, :, 2])
            if key == "src":
                nc.vector.tensor_scalar(cols[2][:, :], rows[:, :, 3], float(E - 1), None, ALU.min)
            c.step(nc.vector.memset(rel[:, :], 1.0))
            dve.wait_ge(s["next"], 16)
            c.step(nc.vector.tensor_copy(end[:, COLS - 1:COLS], near[:, 1:2]))
            c.step(nc.vector.tensor_tensor_scan(ordn[:, :], rel[:, :], first[:, :], -1.0, ALU.mult, ALU.add))
            c.step(nc.vector.tensor_scalar(low[:, :], ordn[:, COLS - 1:COLS], 1.0, None, ALU.add))
            dve.wait_ge(s["summed"], 1)
            c.step(nc.vector.tensor_copy(near[:, 0:1], ps_low[0:ROWS, :]))
            c.step(nc.vector.tensor_scalar(ordn[:, :], ordn[:, :], near[:, 0:1], None, ALU.add))
            by_pair = ordn[:, :].rearrange("p (k c) -> p k c", c=WIN)
            nc.vector.tensor_copy(base_i[:, :], by_pair[:, :, 0])
            c.step(nc.vector.tensor_tensor(rel[:, :].rearrange("p (k c) -> p k c", c=WIN), by_pair,
                                           by_pair[:, :, 0:1].to_broadcast([ROWS, PAIRS, WIN]), ALU.subtract))
            to_tile_columns(nc, None, dve, "dve", fields, ps, packed, k.ident, s["turned"], s["evacuated"])

        @block.tensor
        def _(pe):
            pe.wait_ge(s["steps"], 8)
            nc.tensor.matmul(ps_low[0:ROWS, :], k.before[0:ROWS, 0:ROWS], low[:, :], start=True, stop=True).then_inc(s["summed"], 1)
            pe.wait_ge(s["steps"], 11)
            to_tile_columns(nc, pe, None, "pe", fields, ps, packed, k.ident, s["turned"], s["evacuated"])


def unload_sums(nc, sb, psum, sem, k, acc, sums):
    stage = [sb(f"stage{i}", [P, 4 * P], F32) for i in range(2)]
    out = [sb(f"out{i}", [P, 4 * P], F32) for i in range(2)]
    ps = [psum(f"ps_unload{i}", [P, 4 * P], F32) for i in range(2)]
    fetched, turned, copied, stored = ([sem(f"unload_{x}{i}") for i in range(2)] for x in ("fetched", "turned", "copied", "stored"))
    steps = ORD // (4 * P)
    half = -(-steps // 2)
    with nc.Block() as block:
        @block.scalar
        def _(act):
            with act.Fori(0, half) as it:
                for i in range(2):
                    act.wait_ge(turned[i], it)
                    nc.scalar.copy(stage[i][:, :], acc[:, bass.ds((it + i * (steps - half)) * 4 * P, 4 * P)]).then_inc(fetched[i], 1)

        @block.tensor
        def _(pe):
            with pe.Fori(0, half) as it:
                for i in range(2):
                    pe.wait_ge(fetched[i], it + 1)
                    pe.wait_ge(copied[i], it)
                    for j in range(4):
                        last = nc.tensor.transpose(ps[i][:, j * P:(j + 1) * P], stage[i][:, j * P:(j + 1) * P], k.ident[:, :])
                    last.then_inc(turned[i], 1)

        @block.vector
        def _(dve):
            with dve.Fori(0, half) as it:
                for i in range(2):
                    dve.wait_ge(turned[i], it + 1)
                    dve.wait_ge(stored[i], it * 16)
                    nc.vector.tensor_copy(out[i][:, :], ps[i][:, :]).then_inc(copied[i], 1)

        @block.sync
        def _(sp):
            with sp.Fori(0, half) as it:
                for i in range(2):
                    sp.wait_ge(copied[i], it + 1)
                    if i == 1:
                        sp.wait_ge(stored[0], it * 16 + 16)
                    sp.dma_start(sums[bass.ds((it + i * (steps - half)) * 4 * P, 4 * P), :].rearrange("(j p) f -> p j f", p=P),
                                 out[i][:, :].rearrange("p (j f) -> p j f", j=4)).then_inc(stored[i], 16)
            for i in range(2):
                sp.wait_ge(stored[i], half * 16)


class SumPass:

    def __init__(self, nc, sb, psum, sem, k, name, bases, width, slots=4):
        self.nc, self.k, self.width, self.slots = nc, k, width, slots
        self.acc = k.acc
        self.bases_dram = bases
        self.base = sb("base", [1, ROWS * PAIRS], I32)
        self.meta = [sb(f"meta{h}", [P, 4 * TPR], F32) for h in range(2)]
        self.hot = [sb(f"hot{h}", [P, TPR, WIN], F32) for h in range(2)]
        self.ps = [psum(f"ps_sum{i}", [P, WIN], F32) for i in range(slots)]
        self.base_loaded, self.cleared = sem(f"{name}_base_loaded"), sem(f"{name}_cleared")
        self.meta_loaded, self.hots, self.summed = ([sem(f"{name}_{x}{h}") for h in range(2)]
                                                    for x in ("meta_loaded", "hots", "summed"))
        self.added = [sem(f"{name}_added{i}") for i in range(slots)]

    def wait_read(self, eng, it, h):
        eng.wait_ge(self.summed[h], it * PAIRS)

    def load_bases(self, sp):
        sp.dma_start(self.base[:, :], self.bases_dram).then_inc(self.base_loaded, 16)

    def load_meta(self, sp, it, h, edge_meta):
        sp.wait_ge(self.hots[h], it)
        sp.dma_start(self.meta[h][:, :], edge_meta[it * 2 + h]).then_inc(self.meta_loaded[h], 16)

    def start_dve(self, dve):
        dve.wait_ge(self.base_loaded, 16)
        self.nc.vector.memset(self.acc[:, :], 0.0).then_inc(self.cleared, 1)
        dve.wait_ge(self.cleared, 1)

    def registers(self, q):
        return self.nc.values_load_multi_w_load_instructions(
            self.base[0:1, bass.ds(q * PAIRS, PAIRS)], engines=(self.nc.vector.engine,),
            min_val=0, max_val=N)[1]

    def make_hots(self, dve, it, h, weights=None):
        dve.wait_ge(self.meta_loaded[h], it * 16 + 16)
        self.wait_read(dve, it, h)
        for t in range(TPR):
            at = self.meta[h][:, 2 * TPR + t:2 * TPR + t + 1]
            w = None if weights is None else weights[:, t:t + 1]
            last = self.nc.vector.tensor_scalar(self.hot[h][:, t, :], self.k.iota[:, :], at, w, ALU.is_equal,
                                                *(() if w is None else (ALU.mult,)))
        last.then_inc(self.hots[h], 1)

    def add_pair(self, dve, it, h, pair, at):
        w, q, n = self.width, it * 2 + h, self.slots
        dve.wait_ge(self.summed[h], it * PAIRS + (pair + 1))
        before = pair - 1
        dve.wait_ge(self.added[before % n], q * (PAIRS // n) + (before // n + 1 if pair else 0))
        to = self.acc[0:w, bass.ds(at, WIN)]
        self.nc.vector.tensor_tensor(to, self.ps[pair % n][0:w, :], to, ALU.add).then_inc(self.added[pair % n], 1)

    def sum_pair(self, pe, it, h, pair, row_of_tile):
        q, n = it * 2 + h, self.slots
        pe.wait_ge(self.added[pair % n], q * (PAIRS // n) + pair // n)
        for j in range(2):
            t = 2 * pair + j
            last = self.nc.tensor.matmul(self.ps[pair % n][0:self.width, :], row_of_tile(t), self.hot[h][:, t, :],
                                         start=j == 0, stop=j == 1)
        last.then_inc(self.summed[h], 1)


def gather_and_sum(nc, sb, psum, sem, k, edge_meta, bases, table):
    sums = SumPass(nc, sb, psum, sem, k, "l0", bases, D)
    rows = [sb(f"rows{h}", [P, TPR, D], F32) for h in range(2)]
    gathered, g0 = k.pool_dma.take(ROWS // 2 * 16 * TPR)
    with nc.Block() as block:
        @block.sync
        def _(sp):
            sums.load_bases(sp)
            with sp.Fori(0, ROWS // 2) as it:
                for h in range(2):
                    sp.wait_ge(gathered[h], it * (16 * TPR) + g0[h])
                    sums.load_meta(sp, it, h, edge_meta)

        @block.gpsimd
        def _(pool):
            with pool.Fori(0, ROWS // 2) as it:
                for h in range(2):
                    pool.wait_ge(sums.meta_loaded[h], it * 16 + 16)
                    sums.wait_read(pool, it, h)
                    pool.sem_inc(k.turns, 1)
                    index = sums.meta[h][:, :].bitcast(U32)
                    for t in range(TPR):
                        pool.indirect_dma_start(out=rows[h][:, t, :], out_offset=None, in_=table,
                                                in_offset=bass.IndirectOffsetOnAxis(ap=index[:, t:t + 1], axis=0)
                                                ).then_inc(gathered[h], 16)

        @block.vector
        def _(dve):
            sums.start_dve(dve)
            with dve.Fori(0, ROWS // 2) as it:
                for h in range(2):
                    q = it * 2 + h
                    sums.make_hots(dve, it, h, sums.meta[h][:, TPR:2 * TPR])
                    at = sums.registers(q)
                    for pair in range(PAIRS):
                        sums.add_pair(dve, it, h, pair, at[pair])

        @block.tensor
        def _(pe):
            with pe.Fori(0, ROWS // 2) as it:
                for h in range(2):
                    pe.wait_ge(sums.hots[h], it + 1)
                    pe.wait_ge(gathered[h], it * (16 * TPR) + (g0[h] + 16 * TPR))
                    for pair in range(PAIRS):
                        sums.sum_pair(pe, it, h, pair, lambda t: rows[h][:, t, :])

GROUP = 7
NG = NB // GROUP
assert NG * GROUP == NB


class Signals:

    def __init__(self, sem):
        self.sem, self.sems = sem, {}

    def of(self, name):
        if name not in self.sems:
            self.sems[name] = self.sem(name)
        return self.sems[name]

    def raise_(self, ins, name, by=1):
        ins.then_inc(self.of(name), by)

    def wait(self, eng, name, it, by=1):
        eng.wait_ge(self.of(name), it * by + by)

    def wait_before(self, eng, name, it, by=1):
        eng.wait_ge(self.of(name), it * by)


def over_blocks(ap, n=GROUP):
    p, f = ap.shape
    return ap.rearrange("p (o f) -> p o f", o=1).to_broadcast([p, n, f])


def per_block(ap, f):
    p, n = ap.shape
    return ap.rearrange("p (n o) -> p n o", o=1).to_broadcast([p, n, f])


def update_nodes(nc, sb, psum, sem, k, *, mode, weights, biases, K, x_in=None, x_out=None, sums=None,
                 row_of=None, extra=None, tables=(), norm=None, cnt=None, own=None, loop=None):
    sig = Signals(sem)
    per_turn = 16 * GROUP * (2 if loop else 1)
    gathered, g0 = k.pool_dma.take(NG * per_turn if sums is not None else 0, 1)
    EF = extra.shape[-1] if extra is not None else D
    F = weights[0].shape[1]
    BANK = 512 // F if F <= 512 else 1
    banks = min(-(-GROUP // BANK), 4)
    rounds = [range(a, min(a + banks * BANK, GROUP)) for a in range(0, GROUP, banks * BANK)]
    x = sb("x", [P, GROUP, D], F32)
    s = sb("s", [P, GROUP, D], F32)
    h = sb("h", [P, GROUP, D], F32)
    t0 = sb("t0", [P, GROUP, D], F32)
    h_t = sb("h_t", [P, GROUP * P], F32)
    out = sb("out", [P, GROUP, F], F32)
    ex = sb("ex", [P, GROUP, D], F32)
    index = sb("index", [P, 2, GROUP], U32)
    loop_alpha = sb("loop_alpha", [P, GROUP, loop[0] if loop else 1], F32)
    stats = sb("stats", [P, GROUP, 6], F32)
    mv = sb("mv", [P, GROUP, 2], F32)
    rstd, dev, shift, count = (sb(n, [P, GROUP], F32) for n in ("rstd", "dev", "shift", "count"))
    eps = sb("eps", [P, 1], F32)
    w = sb("w", [P, F], F32)
    b_in = sb("b_in", [P, D], F32)
    b_out = sb("b_out", [P, F], F32)
    bn = sb("bn", [P, 6, D], F32)
    ps_t = psum("ps_t", [P, 2, 512], F32)
    ps_o = psum("ps_o", [P, banks, 512], F32)
    ready, made = sem("nodes_ready"), sem("nodes_made")
    has_x, has_sums = x_in is not None, sums is not None
    n_loads = 0

    def wide(v, f):
        return v.rearrange("(o f) -> o f", o=1).to_broadcast([P, f])
    with nc.Block() as block:
        @block.sync
        def _(sp):
            nonlocal n_loads
            loads = [(w[0:K, :], weights[0])]
            if biases[0] is not None:
                f = biases[0].shape[0]
                loads.append((b_in[:, 0:f], wide(biases[0], f)))
            at = 0
            for b, f in biases[1]:
                if b is not None:
                    loads.append((b_out[:, at:at + f], wide(b, f)))
                at += f
            for i, v in enumerate(norm or ()):
                loads.append((bn[:, i, :], wide(v, D)))
            if biases[1]:
                sp.wait_ge(made, 1)
            for to, of in loads:
                sp.dma_start(to, of).then_inc(ready, 16)
            n_loads = len(loads)
            with sp.Fori(0, NG) as it:
                sig.wait_before(sp, "h_made", it)
                sp.sem_inc(k.held, 1)
                if has_x:
                    if x_out is not None:
                        sig.wait_before(sp, "x_stored", it, 16)
                    sig.raise_(sp.dma_start(x[:, :, :], x_in[it]), "x_loaded", 16)
                if extra is not None:
                    sig.raise_(sp.dma_start(ex[:, :, 0:EF], extra[it]), "extra_loaded", 16)
                if x_out is not None:
                    sig.wait(sp, "x_made", it)
                    sig.raise_(sp.dma_start(x_out[it], x[:, :, :]), "x_stored", 16)
                sig.wait(sp, "out_made", it)
                for i, (table, a, f) in enumerate(tables):
                    ins = sp.dma_start(table[it], out[:, :, a:a + f])
                    sig.raise_(ins, f"table{i}_stored", 16)
            for i in range(len(tables)):
                sig.wait(sp, f"table{i}_stored", NG - 1, 16)
            if x_out is not None:
                sig.wait(sp, "x_stored", NG - 1, 16)

        @block.gpsimd
        def _(pool):
            if has_sums:
                with pool.Fori(0, NG) as it:
                    sig.wait(pool, "index_made", it)
                    sig.wait_before(pool, "h_made", it)
                    pool.sem_inc(k.turns, 1)
                    for j in range(GROUP):
                        pool.indirect_dma_start(
                            out=s[:, j, :], out_offset=None, in_=sums,
                            in_offset=bass.IndirectOffsetOnAxis(ap=index[:, 0, j:j + 1], axis=0)).then_inc(gathered[0], 16)
                        if loop:
                            pool.indirect_dma_start(
                                out=loop_alpha[:, j, :], out_offset=None, in_=loop[1],
                                in_offset=bass.IndirectOffsetOnAxis(ap=index[:, 1, j:j + 1], axis=0)).then_inc(gathered[0], 16)

        @block.vector
        def _(dve):
            nc.vector.memset(eps[:, :], 1e-5)
            if norm:
                nc.vector.memset(bn[:, 4, :], 1e-3)
            nc.vector.memset(b_out[:, :], 0.0).then_inc(made, 1)
            dve.wait_ge(made, 1)
            dve.wait_ge(ready, n_loads * 16)
            if norm:
                c = Chain(dve, made, 1)
                c.step(nc.vector.tensor_tensor(bn[:, 4, :], bn[:, 4, :], bn[:, 3, :], ALU.add))
                dve.wait_ge(made, 3)
                c.n += 1
                c.step(nc.vector.reciprocal(bn[:, 5, :], bn[:, 5, :]))
                c.step(nc.vector.tensor_tensor(bn[:, 4, :], bn[:, 5, :], bn[:, 0, :], ALU.mult))
                c.step(nc.vector.tensor_tensor(bn[:, 5, :], bn[:, 4, :], bn[:, 2, :], ALU.mult))
                c.step(nc.vector.tensor_tensor(bn[:, 5, :], bn[:, 1, :], bn[:, 5, :], ALU.subtract))
            with dve.Fori(0, NG) as it:
                if has_sums:
                    dve.wait_ge(gathered[0], it * per_turn + g0[0])
                    if loop:
                        nc.vector.tensor_copy(index[:, 1, :], loop[2][:, bass.ds(it * GROUP, GROUP)])
                    sig.raise_(nc.vector.tensor_copy(index[:, 0, :], row_of[:, bass.ds(it * GROUP, GROUP)]), "index_made")
                    dve.wait_ge(gathered[0], it * per_turn + (g0[0] + per_turn))
                if has_x:
                    sig.wait(dve, "x_loaded", it, 16)
                if loop:
                    sig.wait(dve, "extra_loaded", it, 16)
                    by_head = ex[:, :, 0:EF].rearrange("p n (h c) -> p n h c", h=loop[0])
                    sig.raise_(nc.vector.tensor_tensor(by_head, by_head, loop_alpha[:, :, :].rearrange(
                        "p n (h o) -> p n h o", o=1).to_broadcast([P, GROUP, loop[0], EF // loop[0]]), ALU.mult), "l0")
                    sig.wait(dve, "l0", it)
                    sig.raise_(nc.vector.tensor_tensor(s[:, :, 0:EF], s[:, :, 0:EF], ex[:, :, 0:EF], ALU.add), "l1")
                    sig.wait(dve, "l1", it)
                if mode == "residual":
                    sig.raise_(nc.vector.tensor_tensor(s[:, :, :], s[:, :, :], over_blocks(b_in[:, :]), ALU.add), "u0")
                    sig.wait(dve, "u0", it)
                    sig.raise_(nc.vector.tensor_tensor(x[:, :, :], x[:, :, :], s[:, :, :], ALU.add), "x_made")
                    sig.wait(dve, "x_made", it)
                if mode == "norm":
                    sig.wait(dve, "extra_loaded", it, 16)
                    sig.raise_(nc.vector.tensor_scalar(count[:, :], cnt[:, bass.ds(it * GROUP, GROUP)], 1.0, None, ALU.max), "u0")
                    sig.wait(dve, "u0", it)
                    sig.raise_(nc.vector.reciprocal(count[:, :], count[:, :]), "u1")
                    sig.wait(dve, "u1", it)
                    sig.raise_(nc.vector.tensor_tensor(s[:, :, :], s[:, :, :], per_block(count[:, :], D), ALU.mult), "u2")
                    sig.wait(dve, "u2", it)
                    sig.raise_(nc.vector.tensor_tensor(s[:, :, :], s[:, :, :], ex[:, :, :], ALU.add), "u3")
                    sig.wait(dve, "u3", it)
                    sig.raise_(nc.vector.tensor_tensor(s[:, :, :], s[:, :, :], over_blocks(bn[:, 4, :]), ALU.mult), "u4")
                    sig.wait(dve, "u4", it)
                    sig.raise_(nc.vector.tensor_tensor(s[:, :, :], s[:, :, :], over_blocks(bn[:, 5, :]), ALU.add), "u5")
                    sig.wait(dve, "u5", it)
                    sig.raise_(nc.vector.scalar_tensor_tensor(x[:, :, :], s[:, :, :], 0.0, x[:, :, :], ALU.max, ALU.add), "x_made")
                    sig.wait(dve, "x_made", it)
                if mode == "elu":
                    sig.wait_before(dve, "h_turned", it)
                    sig.raise_(nc.vector.tensor_tensor(s[:, :, 0:K], s[:, :, 0:K], over_blocks(b_in[:, 0:K]), ALU.add), "u0")
                    sig.wait(dve, "u0", it)
                    sig.raise_(nc.vector.tensor_scalar(t0[:, :, 0:K], s[:, :, 0:K], 0.0, None, ALU.min), "u1")
                    sig.wait(dve, "exp_made", it)
                    sig.raise_(nc.vector.tensor_scalar(s[:, :, 0:K], s[:, :, 0:K], 0.0, None, ALU.max), "u2")
                    sig.wait(dve, "u2", it)
                    sig.raise_(nc.vector.scalar_tensor_tensor(h[:, :, 0:K], t0[:, :, 0:K], -1.0, s[:, :, 0:K], ALU.add, ALU.add), "h_made")
                    sig.wait(dve, "h_made", it)
                else:
                    sig.wait_before(dve, "h_made", it)
                    for j in range(GROUP):
                        last = nc.vector.bn_stats(stats[:, j, :], x[:, j, :])
                    sig.raise_(last, "n0")
                    sig.wait(dve, "n0", it)
                    dve.sem_inc(k.held, 1)
                    for j in range(GROUP):
                        last = nc.vector.bn_aggr(mv[:, j, :], stats[:, j, :])
                    sig.raise_(last, "stats_made")
                    sig.wait(dve, "dev_made", it)
                    sig.raise_(nc.vector.reciprocal(rstd[:, :], dev[:, :]), "n1")
                    sig.wait(dve, "n1", it)
                    sig.raise_(nc.vector.scalar_tensor_tensor(shift[:, :], mv[:, :, 0], -1.0, rstd[:, :], ALU.mult, ALU.mult), "scale_made")
                for i in range(len(tables)):
                    sig.wait_before(dve, f"table{i}_stored", it, 16)
                for r, blocks in enumerate(rounds):
                    sig.wait(dve, f"product{r}_made", it)
                    for b, a in enumerate(range(blocks[0], blocks[-1] + 1, BANK)):
                        n = min(BANK, blocks[-1] + 1 - a)
                        last = nc.vector.tensor_tensor(out[:, a:a + n, :], ps_o[:, b, 0:n * F].rearrange("p (n f) -> p n f", n=n),
                                                       over_blocks(b_out[:, :], n), ALU.add)
                    sig.raise_(last, "out_made" if r == len(rounds) - 1 else "bank_read")
                if own is not None:
                    sig.wait(dve, "out_made", it)
                    sig.raise_(nc.vector.tensor_copy(own[:, bass.ds(it * GROUP, GROUP), :],
                                                     out[:, :, F - own.shape[2]:F]), "own_copied")
                    sig.wait(dve, "own_copied", it)

        @block.scalar
        def _(act):
            if norm:
                act.wait_ge(made, 2)
                nc.scalar.activation(bn[:, 5, :], bn[:, 4, :], ACT.Sqrt).then_inc(made, 1)
            else:
                act.wait_ge(made, 1)
            with act.Fori(0, NG) as it:
                if mode == "elu":
                    sig.wait(act, "u1", it)
                    sig.raise_(nc.scalar.activation(t0[:, :, 0:K], t0[:, :, 0:K], ACT.Exp), "exp_made")
                else:
                    sig.wait(act, "stats_made", it)
                    sig.raise_(nc.scalar.activation(dev[:, :], mv[:, :, 1], ACT.Sqrt, bias=eps[:, :]), "dev_made")
                    sig.wait(act, "scale_made", it)
                    sig.wait_before(act, "h_turned", it)
                    for j in range(GROUP):
                        last = nc.scalar.activation(h[:, j, :], x[:, j, :], ACT.Relu, scale=rstd[:, j:j + 1], bias=shift[:, j:j + 1])
                    sig.raise_(last, "h_made")
                sig.wait(act, "h_turned", it)
                sig.wait_before(act, f"product{len(rounds) - 1}_made", it)
                nc.scalar.copy(h_t[0:K, 0:512], ps_t[0:K, 0, :])
                sig.raise_(nc.scalar.copy(h_t[0:K, 512:GROUP * P], ps_t[0:K, 1, 0:GROUP * P - 512]), "h_t_made")

        @block.tensor
        def _(pe):
            pe.wait_ge(ready, n_loads * 16)
            with pe.Fori(0, NG) as it:
                sig.wait(pe, "h_made", it)
                sig.wait_before(pe, "h_t_made", it)
                for j in range(GROUP):
                    last = nc.tensor.transpose(ps_t[0:K, j // 4, (j % 4) * P:(j % 4 + 1) * P], h[:, j, 0:K], k.ident[:, :])
                sig.raise_(last, "h_turned")
                sig.wait(pe, "h_t_made", it)
                sig.wait_before(pe, "out_made", it)
                for r, blocks in enumerate(rounds):
                    if r:
                        sig.wait(pe, "bank_read", it)
                    for j in blocks:
                        i = j - blocks[0]
                        last = nc.tensor.matmul(ps_o[:, i // BANK, (i % BANK) * F:(i % BANK + 1) * F],
                                                h_t[0:K, j * P:(j + 1) * P], w[0:K, :], start=True, stop=True,
                                                skip_group_check=True)
                    sig.raise_(last, f"product{r}_made")


def fold_attention(nc, sb, psum, sem, k, layer, w, a_src, a_dst, K, folded):
    heads, c = a_src.shape
    F = heads * c
    w_sb, a_sb = sb("w", [P, F + 2 * heads], F32), sb("a", [P, 2 * heads], F32)
    w_t = sb("w_t", [P, P], F32)
    ps = psum("ps", [P, 2, P], F32)
    s = {x: sem(f"fold{layer}_{x}") for x in ("made", "loaded", "turned", "copied", "product", "done", "stored")}
    with nc.Block() as block:
        @block.sync
        def _(sp):
            sp.dma_start(w_sb[0:K, 0:F], w).then_inc(s["loaded"], 16)
            sp.wait_ge(s["made"], 1)
            for i, a in enumerate((a_src, a_dst)):
                for h in range(heads):
                    sp.dma_start(a_sb[h * c:(h + 1) * c, i * heads + h:i * heads + h + 1],
                                 a[h:h + 1, :].rearrange("o c -> c o")).then_inc(s["loaded"], 16)
            sp.wait_ge(s["done"], 1)
            sp.dma_start(folded, w_sb[0:K, :]).then_inc(s["stored"], 16)
            sp.wait_ge(s["stored"], 16)

        @block.vector
        def _(dve):
            nc.vector.memset(a_sb[:, :], 0.0).then_inc(s["made"], 1)
            dve.wait_ge(s["turned"], 1)
            nc.vector.tensor_copy(w_t[0:F, 0:K], ps[0:F, 0, 0:K]).then_inc(s["copied"], 1)
            dve.wait_ge(s["product"], 1)
            nc.vector.tensor_copy(w_sb[0:K, F:F + 2 * heads], ps[0:K, 1, 0:2 * heads]).then_inc(s["done"], 1)

        @block.tensor
        def _(pe):
            pe.wait_ge(s["loaded"], (1 + 2 * heads) * 16)
            nc.tensor.transpose(ps[0:F, 0, 0:K], w_sb[0:K, 0:F], k.ident[0:K, 0:K]).then_inc(s["turned"], 1)
            pe.wait_ge(s["copied"], 1)
            nc.tensor.matmul(ps[0:K, 1, 0:2 * heads], w_t[0:F, 0:K], a_sb[0:F, :], start=True, stop=True).then_inc(s["product"], 1)


def finish_nodes(nc, sb, psum, sem, k, *, x_in, own, sums, row_of, has, w1b, w2, b2, x_out):
    sig = Signals(sem)
    gathered, g0 = k.pool_dma.take(NG * 16 * GROUP, 1)
    x, s, r = (sb(n, [P, GROUP, D], F32) for n in ("x", "s", "r"))
    o = sb("own", [P, GROUP, 2 * D], F32)
    flag = sb("flag", [P, GROUP], F32)
    index = sb("index", [P, GROUP], U32)
    turned = sb("turned", [P, GROUP * P], F32)
    w = sb("w", [P, 2, D], F32)
    b = sb("b", [P, D], F32)
    ps_t, ps_o = psum("ps_t", [P, 2, 512], F32), psum("ps_o", [P, 2, 512], F32)
    ready = sem("nodes_ready")
    with nc.Block() as block:
        @block.sync
        def _(sp):
            sp.dma_start(w[:, 0, :], w1b).then_inc(ready, 16)
            sp.dma_start(w[:, 1, :], w2).then_inc(ready, 16)
            sp.dma_start(b[:, :], b2.rearrange("(o f) -> o f", o=1).to_broadcast([P, D])).then_inc(ready, 16)
            with sp.Fori(0, NG) as it:
                sig.wait_before(sp, "x_stored", it, 16)
                sig.raise_(sp.dma_start(x[:, :, :], x_in[it]), "x_loaded", 16)
                sig.raise_(sp.dma_start(o[:, :, :], own[it]), "extra_loaded", 16)
                sig.wait(sp, "out_made", it)
                sig.raise_(sp.dma_start(x_out[it], x[:, :, :]), "x_stored", 16)
            sig.wait(sp, "x_stored", NG - 1, 16)

        @block.gpsimd
        def _(pool):
            with pool.Fori(0, NG) as it:
                sig.wait(pool, "index_made", it)
                pool.sem_inc(k.turns, 1)
                for j in range(GROUP):
                    pool.indirect_dma_start(
                        out=s[:, j, :], out_offset=None, in_=sums,
                        in_offset=bass.IndirectOffsetOnAxis(ap=index[:, j:j + 1], axis=0)).then_inc(gathered[0], 16)

        @block.vector
        def _(dve):
            dve.wait_ge(ready, 48)
            with dve.Fori(0, NG) as it:
                sig.wait_before(dve, "out_made", it)
                nc.vector.tensor_copy(flag[:, :], has[:, bass.ds(it * GROUP, GROUP)])
                sig.raise_(nc.vector.tensor_copy(index[:, :], row_of[:, bass.ds(it * GROUP, GROUP)]), "index_made")
                sig.wait(dve, "index_made", it)
                dve.wait_ge(gathered[0], it * (16 * GROUP) + (g0[0] + 16 * GROUP))
                sig.wait(dve, "extra_loaded", it, 16)
                sig.raise_(nc.vector.tensor_tensor(s[:, :, :], s[:, :, :], o[:, :, 0:D], ALU.add), "u0")
                sig.wait(dve, "u0", it)
                sig.raise_(nc.vector.tensor_tensor(s[:, :, :], s[:, :, :], per_block(flag[:, :], D), ALU.mult), "h_made")
                sig.wait(dve, "product_made", it)
                for i, (a, n) in enumerate(((0, 4), (4, GROUP - 4))):
                    last = nc.vector.tensor_tensor(r[:, a:a + n, :], ps_o[:, i, 0:n * D].rearrange("p (n f) -> p n f", n=n),
                                                   o[:, a:a + n, D:2 * D], ALU.add)
                sig.raise_(last, "u1")
                sig.wait(dve, "u1", it)
                sig.raise_(nc.vector.tensor_scalar(r[:, :, :], r[:, :, :], 0.0, None, ALU.max), "u2")
                sig.wait(dve, "x_loaded", it, 16)
                sig.raise_(nc.vector.tensor_tensor(x[:, :, :], x[:, :, :], over_blocks(b[:, :]), ALU.add), "u3")
                sig.wait(dve, "u3", it)
                sig.wait(dve, "product2_made", it)
                for i, (a, n) in enumerate(((0, 4), (4, GROUP - 4))):
                    last = nc.vector.tensor_tensor(x[:, a:a + n, :], ps_o[:, i, 0:n * D].rearrange("p (n f) -> p n f", n=n),
                                                   x[:, a:a + n, :], ALU.add)
                sig.raise_(last, "out_made")

        @block.scalar
        def _(act):
            with act.Fori(0, NG) as it:
                for x in ("h_turned", "r_turned"):
                    sig.wait(act, x, it)
                    nc.scalar.copy(turned[:, 0:512], ps_t[:, 0, :])
                    sig.raise_(nc.scalar.copy(turned[:, 512:GROUP * P], ps_t[:, 1, 0:GROUP * P - 512]), x + "_copied")

        @block.tensor
        def _(pe):
            pe.wait_ge(ready, 48)
            with pe.Fori(0, NG) as it:
                sig.wait_before(pe, "out_made", it)
                for i, (src, made, name_t, product) in enumerate(((s, "h_made", "h_turned", "product_made"),
                                                                  (r, "u2", "r_turned", "product2_made"))):
                    sig.wait(pe, made, it)
                    for j in range(GROUP):
                        last = nc.tensor.transpose(ps_t[:, j // 4, (j % 4) * P:(j % 4 + 1) * P], src[:, j, :], k.ident[:, :])
                    sig.raise_(last, name_t)
                    sig.wait(pe, name_t + "_copied", it)
                    for j in range(GROUP):
                        last = nc.tensor.matmul(ps_o[:, j // 4, (j % 4) * P:(j % 4 + 1) * P], turned[:, j * P:(j + 1) * P],
                                                w[:, i, :], start=True, stop=True, skip_group_check=True)
                    sig.raise_(last, product)
def gather_rows(nc, sb, psum, sem, k, F, H, edge_meta, table, rows_out, scores_out):
    WROW = F + H
    meta = [sb(f"meta{h}", [P, TPR], U32) for h in range(2)]
    rows = [sb(f"rows{h}", [P, TPR, WROW], F32) for h in range(2)]
    score = [sb(f"score{h}", [TPR * H, P], F32) for h in range(2)]
    ps = [psum(f"ps{h}", [TPR * H, P], F32) for h in range(2)]
    gathered, g0 = k.pool_dma.take(ROWS // 2 * 16 * TPR)
    column = [sb(f"column{h}", [P, TPR * H], F32) for h in range(2)]
    loaded, picked, turned, copied, stored, kept = ([sem(f"gat_rows_{x}{h}") for h in range(2)] for x in
                                                    ("loaded", "picked", "turned", "copied", "stored", "kept"))
    with nc.Block() as block:
        @block.sync
        def _(sp):
            with sp.Fori(0, ROWS // 2) as it:
                for h in range(2):
                    sp.wait_ge(gathered[h], it * (16 * TPR) + g0[h])
                    sp.dma_start(meta[h][:, :], edge_meta[it * 2 + h, :, 0:TPR].bitcast(U32)).then_inc(loaded[h], 16)

        @block.gpsimd
        def _(pool):
            with pool.Fori(0, ROWS // 2) as it:
                for h in range(2):
                    pool.wait_ge(loaded[h], it * 16 + 16)
                    pool.wait_ge(stored[h], it * 16)
                    pool.wait_ge(turned[h], it)
                    pool.sem_inc(k.turns, 1)
                    for t in range(TPR):
                        pool.indirect_dma_start(out=rows[h][:, t, :], out_offset=None, in_=table,
                                                in_offset=bass.IndirectOffsetOnAxis(ap=meta[h][:, t:t + 1], axis=0)
                                                ).then_inc(gathered[h], 16)

        @block.tensor
        def _(pe):
            with pe.Fori(0, ROWS // 2) as it:
                for h in range(2):
                    pe.wait_ge(picked[h], it + 1)
                    pe.wait_ge(copied[h], it)
                    pe.sem_inc(k.held, 1)
                    nc.tensor.transpose(ps[h][:, :], column[h][:, :], k.ident[:, :]).then_inc(turned[h], 1)

        @block.vector
        def _(dve):
            with dve.Fori(0, ROWS // 2) as it:
                for h in range(2):
                    dve.wait_ge(turned[h], it + 1)
                    dve.wait_ge(kept[h], it * 16)
                    nc.vector.tensor_copy(score[h][:, :], ps[h][:, :]).then_inc(copied[h], 1)

        @block.scalar
        def _(act):
            with act.Fori(0, ROWS // 2) as it:
                for h in range(2):
                    act.wait_ge(gathered[h], it * (16 * TPR) + (g0[h] + 16 * TPR))
                    act.dma_start(rows_out[it * 2 + h], rows[h][:, :, :]).then_inc(stored[h], 16)
                    act.wait_ge(turned[h], it)
                    nc.scalar.copy(column[h][:, :].rearrange("p (t h) -> p t h", h=H), rows[h][:, :, F:WROW]).then_inc(picked[h], 1)
                    act.wait_ge(copied[h], it + 1)
                    act.dma_start(scores_out[it * 2 + h], score[h][:, :]).then_inc(kept[h], 16)
            for h in range(2):
                act.wait_ge(stored[h], ROWS // 2 * 16)
                act.wait_ge(kept[h], ROWS // 2 * 16)


def place_scores(nc, sb, psum, sem, k, own, spot, placed):
    scattered, g0 = k.pool_dma.take(NB * 16, 1)
    with nc.Block() as block:
        @block.gpsimd
        def _(pool):
            for b in range(NB):
                pool.indirect_dma_start(out=placed, out_offset=bass.IndirectOffsetOnAxis(ap=spot[:, b:b + 1], axis=0),
                                        in_=own[:, b, :], in_offset=None).then_inc(scattered[0], 16)
            pool.wait_ge(scattered[0], g0[0] + NB * 16)


def softmax_by_segment(nc, sb, psum, sem, k, H, flags, scores, placed, alphas, loop_alphas):
    keep = [sb(f"keep{i}", [ROWS, COLS], F32) for i in range(2)]
    drop = [sb(f"drop{i}", [ROWS, COLS], F32) for i in range(2)]
    room = sb("room", [P, COLS * H], F32)
    sc = room[0:ROWS, :].rearrange("g (t h i) -> g t h i", t=TPR, h=H)
    packed = room[:, 0:ROWS * H * TPR].rearrange("p (g c) -> p g c", g=ROWS)
    v = sb("v", [ROWS, COLS, 2 * H], F32)
    alone = sb("alone", [ROWS, COLS, H], F32)
    one, two, p, m = (sb(x, [ROWS, COLS], F32) for x in ("one", "two", "p", "m"))
    totals = sb("totals", [ROWS, 4], F32)
    last, carry = sb("last", [ROWS, 1], F32), sb("carry", [ROWS, 1], F32)
    line = sb("line", [1, ROWS], F32)
    total_line = sb("total_line", [1, 4, ROWS], F32)
    run = sb("run", [1, ROWS + 2], F32)
    ps_line, ps_col = psum("ps_line", [1, ROWS], F32), psum("ps_col", [ROWS, 1], F32)
    ps = [psum(f"ps_turn{i}", [P, 512], F32) for i in range(2)]
    names = ("loaded", "steps", "asked", "answered", "shifted", "exp_made", "alpha_made", "loops_made", "turned", "evacuated", "stored")
    s = {x: sem(f"softmax_{x}") for x in names}
    BACK = (0, 0, 1, 0, 1)
    requests = 4 + 2 * len(BACK) * H
    with nc.Block() as block:
        @block.sync
        def _(sp):
            sp.dma_start(keep[0][:, :], flags[0]).then_inc(s["loaded"], 16)
            sp.dma_start(keep[1][:, :], flags[1]).then_inc(s["loaded"], 16)
            sp.dma_start(sc[:, :, :, :], scores.rearrange("g (t h) i -> g t h i", h=H)).then_inc(s["loaded"], 16)
            sp.dma_start(v[:, :, :], placed[0:EP, :].rearrange("(g c) h -> g c h", c=COLS)).then_inc(s["loaded"], 16)
            sp.dma_start(loop_alphas[EP:EP + P, :], k.ones[:, 0:H]).then_inc(s["stored"], 16)
            sp.wait_ge(s["loops_made"], H)
            sp.dma_start(loop_alphas[0:EP, :].rearrange("(g c) h -> g c h", c=COLS), alone[:, :, :]).then_inc(s["stored"], 16)
            sp.wait_ge(s["evacuated"], H * TPR // 4)
            sp.dma_start(alphas.rearrange("g p c -> p g c"), packed[:, :, :]).then_inc(s["stored"], 16)
            sp.wait_ge(s["stored"], 48)

        @block.vector
        def _(dve):
            c = Chain(dve, s["steps"])
            asked = Chain(dve, s["answered"])
            dve.wait_ge(s["loaded"], 64)

            def ask(ins):
                ins.then_inc(s["asked"], 1)
                asked.n += 1
                dve.wait_ge(s["answered"], asked.base + asked.n)

            for i in range(2):
                c.step(nc.vector.tensor_scalar(drop[i][:, :], keep[i][:, :], -BIG, None, ALU.mult))
                c.step(nc.vector.tensor_scalar(keep[i][:, :], keep[i][:, :], -1.0, 1.0, ALU.mult, ALU.add))
                for j, x in enumerate((keep[i], drop[i])):
                    n = 2 * i + j
                    ask(nc.vector.tensor_reduce(totals[:, n:n + 1], x[:, :], mybir.AxisListType.X, ALU.min))
                    c.step(nc.vector.tensor_copy(total_line[:, n, :], ps_line[:, :]))

            def running(out, data, back, largest):
                mask = (drop if largest else keep)[back]
                ops = (ALU.add, ALU.max) if largest else (ALU.mult, ALU.add)
                start = -BIG if largest else 0.0
                fl = (lambda a: a[:, ::-1]) if back else (lambda a: a)
                c.step(nc.vector.tensor_tensor_scan(fl(out), fl(mask[:, :]), fl(data), start, *ops))
                edge = 0 if back else COLS - 1
                c.step(nc.vector.memset(run[:, :], start))
                ask(nc.vector.tensor_copy(last[:, :], out[:, edge:edge + 1]))
                c.step(nc.vector.tensor_copy(line[:, :], ps_line[:, :]))
                ask(nc.vector.tensor_tensor_scan(fl(run[:, 1:ROWS + 1]), fl(total_line[:, 2 * back + largest, :]),
                                                 fl(line[:, :]), start, *ops))
                c.step(nc.vector.tensor_copy(carry[:, :], ps_col[:, :]))
                c.step(nc.vector.tensor_tensor_scan(fl(out), fl(mask[:, :]), fl(data), carry[:, 0:1], *ops))

            def tiled(a):
                return a[:, :].rearrange("g (t i) -> g t i", i=P)

            for h in range(H):
                own = alone[:, :, h]
                running(one[:, :], v[:, :, H + h], 0, 0)
                c.step(nc.vector.tensor_tensor(tiled(two), sc[:, :, h, :], tiled(one), ALU.add))
                c.step(nc.vector.scalar_tensor_tensor(p[:, :], two[:, :], 0.2, two[:, :], ALU.mult, ALU.max))
                c.step(nc.vector.tensor_tensor(two[:, :], v[:, :, h], v[:, :, H + h], ALU.add))
                c.step(nc.vector.scalar_tensor_tensor(m[:, :], two[:, :], 0.2, two[:, :], ALU.mult, ALU.max))
                c.step(nc.vector.scalar_tensor_tensor(own, keep[0][:, :], -BIG, m[:, :], ALU.mult, ALU.add))
                c.step(nc.vector.tensor_tensor(v[:, :, h], p[:, :], own, ALU.max))
                running(one[:, :], v[:, :, h], 0, 1)
                running(two[:, :], v[:, :, h], 1, 1)
                c.step(nc.vector.tensor_tensor(m[:, :], one[:, :], two[:, :], ALU.max))
                nc.vector.tensor_tensor(own, own, m[:, :], ALU.subtract)
                nc.vector.tensor_tensor(p[:, :], p[:, :], m[:, :], ALU.subtract).then_inc(s["shifted"], 1)
                dve.wait_ge(s["exp_made"], h + 1)
                c.step(nc.vector.tensor_tensor(v[:, :, h], p[:, :], own, ALU.add))
                running(one[:, :], v[:, :, h], 0, 0)
                running(two[:, :], v[:, :, h], 1, 0)
                c.step(nc.vector.tensor_tensor(m[:, :], one[:, :], two[:, :], ALU.add))
                c.step(nc.vector.tensor_tensor(m[:, :], m[:, :], v[:, :, h], ALU.subtract))
                c.step(nc.vector.tensor_scalar(m[:, :], m[:, :], 1e-16, None, ALU.add))
                c.step(nc.vector.reciprocal(m[:, :], m[:, :]))
                nc.vector.tensor_tensor(own, own, m[:, :], ALU.mult).then_inc(s["loops_made"], 1)
                nc.vector.tensor_tensor(v[:, :, h], p[:, :], m[:, :], ALU.mult).then_inc(s["alpha_made"], 1)
            c.step(nc.vector.memset(run[:, :], 0.0))
            to_tile_columns(nc, None, dve, "dve", [(v[:, :, h], F32) for h in range(H)], ps, packed, k.ident,
                            s["turned"], s["evacuated"])

        @block.scalar
        def _(act):
            for h in range(H):
                act.wait_ge(s["shifted"], h + 1)
                nc.scalar.activation(alone[:, :, h], alone[:, :, h], ACT.Exp)
                nc.scalar.activation(p[:, :], p[:, :], ACT.Exp).then_inc(s["exp_made"], 1)

        @block.tensor
        def _(pe):
            n = 0

            def answer(out, lhs_t, rhs):
                nonlocal n
                pe.wait_ge(s["asked"], n + 1)
                nc.tensor.matmul(out, lhs_t, rhs, start=True, stop=True).then_inc(s["answered"], 1)
                n += 1
            for i in range(4):
                answer(ps_line[:, :], totals[:, i:i + 1], k.ident[0:ROWS, 0:ROWS])
            for h in range(H):
                for back in BACK:
                    answer(ps_line[:, :], last[:, :], k.ident[0:ROWS, 0:ROWS])
                    at = 2 if back else 0
                    answer(ps_col[:, :], run[:, at:at + ROWS], k.ones[0:1, 0:1])
            assert n == requests
            pe.wait_ge(s["alpha_made"], H)
            to_tile_columns(nc, pe, None, "pe", [(v[:, :, h], F32) for h in range(H)], ps, packed, k.ident,
                            s["turned"], s["evacuated"])


def sum_weighted_rows(nc, sb, psum, sem, k, F, H, edge_meta, bases, rows_in, alphas):
    WROW = F + H
    sums = SumPass(nc, sb, psum, sem, k, "gat", bases, F)
    rows = [sb(f"rows{h}", [P, TPR, WROW], F32) for h in range(2)]
    alpha = [sb(f"alpha{h}", [P, H * TPR], F32) for h in range(2)]
    scaled = [sb(f"scaled{h}", [P, TPR, F], F32) for h in range(2)] if H > 1 else None
    rows_loaded, alpha_loaded, rows_scaled = ([sem(f"gat_{x}{h}") for h in range(2)] for x in
                                              ("rows_loaded", "alpha_loaded", "rows_scaled"))
    with nc.Block() as block:
        @block.sync
        def _(sp):
            sums.load_bases(sp)
            with sp.Fori(0, ROWS // 2) as it:
                for h in range(2):
                    sums.load_meta(sp, it, h, k.meta_dst)
                    if H > 1:
                        sp.wait_ge(rows_scaled[h], it)
                    else:
                        sums.wait_read(sp, it, h)
                    sp.dma_start(rows[h][:, :, :], rows_in[it * 2 + h]).then_inc(rows_loaded[h], 16)
                    sp.dma_start(alpha[h][:, :], alphas[it * 2 + h]).then_inc(alpha_loaded[h], 16)

        @block.vector
        def _(dve):
            sums.start_dve(dve)
            with dve.Fori(0, ROWS // 2) as it:
                for h in range(2):
                    q = it * 2 + h
                    if H == 1:
                        dve.wait_ge(alpha_loaded[h], it * 16 + 16)
                    sums.make_hots(dve, it, h, alpha[h] if H == 1 else None)
                    at = sums.registers(q)
                    for pair in range(PAIRS):
                        sums.add_pair(dve, it, h, pair, at[pair])

        if H > 1:
            @block.gpsimd
            def _(pool):
                with pool.Fori(0, ROWS // 2) as it:
                    for h in range(2):
                        pool.wait_ge(rows_loaded[h], it * 16 + 16)
                        pool.wait_ge(alpha_loaded[h], it * 16 + 16)
                        sums.wait_read(pool, it, h)
                        nc.gpsimd.tensor_tensor(
                            scaled[h][:, :, :].rearrange("p t (h c) -> p t h c", h=H),
                            rows[h][:, :, 0:F].rearrange("p t (h c) -> p t h c", h=H),
                            alpha[h][:, :].rearrange("p (h t o) -> p t h o", h=H, o=1).to_broadcast([P, TPR, H, F // H]),
                            ALU.mult).then_inc(rows_scaled[h], 1)

        @block.tensor
        def _(pe):
            with pe.Fori(0, ROWS // 2) as it:
                for h in range(2):
                    pe.wait_ge(sums.hots[h], it + 1)
                    if H > 1:
                        pe.wait_ge(rows_scaled[h], it + 1)
                        source = lambda t: scaled[h][:, t, :]
                    else:
                        pe.wait_ge(rows_loaded[h], it * 16 + 16)
                        source = lambda t: rows[h][:, t, 0:F]
                    for pair in range(PAIRS):
                        sums.sum_pair(pe, it, h, pair, source)
def sum_gated_messages(nc, sb, psum, sem, k, edge_meta, bases, table, edge_attr, w_gate, b_gate, w_filt, b_filt):
    sums = SumPass(nc, sb, psum, sem, k, "l2", bases, D)
    attr, near = ([sb(f"{x}{h}", [P, TPR, D], F32) for h in range(2)] for x in ("attr", "near"))
    msg = [sb(f"msg{h}", [P, TPR, D], F32) for h in range(2)]
    attr_t, gate, part = ([sb(f"{x}{i}", [P, D], F32) for i in range(2)] for x in ("attr_t", "gate", "part"))
    w = sb("w", [P, 2 * D], F32)
    b = sb("b", [1, 2 * D], F32)
    ps_e = [psum(f"ps_e{i}", [P, D], F32) for i in range(2)]
    ps_g = [psum(f"ps_g{i}", [P, 2 * D], F32) for i in range(2)]
    gathered, g0 = k.pool_dma.take(ROWS // 2 * 32 * TPR)
    made = [sem(f"l2_made{h}") for h in range(2)]
    turned, copied, product, gated, filtered = ([sem(f"l2_{x}{i}") for i in range(2)] for x in
                                                ("turned", "copied", "product", "gated", "filtered"))
    ready = sem("l2_ready")
    half = TPR // 2

    def nth(q, t):
        return q * half + t // 2
    with nc.Block() as block:
        @block.sync
        def _(sp):
            sums.load_bases(sp)
            for to, of in ((w[:, 0:D], w_gate), (w[:, D:2 * D], w_filt), (b[:, 0:D], b_gate.rearrange("(o f) -> o f", o=1)),
                           (b[:, D:2 * D], b_filt.rearrange("(o f) -> o f", o=1))):
                sp.dma_start(to, of).then_inc(ready, 16)
            with sp.Fori(0, ROWS // 2) as it:
                for h in range(2):
                    sp.wait_ge(gathered[h], it * (32 * TPR) + g0[h])
                    sums.load_meta(sp, it, h, edge_meta)

        @block.gpsimd
        def _(pool):
            with pool.Fori(0, ROWS // 2) as it:
                for h in range(2):
                    pool.wait_ge(sums.meta_loaded[h], it * 16 + 16)
                    sums.wait_read(pool, it, h)
                    pool.sem_inc(k.turns, 1)
                    index = sums.meta[h][:, :].bitcast(U32)
                    for t in range(TPR):
                        for to, of, c in ((attr, edge_attr, 3 * TPR), (near, table, 0)):
                            pool.indirect_dma_start(out=to[h][:, t, :], out_offset=None, in_=of,
                                                    in_offset=bass.IndirectOffsetOnAxis(ap=index[:, c + t:c + t + 1], axis=0)
                                                    ).then_inc(gathered[h], 16)

        @block.tensor
        def _(pe):
            pe.wait_ge(ready, 64)
            with pe.Fori(0, ROWS // 2) as it:
                for h in range(2):
                    q = it * 2 + h
                    pe.wait_ge(gathered[h], it * (32 * TPR) + (g0[h] + 32 * TPR))
                    pe.wait_ge(sums.hots[h], it + 1)
                    for step in range(TPR + 4):
                        t = step
                        if t < TPR:
                            pe.wait_ge(copied[t % 2], nth(q, t))
                            nc.tensor.transpose(ps_e[t % 2][:, :], attr[h][:, t, :], k.ident[:, :]).then_inc(turned[t % 2], 1)
                        t = step - 1
                        if 0 <= t < TPR:
                            pe.wait_ge(copied[t % 2], nth(q, t) + 1)
                            pe.wait_ge(filtered[t % 2], nth(q, t))
                            nc.tensor.matmul(ps_g[t % 2][:, :], k.ones[0:1, 0:P], b[:, :], start=True, stop=False)
                            nc.tensor.matmul(ps_g[t % 2][:, :], attr_t[t % 2][:, :], w[:, :], start=False,
                                             stop=True).then_inc(product[t % 2], 1)
                        t = step - 4
                        if t >= 0 and t % 2 == 1:
                            pe.wait_ge(made[h], it * TPR + t + 1)
                            sums.sum_pair(pe, it, h, t // 2, lambda t: msg[h][:, t, :])

        @block.scalar
        def _(act):
            with act.Fori(0, ROWS // 2) as it:
                for h in range(2):
                    q = it * 2 + h
                    for step in range(TPR + 1):
                        t = step
                        if t < TPR:
                            act.wait_ge(turned[t % 2], nth(q, t) + 1)
                            act.wait_ge(product[t % 2], nth(q, t))
                            nc.scalar.copy(attr_t[t % 2][:, :], ps_e[t % 2][:, :]).then_inc(copied[t % 2], 1)
                        t = step - 1
                        if t >= 0:
                            act.wait_ge(product[t % 2], nth(q, t) + 1)
                            act.wait_ge(filtered[t % 2], nth(q, t))
                            nc.scalar.activation(gate[t % 2][:, :], ps_g[t % 2][:, 0:D], ACT.Sigmoid).then_inc(gated[t % 2], 1)

        @block.vector
        def _(dve):
            sums.start_dve(dve)
            with dve.Fori(0, ROWS // 2) as it:
                for h in range(2):
                    q = it * 2 + h
                    sums.make_hots(dve, it, h)
                    at = sums.registers(q)
                    dve.wait_ge(gathered[h], it * (32 * TPR) + (g0[h] + 32 * TPR))
                    for t in range(TPR):
                        dve.wait_ge(gated[t % 2], nth(q, t) + 1)
                        dve.wait_ge(made[h], it * TPR + max(t - 1, 0))
                        nc.vector.tensor_tensor(part[t % 2][:, :], ps_g[t % 2][:, D:2 * D], gate[t % 2][:, :],
                                                ALU.mult).then_inc(filtered[t % 2], 1)
                        dve.wait_ge(filtered[t % 2], nth(q, t) + 1)
                        nc.vector.tensor_tensor(msg[h][:, t, :], part[t % 2][:, :], near[h][:, t, :], ALU.mult).then_inc(made[h], 1)
                        if t % 2 == 1 and t >= 5:
                            sums.add_pair(dve, it, h, (t - 5) // 2, at[(t - 5) // 2])
                    for pair in range(PAIRS - 2, PAIRS):
                        sums.add_pair(dve, it, h, pair, at[pair])


def largest_messages(nc, sb, psum, sem, k, edge_meta, bases, flags, table, w_edge):
    sums = SumPass(nc, sb, psum, sem, k, "l3", bases, D, slots=2)
    rows = [sb(f"rows{h}", [P, TPR, D], F32) for h in range(2)]
    first = sb("first", [ROWS, COLS], F32)
    drop = sb("drop", [ROWS, COLS], BF16)
    pick = [sb(f"pick{i}", [ROWS, P], BF16) for i in range(2)]
    wide = sb("wide", [P, D], F32)
    rows_t, best, back = ([sb(f"{x}{i}", [P, 4 * P], F32) for i in range(2)] for x in ("rows_t", "best", "back"))
    ps_d, ps_m, ps_b = ([psum(f"{x}{i}", [P, 4 * P], F32) for i in range(2)] for x in ("ps_d", "ps_m", "ps_b"))
    gathered, g0 = k.pool_dma.take(ROWS // 2 * 16 * TPR)
    mixed, picked = ([sem(f"l3_{x}{h}") for h in range(2)] for x in ("mixed", "picked"))
    turned, copied, spread, best_made, back_turned, back_copied = (
        [sem(f"l3_{x}{i}") for i in range(2)] for x in ("turned", "copied", "spread", "best_made", "back_turned", "back_copied"))
    ready, drop_made = sem("l3_ready"), sem("l3_drop_made")
    CH = TPR // 4

    def nth(q, c):
        return q * (CH // 2) + c // 2
    with nc.Block() as block:
        @block.sync
        def _(sp):
            sums.load_bases(sp)
            sp.dma_start(first[:, :], flags[0]).then_inc(ready, 16)
            sp.dma_start(wide[:, :], w_edge.to_broadcast([P, D])).then_inc(ready, 16)
            with sp.Fori(0, ROWS // 2) as it:
                for h in range(2):
                    sp.wait_ge(gathered[h], it * (16 * TPR) + g0[h])
                    sp.sem_inc(k.held, 1)
                    sp.wait_ge(mixed[h], it * CH)
                    sums.load_meta(sp, it, h, edge_meta)

        @block.gpsimd
        def _(pool):
            with pool.Fori(0, ROWS // 2) as it:
                for h in range(2):
                    pool.wait_ge(sums.meta_loaded[h], it * 16 + 16)
                    sums.wait_read(pool, it, h)
                    pool.sem_inc(k.turns, 1)
                    index = sums.meta[h][:, :].bitcast(U32)
                    for t in range(TPR):
                        pool.indirect_dma_start(out=rows[h][:, t, :], out_offset=None, in_=table,
                                                in_offset=bass.IndirectOffsetOnAxis(ap=index[:, t:t + 1], axis=0)
                                                ).then_inc(gathered[h], 16)

        @block.tensor
        def _(pe):
            pe.wait_ge(drop_made, 2)
            with pe.Fori(0, ROWS // 2) as it:
                for h in range(2):
                    q = it * 2 + h
                    pe.wait_ge(sums.hots[h], it + 1)
                    pe.wait_ge(picked[h], it + 1)
                    for step in range(CH + 2):
                        c = step
                        if c < CH:
                            i = c % 2
                            pe.wait_ge(best_made[i], nth(q, c))
                            nc.tensor.matmul(ps_d[i][:, :], pick[h][:, :], drop[:, c * 4 * P:(c + 1) * 4 * P],
                                             start=True, stop=True).then_inc(spread[i], 1)
                            pe.wait_ge(mixed[h], it * CH + (c + 1))
                            pe.wait_ge(copied[i], nth(q, c))
                            for j in range(4):
                                last = nc.tensor.transpose(ps_m[i][:, j * P:(j + 1) * P], rows[h][:, 4 * c + j, :], k.ident[:, :])
                            last.then_inc(turned[i], 1)
                        c = step - 1
                        if 0 <= c < CH:
                            i = c % 2
                            pe.wait_ge(best_made[i], nth(q, c) + 1)
                            pe.wait_ge(back_copied[i], nth(q, c))
                            for j in range(4):
                                last = nc.tensor.transpose(ps_b[i][:, j * P:(j + 1) * P], best[i][:, j * P:(j + 1) * P], k.ident[:, :])
                            last.then_inc(back_turned[i], 1)
                        c = step - 2
                        if c >= 0:
                            i = c % 2
                            pe.wait_ge(back_copied[i], nth(q, c) + 1)
                            for pair in (2 * c, 2 * c + 1):
                                sums.sum_pair(pe, it, h, pair, lambda t: back[i][:, (t % 4) * P:(t % 4 + 1) * P])

        @block.scalar
        def _(act):
            with act.Fori(0, ROWS // 2) as it:
                for h in range(2):
                    q = it * 2 + h
                    act.wait_ge(spread[1], q * (CH // 2))
                    nc.scalar.copy(pick[h][:, :], k.ident[0:ROWS, bass.ds(q, 1)].to_broadcast([ROWS, P])).then_inc(picked[h], 1)
                    for step in range(CH + 1):
                        c = step
                        if c < CH:
                            i = c % 2
                            act.wait_ge(turned[i], nth(q, c) + 1)
                            act.wait_ge(best_made[i], nth(q, c))
                            nc.scalar.copy(rows_t[i][:, :], ps_m[i][:, :]).then_inc(copied[i], 1)
                        c = step - 1
                        if c >= 0:
                            i = c % 2
                            act.wait_ge(back_turned[i], nth(q, c) + 1)
                            if c >= 2:
                                act.wait_ge(sums.summed[h], it * PAIRS + 2 * (c - 1))
                            elif h == 1:
                                act.wait_ge(sums.summed[0], it * PAIRS + (PAIRS - 2 * (1 - c)))
                            else:
                                act.wait_ge(sums.summed[1], it * PAIRS)
                            nc.scalar.copy(back[i][:, :], ps_b[i][:, :]).then_inc(back_copied[i], 1)

        @block.vector
        def _(dve):
            sums.start_dve(dve)
            dve.wait_ge(ready, 32)
            nc.vector.memset(best[1][:, :], -BIG).then_inc(drop_made, 1)
            nc.vector.tensor_scalar(drop[:, :], first[:, :], -BIG, None, ALU.mult).then_inc(drop_made, 1)
            dve.wait_ge(drop_made, 2)
            with dve.Fori(0, ROWS // 2) as it:
                for h in range(2):
                    q = it * 2 + h
                    sums.make_hots(dve, it, h, sums.meta[h][:, 3 * TPR:4 * TPR])
                    at = sums.registers(q)
                    dve.wait_ge(gathered[h], it * (16 * TPR) + (g0[h] + 16 * TPR))
                    for t in range(TPR):
                        ins = nc.vector.scalar_tensor_tensor(rows[h][:, t, :], wide[:, :], sums.meta[h][:, TPR + t:TPR + t + 1],
                                                             rows[h][:, t, :], ALU.mult, ALU.add)
                        if t % 4 == 3:
                            ins.then_inc(mixed[h], 1)
                    for c in range(CH + 1):
                        if c < CH:
                            i = c % 2
                            dve.wait_ge(spread[i], nth(q, c) + 1)
                            dve.wait_ge(copied[i], nth(q, c) + 1)
                            dve.wait_ge(back_turned[i], nth(q, c))
                            dve.wait_ge(best_made[1 - i], nth(q, c) + i)
                            nc.vector.tensor_tensor_scan(best[i][:, :], ps_d[i][:, :], rows_t[i][:, :],
                                                         best[1 - i][:, 4 * P - 1:4 * P], ALU.add, ALU.max).then_inc(best_made[i], 1)
                        if c >= 1:
                            for pair in (2 * c - 2, 2 * c - 1):
                                sums.add_pair(dve, it, h, pair, at[pair])
def copy_padded(nc, sb, psum, sem, k, src, dst, rows, total):
    done, zeroed = sem("copy_done"), sem("copy_zeroed")
    fill = total > rows
    z = sb("zeros", [total - rows, src.shape[1]], F32) if fill else None
    with nc.Block() as block:
        @block.sync
        def _(sp):
            sp.dma_start(dst[0:rows, :], src[0:rows, :]).then_inc(done, 16)
            if fill:
                sp.wait_ge(zeroed, 1)
                sp.dma_start(dst[rows:total, :], z[:, :]).then_inc(done, 16)
            sp.wait_ge(done, 32 if fill else 16)
        if fill:
            @block.vector
            def _(dve):
                nc.vector.memset(z[:, :], 0.0).then_inc(zeroed, 1)


def clear_rows(nc, sb, psum, sem, k, tensors):
    done, zeroed = sem("clear_done"), sem("clear_zeroed")
    width = (EP + P) // P * 2 * HEADS
    z = sb("zeros", [P, width], F32)
    with nc.Block() as block:
        @block.vector
        def _(dve):
            nc.vector.memset(z[:, :], 0.0).then_inc(zeroed, 1)

        @block.sync
        def _(sp):
            sp.wait_ge(zeroed, 1)
            for x in tensors:
                h = x.shape[1]
                sp.dma_start(x.rearrange("(p c) h -> p (c h)", p=P), z[:, 0:(EP + P) // P * h]).then_inc(done, 16)
            sp.wait_ge(done, 16 * len(tensors))


class PoolDmas:

    def __init__(self, make):
        self.make, self.counts = make, [0, 0]
        self.sems = make()

    def take(self, each, slots=2):
        if max(self.counts) + each >= 1 << 16:
            self.sems, self.counts = self.make(), [0, 0]
        before = list(self.counts)
        for i in range(slots):
            self.counts[i] += each
        return self.sems, before


class Store:
    pass


def gnn_kernel(nc, x, src, dst, edge_attr_128, edge_weight, L0_gnn_weight, L0_gnn_bias, L1_gnn_W1, L1_gnn_as1, L1_gnn_ad1,
               L1_gnn_b1, L1_gnn_W2, L1_gnn_as2, L1_gnn_ad2, L1_gnn_b2, L1_gnn_W3, L1_gnn_as3, L1_gnn_ad3, L1_gnn_b3,
               L2_gnn_W_node, L2_gnn_b_node, L2_gnn_W_gate, L2_gnn_b_gate, L2_gnn_W_filt, L2_gnn_b_filt, L2_gnn_bn_gamma,
               L2_gnn_bn_beta, L2_gnn_bn_mean, L2_gnn_bn_var, L3_gnn_Wm, L3_gnn_bm, L3_gnn_W1, L3_gnn_b1, L3_gnn_W2,
               L3_gnn_b2, out):
    def dram(name, shape, dt=F32):
        return nc.dram_tensor(name, shape, dt, kind="Internal").ap()

    def by_group(t):
        return t.rearrange("(g b p) f -> g p b f", b=GROUP, p=P)

    xs = [dram(f"x{i}", (NP, D)) for i in range(5)]
    own = dram("own", (NP, 2 * D))
    sort_meta = dram("sort_meta", (ROWS, P, 8 * TPR))
    ordered = {key: dram(f"ordered_{key}", (EP, 4)) for key in ("src", "dst")}
    meta = {key: dram(f"meta_{key}", (ROWS, P, 4 * TPR)) for key in ("src", "dst")}
    bases = {key: dram(f"bases_{key}", (1, ROWS * PAIRS), I32) for key in ("src", "dst")}
    flags = {key: dram(f"flags_{key}", (2, ROWS, COLS)) for key in ("src", "dst")}
    table_l0, table_l2, table_l3 = (dram(f"table_{i}", (NP, D)) for i in ("l0", "l2", "l3"))
    sums = dram("sums", (ORD, D))
    rows_kept = [dram(f"rows_kept{i}", (ROWS, P, TPR * w)) for i, w in ((0, HEADS * HID + HEADS), (1, D + 1))]
    gat = ((L1_gnn_W1, L1_gnn_as1, L1_gnn_ad1, L1_gnn_b1, D), (L1_gnn_W2, L1_gnn_as2, L1_gnn_ad2, L1_gnn_b2, HEADS * HID),
           (L1_gnn_W3, L1_gnn_as3, L1_gnn_ad3, L1_gnn_b3, HEADS * HID))
    heads = [a.shape[0] for _, a, _, _, _ in gat]
    width = [w.shape[1] for w, _, _, _, _ in gat]
    folded = [dram(f"folded{i}", (gat[i][4], width[i] + 2 * heads[i])) for i in range(3)]
    gat_table = [dram(f"gat_table{i}", (NP, width[i] + heads[i])) for i in range(3)]
    placed = [dram(f"placed{i}", (EP + P, 2 * h)) for i, h in ((0, HEADS), (1, 1))]
    loop_alphas = [dram(f"loop_alphas{i}", (EP + P, h)) for i, h in ((0, HEADS), (1, 1))]
    scores = [dram(f"scores{i}", (ROWS, TPR * h, P)) for i, h in ((0, HEADS), (1, 1))]
    alphas = [dram(f"alphas{i}", (ROWS, P, h * TPR)) for i, h in ((0, HEADS), (1, 1))]

    with ExitStack() as ctx:
        phases = [0]
        used = []

        def sem(name):
            used.append(nc.alloc_semaphore(name=f"{name}_{phases[0]}"))
            return used[-1]

        def keep(name, shape, dt=F32):
            return ctx.enter_context(nc.sbuf_tensor(name, shape, dt))

        k = Store()
        k.iota, k.spare, k.eid = keep("iota", [P, WIN]), keep("spare", [P, 1]), keep("edge_number", [ROWS, COLS])
        k.ones, k.ident, k.before, k.after = (keep(n, [P, P]) for n in ("ones", "ident", "before", "after"))
        cnt, start = ({key: keep(f"{n}_{key}", [P, NB]) for key in ("src", "dst")} for n in ("cnt", "start"))
        has_dst = keep("has_dst", [P, NB])
        own_score = [keep(f"own_score{h}", [P, NB, 2 * h]) for h in (HEADS, 1)]
        row_of, spot = ({key: keep(f"{n}_{key}", [P, NB], U32) for key in ("src", "dst")} for n in ("row_of", "spot"))
        k.held = nc.alloc_semaphore(name="waits_held")
        k.turns = nc.alloc_semaphore(name="pool_turns")
        k.pool_dma = PoolDmas(lambda: [nc.alloc_semaphore(name=f"pool_dma{h}_{phases[0]}") for h in range(2)])
        k.meta_dst = meta["dst"]

        def run(phase, *args, **kw):
            phases[0] += 1
            tag = f"p{phases[0]}_"
            with ExitStack() as st:
                phase(nc, lambda n, s, d: st.enter_context(nc.sbuf_tensor(tag + n, s, d)),
                      lambda n, s, d: st.enter_context(nc.psum_tensor(tag + n, s, d)), sem, k, *args, **kw)
            nc.clear_and_free_semaphores(used)
            nc.all_engine_barrier()
            used.clear()

        run(make_constants)
        run(copy_padded, x, xs[0], N, NP)
        run(clear_rows, placed)
        run(stage_edges, src, dst, edge_weight, sort_meta)
        for key in ("src", "dst"):
            run(count_keys, key, sort_meta, cnt[key])
            run(node_offsets, key, cnt[key], start[key], row_of[key], spot[key])
            run(sort_edges, key, sort_meta, start[key], ordered[key])
            run(lay_out_segments, key, ordered[key], meta[key], bases[key], flags[key])
        for i, (w, a_src, a_dst, _, K) in enumerate(gat):
            run(fold_attention, i, w, a_src, a_dst, K, folded[i])
        epoch = [0]

        def edge_pass(phase, *args):
            with ExitStack() as held:
                k.acc = held.enter_context(nc.sbuf_tensor(f"acc{epoch[0]}", [P, ORD], F32))
                run(phase, *args)
                run(unload_sums, k.acc, sums)
            epoch[0] += 1

        xg = [by_group(t) for t in xs]
        run(update_nodes, mode="first", weights=[L0_gnn_weight], biases=(None, ()), K=D, x_in=xg[0],
            tables=[(by_group(table_l0), 0, D)])
        edge_pass(gather_and_sum, meta["src"], bases["src"], table_l0)
        for i, (_, _, _, b, K) in enumerate(gat):
            F, H = width[i], heads[i]
            j = 0 if i < 2 else 1
            tables = [(by_group(gat_table[i]), 0, F + H)]
            if i == 0:
                run(update_nodes, mode="residual", weights=[folded[0]], biases=(L0_gnn_bias, ()), K=K,
                    x_in=xg[0], x_out=xg[1], sums=sums, row_of=row_of["src"], tables=tables, own=own_score[j])
            else:
                run(update_nodes, mode="elu", weights=[folded[i]], biases=(gat[i - 1][3], ()), K=K,
                    sums=sums, row_of=row_of["dst"], tables=tables, own=own_score[j],
                    extra=by_group(gat_table[i - 1][:, 0:width[i - 1]]), loop=(heads[i - 1], loop_alphas[0], spot["dst"]))
            run(place_scores, own_score[j], spot["dst"], placed[j])
            run(gather_rows, F, H, meta["dst"], gat_table[i], rows_kept[j], scores[j])
            run(softmax_by_segment, H, flags["dst"], scores[j], placed[j], alphas[j], loop_alphas[j])
            edge_pass(sum_weighted_rows, F, H, meta["dst"], bases["dst"], rows_kept[j], alphas[j])
        run(update_nodes, mode="residual", weights=[L2_gnn_W_node], biases=(gat[2][3], ((L2_gnn_b_node, D),)), K=D,
            x_in=xg[1], x_out=xg[2], sums=sums, row_of=row_of["dst"], tables=[(by_group(table_l2), 0, D)],
            extra=by_group(gat_table[2][:, 0:D]), loop=(1, loop_alphas[1], spot["dst"]))
        edge_pass(sum_gated_messages, meta["src"], bases["src"], table_l2, edge_attr_128, L2_gnn_W_gate, L2_gnn_b_gate,
                  L2_gnn_W_filt, L2_gnn_b_filt)
        w3 = dram("w3", (D, 3 * D))
        run(join_weights, w3, (L3_gnn_Wm[D:2 * D, :], L3_gnn_Wm[0:D, :], L3_gnn_W1[0:D, :]))
        run(update_nodes, mode="norm", weights=[w3], biases=(None, ((None, D), (L3_gnn_bm, D), (L3_gnn_b1, D))),
            K=D, x_in=xg[2], x_out=xg[3], sums=sums, row_of=row_of["src"], extra=by_group(table_l2),
            tables=[(by_group(table_l3), 0, D), (by_group(own), D, 2 * D)],
            norm=(L2_gnn_bn_gamma, L2_gnn_bn_beta, L2_gnn_bn_mean, L2_gnn_bn_var), cnt=cnt["src"])
        edge_pass(largest_messages, meta["dst"], bases["dst"], flags["dst"], table_l3, L3_gnn_Wm[2 * D:2 * D + 1, :])
        run(note_present, cnt["dst"], has_dst)
        run(finish_nodes, x_in=xg[3], own=by_group(own), sums=sums, row_of=row_of["dst"], has=has_dst,
            w1b=L3_gnn_W1[D:2 * D, :], w2=L3_gnn_W2, b2=L3_gnn_b2, x_out=xg[4])
        run(copy_padded, xs[4], out, N, N)


def join_weights(nc, sb, psum, sem, k, joined, parts):
    done = sem("weights_joined")
    with nc.Block() as block:
        @block.sync
        def _(sp):
            for i, w in enumerate(parts):
                sp.dma_start(joined[:, i * D:(i + 1) * D], w).then_inc(done, 16)
            sp.wait_ge(done, 16 * len(parts))


def note_present(nc, sb, psum, sem, k, cnt, has):
    made = sem("present_made")
    with nc.Block() as block:
        @block.vector
        def _(dve):
            nc.vector.tensor_scalar(has[:, :], cnt[:, :], 0.0, None, ALU.is_gt).then_inc(made, 1)
            dve.wait_ge(made, 1)


_INS = ['x', 'src', 'dst', 'edge_attr_128', 'edge_weight', 'L0_gnn_weight', 'L0_gnn_bias', 'L1_gnn_W1', 'L1_gnn_as1',
        'L1_gnn_ad1', 'L1_gnn_b1', 'L1_gnn_W2', 'L1_gnn_as2', 'L1_gnn_ad2', 'L1_gnn_b2', 'L1_gnn_W3', 'L1_gnn_as3',
        'L1_gnn_ad3', 'L1_gnn_b3', 'L2_gnn_W_node', 'L2_gnn_b_node', 'L2_gnn_W_gate', 'L2_gnn_b_gate', 'L2_gnn_W_filt',
        'L2_gnn_b_filt', 'L2_gnn_bn_gamma', 'L2_gnn_bn_beta', 'L2_gnn_bn_mean', 'L2_gnn_bn_var', 'L3_gnn_Wm',
        'L3_gnn_bm', 'L3_gnn_W1', 'L3_gnn_b1', 'L3_gnn_W2', 'L3_gnn_b2']


def kernel(**inputs):
    import numpy as _np
    import concourse.bacc as _bacc
    from concourse import mybir as _mybir
    from concourse.bass_utils import run_bass_kernel_spmd as _run

    nc = _bacc.Bacc("TRN2", target_bir_lowering=False, num_devices=1)
    arrays, args = {}, []
    for name in _INS:
        a = _np.ascontiguousarray(inputs[name])
        arrays[f"in_{name}"] = a
        args.append(nc.dram_tensor(f"in_{name}", a.shape, _mybir.dt.from_np(a.dtype), kind="ExternalInput").ap())
    args.append(nc.dram_tensor("out_0", (N, D), F32, kind="ExternalOutput").ap())
    gnn_kernel(nc, *args)
    r = _run(nc, [arrays], core_ids=[0])
    return r.results[0]["out_0"]
```

```python
import concourse.bass as bass
from concourse import mybir
from contextlib import ExitStack

F32 = mybir.dt.float32
BF16 = mybir.dt.bfloat16
I32 = mybir.dt.int32
U32 = mybir.dt.uint32
ALU = mybir.AluOpType
ACT = mybir.ActivationFunctionType

P = 128
N = 12500
E = 212500
D = 128
NB = -(-N // P)
NP = NB * P
COLS = 2048
ROWS = -(-E // COLS)
EP = ROWS * COLS
TPR = COLS // P
PAIRS = TPR // 2
WIN = 2 * P
FULL = E // COLS
LAST = E - FULL * COLS
PAD_NODE = NP - 1
ORD = 12800
ZERO_ROW = ORD - 1
HEADS = 3
HID = 32
BIG = 1.0e38
UP = 1
assert ROWS <= P and N < PAD_NODE and N + WIN < ZERO_ROW and ORD % 512 == 0


class Chain:

    def __init__(self, eng, sem, base=0):
        self.eng, self.sem, self.base, self.n = eng, sem, base, 0

    def step(self, ins):
        self.n += 1
        ins.then_inc(self.sem, 1)
        self.eng.wait_ge(self.sem, self.base + self.n + UP)


def make_constants(nc, sb, psum, sem, k):
    made = sem("constants_made")
    with k.block() as block:
        @block.gpsimd
        def _(pool):
            c = Chain(pool, made)
            nc.gpsimd.iota(k.iota[:, :], [[1, WIN]], base=0, channel_multiplier=0,
                           allow_small_or_imprecise_dtypes=True)
            nc.gpsimd.iota(k.spare[:, :], [[1, 1]], base=EP, channel_multiplier=1,
                           allow_small_or_imprecise_dtypes=True)
            nc.gpsimd.iota(k.eid[:, :], [[1, COLS]], base=0, channel_multiplier=COLS,
                           allow_small_or_imprecise_dtypes=True)
            nc.gpsimd.iota(k.number[:, :], [[1, 1]], base=0, channel_multiplier=1,
                           allow_small_or_imprecise_dtypes=True)
            nc.gpsimd.iota(k.joiner[:, :], [[1, 1]], base=1, channel_multiplier=P - 1,
                           allow_small_or_imprecise_dtypes=True)
            c.step(nc.gpsimd.memset(k.ones[:, :], 1.0))
            c.step(nc.gpsimd.memset(k.ident[:, :], 0.0))
            nc.gpsimd.affine_select(out=k.ident[:, :], in_=k.ident[:, :], compare_op=ALU.not_equal, fill=1.0,
                                    base=0, pattern=[[-1, P]], channel_multiplier=1)
            nc.gpsimd.affine_select(out=k.before[:, :], in_=k.ones[:, :], compare_op=ALU.is_gt, fill=0.0,
                                    base=0, pattern=[[1, P]], channel_multiplier=-1)
            c.step(nc.gpsimd.affine_select(out=k.after[:, :], in_=k.ones[:, :], compare_op=ALU.is_gt, fill=0.0,
                                           base=0, pattern=[[-1, P]], channel_multiplier=1))


def to_tile_columns(nc, pe, dve, side, fields, ps, packed, ident, turned, evacuated):
    for f, (src, dtype) in enumerate(fields):
        for b in range(TPR // 4):
            n = f * (TPR // 4) + b
            if side == "pe":
                if n >= 2:
                    pe.wait_ge(evacuated, n - 1 + UP)
                for j in range(4):
                    t = 4 * b + j
                    last = nc.tensor.transpose(ps[n % 2][:, j * ROWS:(j + 1) * ROWS],
                                               src[:, t * P:(t + 1) * P], ident[0:ROWS, 0:ROWS])
                last.then_inc(turned, 1)
            else:
                dve.wait_ge(turned, n + 1 + UP)
                c0 = f * TPR + 4 * b
                out = packed[:, :, c0:c0 + 4]
                if dtype is not F32:
                    out = packed[:, :, :].bitcast(dtype)[:, :, c0:c0 + 4]
                nc.vector.tensor_copy(out.rearrange("p g j -> p j g"),
                                      ps[n % 2][:, 0:4 * ROWS].rearrange("p (j g) -> p j g", j=4)
                                      ).then_inc(evacuated, 1)


def stage_edges(nc, sb, psum, sem, k, src, dst, weight, sort_meta, key_rows):
    loaded, filled, turned, evacuated, stored, cut = (
        sem(f"edges_{x}") for x in ("loaded", "filled", "turned", "evacuated", "stored", "cut"))
    src_i, dst_i = sb("src_i", [ROWS, COLS], I32), sb("dst_i", [ROWS, COLS], I32)
    part = sb("part", [ROWS, COLS], I32)
    src_f, dst_f, w_f = (sb(x, [ROWS, COLS], F32) for x in ("src_f", "dst_f", "w_f"))
    halves = [sb(f"half{i}", [ROWS, COLS], F32) for i in range(4)]
    short = [sb(f"short{i}", [ROWS, COLS], BF16) for i in range(4)]
    packed = sb("packed", [P, ROWS, 8 * TPR], F32)
    ps = [psum(f"ps_turn{i}", [P, 512], F32) for i in range(2)]
    fields = [(x, F32) for x in (*halves, src_f, dst_f, w_f, k.eid)]
    with k.block() as block:
        @block.sync
        def _(sp):
            sp.wait_ge(filled, 1 + UP)
            for to, of in ((src_i, src), (dst_i, dst), (w_f, weight)):
                sp.dma_start(to[0:FULL, :], of[0:FULL * COLS].rearrange("(g c) -> g c", c=COLS)).then_inc(loaded, 16)
                sp.dma_start(to[FULL:ROWS, 0:LAST], of[FULL * COLS:E].rearrange("(g c) -> g c", g=1)).then_inc(loaded, 16)
            sp.wait_ge(cut, 12 + UP)
            for i, rows in enumerate(key_rows):
                for j in range(2):
                    sp.dma_start(rows[:, j, :], short[2 * i + j][:, :]).then_inc(stored, 16)
            sp.wait_ge(evacuated, 8 * TPR // 4 + UP)
            sp.dma_start(sort_meta.rearrange("g p c -> p g c"), packed[:, :, :]).then_inc(stored, 16)
            sp.wait_ge(stored, 5 * 16 + UP)

        @block.vector
        def _(dve):
            nc.vector.memset(src_i[:, :], PAD_NODE)
            nc.vector.memset(dst_i[:, :], PAD_NODE)
            nc.vector.memset(w_f[:, :], 0.0).then_inc(filled, 1)
            dve.wait_ge(loaded, 6 * 16 + UP)
            c = Chain(dve, cut)
            nc.vector.tensor_copy(src_f[:, :], src_i[:, :])
            nc.vector.tensor_copy(dst_f[:, :], dst_i[:, :])
            for i, key in enumerate((src_i, dst_i)):
                for j, (op, by) in enumerate(((ALU.bitwise_and, P - 1), (ALU.logical_shift_right, 7))):
                    c.step(nc.vector.tensor_scalar(part[:, :], key[:, :], by, None, op))
                    c.step(nc.vector.tensor_copy(halves[2 * i + j][:, :], part[:, :]))
            for i in range(4):
                c.step(nc.vector.tensor_copy(short[i][:, :], halves[i][:, :]))
            to_tile_columns(nc, None, dve, "dve", fields, ps, packed, k.ident, turned, evacuated)

        @block.tensor
        def _(pe):
            pe.wait_ge(cut, 8 + UP)
            to_tile_columns(nc, pe, None, "pe", fields, ps, packed, k.ident, turned, evacuated)


def count_keys(nc, sb, psum, sem, k, key, sort_meta, cnt):
    meta = [sb(f"meta{h}", [P, 2 * TPR], F32) for h in range(2)]
    hot = [sb(f"hot{h}", [P, TPR, 2, P], BF16) for h in range(2)]
    total = psum("ps_count", [P, P], F32)
    iota = sb("iota16", [P, P], BF16)
    loaded = [sem(f"count_{key}_loaded{h}") for h in range(2)]
    hots = [sem(f"count_{key}_hot{h}") for h in range(2)]
    used = [sem(f"count_{key}_used{h}") for h in range(2)]
    ready, copied = sem(f"count_{key}_iota"), sem(f"count_{key}_copied")
    c0 = 0 if key == "src" else 2 * TPR
    with k.block() as block:
        @block.sync
        def _(sp):
            with sp.Fori(0, ROWS // 2) as it:
                for h in range(2):
                    sp.wait_ge(hots[h], it + UP)
                    sp.dma_start(meta[h][:, :], sort_meta[it * 2 + h, :, c0:c0 + 2 * TPR]).then_inc(loaded[h], 16)

        @block.vector
        def _(dve):
            nc.vector.tensor_copy(iota[:, :], k.iota[:, 0:P]).then_inc(ready, 1)
            dve.wait_ge(ready, 1 + UP)
            with dve.Fori(0, ROWS // 2) as it:
                for h in range(2):
                    dve.wait_ge(loaded[h], it * 16 + 16 + UP)
                    dve.wait_ge(used[h], it + UP)
                    for t in range(TPR):
                        for half in range(2):
                            last = nc.vector.tensor_scalar(hot[h][:, t, half, :], iota[:, :],
                                                           meta[h][:, half * TPR + t:half * TPR + t + 1], None,
                                                           ALU.is_equal)
                    last.then_inc(hots[h], 1)
            for h in range(2):
                dve.wait_ge(used[h], ROWS // 2 + UP)
            nc.vector.tensor_copy(cnt[:, :], total[:, 0:NB]).then_inc(copied, 1)

        @block.tensor
        def _(pe):
            def group(h, n, first):
                pe.wait_ge(hots[h], n + UP)
                for t in range(TPR):
                    last = nc.tensor.matmul(total[:, :], hot[h][:, t, 0, :], hot[h][:, t, 1, :],
                                            start=first and t == 0, stop=True, skip_group_check=True)
                last.then_inc(used[h], 1)
            group(0, 1, True)
            group(1, 1, False)
            with pe.Fori(1, ROWS // 2) as it:
                for h in range(2):
                    group(h, it + 1, False)


def node_offsets(nc, sb, psum, sem, k, key, cnt, start, row_of, spot):
    has, col, run, tmp = (sb(x, [P, NB], F32) for x in ("has", "col", "run", "tmp"))
    ordf = sb("ordf", [P, NB], F32)
    ps = psum("ps_sums", [P, 2, 2, P], F32)
    d, summed = sem(f"offsets_{key}_steps"), sem(f"offsets_{key}_summed")
    with k.block() as block:
        @block.tensor
        def _(pe):
            pe.wait_ge(d, 1 + UP)
            for i, x in enumerate((cnt, has)):
                nc.tensor.matmul(ps[:, i, 0, 0:NB], k.ones[:, 0:P], x[:, :], start=True, stop=True)
                last = nc.tensor.matmul(ps[:, i, 1, 0:NB], k.before[:, :], x[:, :], start=True, stop=True)
            last.then_inc(summed, 1)

        @block.vector
        def _(dve):
            c = Chain(dve, d)
            c.step(nc.vector.tensor_scalar(has[:, :], cnt[:, :], 0.0, None, ALU.is_gt))
            dve.wait_ge(summed, 1 + UP)
            for i, out in enumerate((start, ordf)):
                c.step(nc.vector.tensor_copy(col[:, :], ps[:, i, 0, 0:NB]))
                c.step(nc.vector.tensor_tensor_scan(run[:, :], k.ones[:, 0:NB], col[:, :], 0.0, ALU.mult, ALU.add))
                c.step(nc.vector.tensor_tensor(tmp[:, :], run[:, :], col[:, :], ALU.subtract))
                c.step(nc.vector.tensor_tensor(out[:, :], tmp[:, :], ps[:, i, 1, 0:NB], ALU.add))
            c.step(nc.vector.scalar_tensor_tensor(tmp[:, :], ordf[:, :], -float(ZERO_ROW), has[:, :], ALU.add, ALU.mult))
            c.step(nc.vector.tensor_scalar(row_of[:, :], tmp[:, :], float(ZERO_ROW), None, ALU.add))
            c.step(nc.vector.scalar_tensor_tensor(tmp[:, :], start[:, :], k.spare[:, :], has[:, :], ALU.subtract, ALU.mult))
            c.step(nc.vector.tensor_scalar(spot[:, :], tmp[:, :], k.spare[:, :], None, ALU.add))


def sort_edges(nc, sb, psum, sem, k, key, sort_meta, key_rows, start, ordered):
    QUAD = 4
    CH = TPR // QUAD
    c0 = 0 if key == "src" else 2 * TPR
    field = 0 if key == "src" else 1
    meta = [sb(f"meta{h}", [P, 2 * TPR], F32) for h in range(2)]
    values = [sb(f"values{h}", [P, 4 * TPR], F32) for h in range(2)]
    key_row = [sb(f"key_row{h}", [2, COLS], BF16) for h in range(2)]
    moved = [sb(f"moved{h}", [P, TPR, 4], F32) for h in range(2)]
    hot = [sb(f"hot{i}", [P, QUAD, 2, P], BF16) for i in range(2)]
    low_t = [sb(f"low_t{i}", [P, QUAD * P], F32) for i in range(2)]
    table = [sb(f"table{i}", [P, NB], F32) for i in range(2)]
    equal = [sb(f"equal{i}", [P, QUAD, 2 * P], BF16) for i in range(2)]
    picked = [sb(f"picked{i}", [P, 2, NB], F32) for i in range(2)]
    parts = [sb(f"parts{h}", [P, 2, TPR], F32) for h in range(2)]
    place = [sb(f"place{h}", [P, TPR], U32) for h in range(2)]
    iota = sb("iota16", [P, P], BF16)
    join, low = sb("join", [2, P], BF16), sb("low", [2, P], BF16)
    wide_after = sb("wide_after", [P, 2 * P], F32)
    ps_key = [psum(f"ps_key{i}", [P, QUAD * P], F32) for i in range(2)]
    ps_low = [psum(f"ps_low{i}", [P, QUAD * P], F32) for i in range(2)]
    ps_read = [psum(f"ps_read{i}", [P, 2, NB], F32) for i in range(2)]
    ps_count = psum("ps_count", [P, NB], F32)
    s = {x: sem(f"sort_{key}_{x}") for x in ("ready", "seeded", "spread", "lows", "hots", "compared", "table_read",
                                            "table_grown", "table_copied", "answered")}
    scattered, g0 = k.pool_dma.take(ROWS // 2 * 16 * TPR)
    loaded, placed = ([sem(f"sort_{key}_{x}{h}") for h in range(2)] for x in ("loaded", "placed"))
    with k.block() as block:
        @block.sync
        def _(sp):
            with sp.Fori(0, ROWS // 2) as it:
                for h in range(2):
                    sp.wait_ge(placed[h], it + UP)
                    sp.dma_start(key_row[h][:, :], key_rows[it * 2 + h]).then_inc(loaded[h], 16)
                    sp.dma_start(meta[h][:, :], sort_meta[it * 2 + h, :, c0:c0 + 2 * TPR]).then_inc(loaded[h], 16)
                    sp.dma_start(values[h][:, :], sort_meta[it * 2 + h, :, 4 * TPR:8 * TPR]).then_inc(loaded[h], 16)

        @block.vector
        def _(dve):
            nc.vector.tensor_copy(wide_after[:, 0:P], k.ones[:, :])
            nc.vector.tensor_copy(wide_after[:, P:2 * P], k.after[:, :])
            nc.vector.tensor_copy(iota[:, :], k.iota[:, 0:P])
            nc.vector.tensor_scalar(join[:, :], k.ones[0:2, :], k.joiner[:, :], None, ALU.mult)
            nc.vector.tensor_scalar(low[:, :], k.ones[0:2, :], k.ident[0:2, 0:1], None, ALU.mult).then_inc(s["ready"], 1)
            dve.wait_ge(s["ready"], 1 + UP)
            with dve.Fori(0, ROWS // 2) as it:
                for h in range(2):
                    q = it * 2 + h
                    dve.wait_ge(loaded[h], it * 48 + 48 + UP)
                    dve.wait_ge(scattered[h], it * (16 * TPR) + g0[h])

                    def compare(c):
                        i, n = c % 2, q * CH + c
                        dve.wait_ge(s["answered"], (q * (2 * CH) + 2 * (c - 1) if c else q * (2 * CH)) + UP)
                        for t in range(QUAD * c, QUAD * c + QUAD):
                            for half in range(2):
                                last = nc.vector.tensor_scalar(hot[i][:, t % QUAD, half, :], iota[:, :],
                                                               meta[h][:, half * TPR + t:half * TPR + t + 1], None,
                                                               ALU.is_equal)
                        last.then_inc(s["hots"], 1)
                        dve.wait_ge(s["spread"], n + 1 + UP)
                        nc.vector.tensor_scalar(low_t[i][:, :], ps_low[i][:, :], k.number[:, :], None,
                                                ALU.is_equal).then_inc(s["lows"], 1)
                        for t in range(QUAD * c, QUAD * c + QUAD):
                            first, n_keys = (t % QUAD) // 2 * 2 * P, (t % 2 + 1) * P
                            last = nc.vector.scalar_tensor_tensor(
                                equal[i][:, t % QUAD, 0:n_keys], ps_key[i][:, first:first + n_keys],
                                values[h][:, field * TPR + t:field * TPR + t + 1], wide_after[:, 2 * P - n_keys:2 * P],
                                ALU.is_equal, ALU.mult, accum_out=parts[h][:, 0, t:t + 1])
                        last.then_inc(s["compared"], 1)

                    def read_answers(pair):
                        i = pair % 2
                        dve.wait_ge(s["table_read"], q * (2 * CH) + pair + 1 + UP)
                        dve.wait_ge(s["answered"], (q * (2 * CH) + (pair - 1) if pair else q * (2 * CH)) + UP)
                        for j in range(2):
                            t = 2 * pair + j
                            last = nc.vector.scalar_tensor_tensor(picked[i][:, j, :], ps_read[i][:, j, :], 1.0,
                                                                  hot[t // QUAD % 2][:, t % QUAD, 1, 0:NB], ALU.mult, ALU.mult,
                                                                  accum_out=parts[h][:, 1, t:t + 1])
                        last.then_inc(s["answered"], 1)
                    for c in range(CH + 1):
                        if c < CH:
                            compare(c)
                        if c:
                            read_answers(2 * c - 2)
                            read_answers(2 * c - 1)
                    dve.wait_ge(s["answered"], q * (2 * CH) + 2 * CH + UP)
                    dve.wait_ge(s["compared"], q * CH + CH + UP)
                    nc.vector.tensor_copy(moved[h][:, :, :].rearrange("p t c -> p c t"),
                                          values[h][:, :].rearrange("p (c t) -> p c t", c=4))
                    nc.vector.tensor_tensor(place[h][:, :], parts[h][:, 0, :], parts[h][:, 1, :],
                                            ALU.add).then_inc(placed[h], 1)

        @block.tensor
        def _(pe):
            pe.wait_ge(s["ready"], 1 + UP)
            nc.tensor.matmul(ps_count[:, :], k.ident[:, :], start[:, :], start=True, stop=True,
                             skip_group_check=True).then_inc(s["seeded"], 1)
            with pe.Fori(0, ROWS // 2) as it:
                for h in range(2):
                    q = it * 2 + h
                    pe.wait_ge(loaded[h], it * 48 + 48 + UP)

                    def spread(c):
                        i, n = c % 2, q * CH + c
                        pe.wait_ge(s["compared"], (n - 1 if c else q * CH) + UP)
                        row = key_row[h][:, c * QUAD * P:(c + 1) * QUAD * P]
                        nc.tensor.matmul(ps_low[i][:, :], low[:, :], row, start=True, stop=True)
                        nc.tensor.matmul(ps_key[i][:, :], join[:, :], row, start=True, stop=True).then_inc(s["spread"], 1)

                    spread(0)
                    for c in range(CH):
                        i = c % 2
                        if c + 1 < CH:
                            spread(c + 1)
                        pe.wait_ge(s["lows"], q * CH + (c + 1) + UP)
                        for pair in (2 * c, 2 * c + 1):
                            n = q * (2 * CH) + pair
                            pe.wait_ge(s["table_copied"], n + 1 + UP)
                            for t in (2 * pair, 2 * pair + 1):
                                last = nc.tensor.matmul(ps_count[:, :], hot[i][:, t % QUAD, 0, :],
                                                        hot[i][:, t % QUAD, 1, 0:NB], start=False,
                                                        stop=True, skip_group_check=True)
                            last.then_inc(s["table_grown"], 1)
                            pe.wait_ge(s["answered"], (n - 1 if pair >= 1 else n) + UP)
                            for t in (2 * pair, 2 * pair + 1):
                                last = nc.tensor.matmul(ps_read[pair % 2][:, t % 2, :], low_t[i][:, t % QUAD * P:(t % QUAD + 1) * P],
                                                        table[pair % 2][:, :], start=True, stop=True, skip_group_check=True)
                            last.then_inc(s["table_read"], 1)

        @block.scalar
        def _(act):
            act.wait_ge(s["seeded"], 1 + UP)
            nc.scalar.copy(table[0][:, :], ps_count[:, :]).then_inc(s["table_copied"], 1)
            with act.Fori(0, ROWS // 2) as it:
                for h in range(2):
                    for pair in range(PAIRS):
                        n = (it * 2 + h) * PAIRS + pair
                        act.wait_ge(s["table_grown"], n + 1 + UP)
                        act.wait_ge(s["table_read"], n + UP)
                        nc.scalar.copy(table[(pair + 1) % 2][:, :], ps_count[:, :]).then_inc(s["table_copied"], 1)

        @block.gpsimd
        def _(pool):
            with pool.Fori(0, ROWS // 2) as it:
                for h in range(2):
                    pool.wait_ge(placed[h], it + 1 + UP)
                    pool.sem_inc(k.turns, 1)
                    for t in range(TPR):
                        pool.indirect_dma_start(
                            out=ordered, out_offset=bass.IndirectOffsetOnAxis(ap=place[h][:, t:t + 1], axis=0),
                            in_=moved[h][:, t, :], in_offset=None).then_inc(scattered[h], 16)
            for h in range(2):
                pool.wait_ge(scattered[h], ROWS // 2 * 16 * TPR + g0[h])


def lay_out_segments(nc, sb, psum, sem, k, key, ordered, edge_meta, bases, flags):
    own, other = (0, 1) if key == "src" else (1, 0)
    rows = sb("rows", [ROWS, COLS, 4], F32)
    near = sb("near", [ROWS, 2], F32)
    first, end, ordn, rel = (sb(x, [ROWS, COLS], F32) for x in ("first", "end", "ordn", "rel"))
    cols = [sb(f"cols{i}", [ROWS, COLS], F32) for i in range(3)]
    low = sb("low", [ROWS, 1], F32)
    base_i = sb("base_i", [ROWS, PAIRS], I32)
    packed = sb("packed", [P, ROWS, 4 * TPR], F32)
    ps = [psum(f"ps_turn{i}", [P, 512], F32) for i in range(2)]
    ps_low = psum("ps_low", [P, 1], F32)
    names = ("loaded", "near", "next", "steps", "summed", "turned", "evacuated", "stored")
    s = {x: sem(f"segments_{key}_{x}") for x in names}
    last_field = cols[2] if key == "src" else end
    last_type = U32 if key == "src" else F32
    fields = [(cols[0], U32), (cols[1], F32), (rel, F32), (last_field, last_type)]
    with k.block() as block:
        @block.sync
        def _(sp):
            sp.dma_start(rows[:, :, :], ordered.rearrange("(g c) f -> g c f", c=COLS)).then_inc(s["loaded"], 16)
            sp.wait_ge(s["loaded"], 16 + UP)
            sp.wait_ge(s["steps"], 1 + UP)
            sp.dma_start(near[1:ROWS, 0:1], rows[0:ROWS - 1, COLS - 1, own:own + 1]).then_inc(s["near"], 16)
            sp.wait_ge(s["steps"], 3 + UP)
            sp.dma_start(near[0:ROWS - 1, 1:2], first[1:ROWS, 0:1]).then_inc(s["next"], 16)
            sp.wait_ge(s["evacuated"], 4 * TPR // 4 + UP)
            sp.dma_start(edge_meta.rearrange("g p c -> p g c"), packed[:, :, :]).then_inc(s["stored"], 16)
            sp.dma_start(bases.rearrange("a (g c) -> (a g) c", c=PAIRS), base_i[:, :]).then_inc(s["stored"], 16)
            sp.dma_start(flags[0], first[:, :]).then_inc(s["stored"], 16)
            sp.dma_start(flags[1], end[:, :]).then_inc(s["stored"], 16)
            sp.wait_ge(s["stored"], 64 + UP)

        @block.vector
        def _(dve):
            c = Chain(dve, s["steps"])
            nc.vector.memset(near[:, 0:1], -1.0)
            c.step(nc.vector.memset(near[:, 1:2], 1.0))
            dve.wait_ge(s["loaded"], 16 + UP)
            c.step(nc.vector.tensor_tensor(first[:, 1:COLS], rows[:, 1:COLS, own], rows[:, 0:COLS - 1, own], ALU.not_equal))
            dve.wait_ge(s["near"], 16 + UP)
            c.step(nc.vector.tensor_tensor(first[:, 0:1], rows[:, 0:1, own], near[:, 0:1], ALU.not_equal))
            c.step(nc.vector.tensor_copy(end[:, 0:COLS - 1], first[:, 1:COLS]))
            nc.vector.tensor_copy(cols[0][:, :], rows[:, :, other])
            nc.vector.tensor_copy(cols[1][:, :], rows[:, :, 2])
            if key == "src":
                nc.vector.tensor_scalar(cols[2][:, :], rows[:, :, 3], float(E - 1), None, ALU.min)
            c.step(nc.vector.memset(rel[:, :], 1.0))
            dve.wait_ge(s["next"], 16 + UP)
            c.step(nc.vector.tensor_copy(end[:, COLS - 1:COLS], near[:, 1:2]))
            c.step(nc.vector.tensor_tensor_scan(ordn[:, :], rel[:, :], first[:, :], -1.0, ALU.mult, ALU.add))
            c.step(nc.vector.tensor_scalar(low[:, :], ordn[:, COLS - 1:COLS], 1.0, None, ALU.add))
            dve.wait_ge(s["summed"], 1 + UP)
            c.step(nc.vector.tensor_copy(near[:, 0:1], ps_low[0:ROWS, :]))
            c.step(nc.vector.tensor_scalar(ordn[:, :], ordn[:, :], near[:, 0:1], None, ALU.add))
            by_pair = ordn[:, :].rearrange("p (k c) -> p k c", c=WIN)
            nc.vector.tensor_copy(base_i[:, :], by_pair[:, :, 0])
            c.step(nc.vector.tensor_tensor(rel[:, :].rearrange("p (k c) -> p k c", c=WIN), by_pair,
                                           by_pair[:, :, 0:1].to_broadcast([ROWS, PAIRS, WIN]), ALU.subtract))
            to_tile_columns(nc, None, dve, "dve", fields, ps, packed, k.ident, s["turned"], s["evacuated"])

        @block.tensor
        def _(pe):
            pe.wait_ge(s["steps"], 8 + UP)
            nc.tensor.matmul(ps_low[0:ROWS, :], k.before[0:ROWS, 0:ROWS], low[:, :], start=True, stop=True).then_inc(s["summed"], 1)
            pe.wait_ge(s["steps"], 11 + UP)
            to_tile_columns(nc, pe, None, "pe", fields, ps, packed, k.ident, s["turned"], s["evacuated"])


def unload_sums(nc, sb, psum, sem, k, acc, sums):
    stage = [sb(f"stage{i}", [P, 4 * P], F32) for i in range(2)]
    out = [sb(f"out{i}", [P, 4 * P], F32) for i in range(2)]
    ps = [psum(f"ps_unload{i}", [P, 4 * P], F32) for i in range(2)]
    fetched, turned, copied, stored = ([sem(f"unload_{x}{i}") for i in range(2)] for x in ("fetched", "turned", "copied", "stored"))
    steps = ORD // (4 * P)
    half = -(-steps // 2)
    with k.block() as block:
        @block.scalar
        def _(act):
            with act.Fori(0, half) as it:
                for i in range(2):
                    act.wait_ge(turned[i], it + UP)
                    nc.scalar.copy(stage[i][:, :], acc[:, bass.ds((it + i * (steps - half)) * 4 * P, 4 * P)]).then_inc(fetched[i], 1)

        @block.tensor
        def _(pe):
            with pe.Fori(0, half) as it:
                for i in range(2):
                    pe.wait_ge(fetched[i], it + 1 + UP)
                    pe.wait_ge(copied[i], it + UP)
                    for j in range(4):
                        last = nc.tensor.transpose(ps[i][:, j * P:(j + 1) * P], stage[i][:, j * P:(j + 1) * P], k.ident[:, :])
                    last.then_inc(turned[i], 1)

        @block.vector
        def _(dve):
            with dve.Fori(0, half) as it:
                for i in range(2):
                    dve.wait_ge(turned[i], it + 1 + UP)
                    dve.wait_ge(stored[i], it * 16 + UP)
                    nc.vector.tensor_copy(out[i][:, :], ps[i][:, :]).then_inc(copied[i], 1)

        @block.sync
        def _(sp):
            with sp.Fori(0, half) as it:
                for i in range(2):
                    sp.wait_ge(copied[i], it + 1 + UP)
                    if i == 1:
                        sp.wait_ge(stored[0], it * 16 + 16 + UP)
                    sp.dma_start(sums[bass.ds((it + i * (steps - half)) * 4 * P, 4 * P), :].rearrange("(j p) f -> p j f", p=P),
                                 out[i][:, :].rearrange("p (j f) -> p j f", j=4)).then_inc(stored[i], 16)
            for i in range(2):
                sp.wait_ge(stored[i], half * 16 + UP)


class SumPass:

    def __init__(self, nc, sb, psum, sem, k, name, bases, width, slots=4):
        self.nc, self.k, self.width, self.slots = nc, k, width, slots
        self.acc = k.acc
        self.bases_dram = bases
        self.base = sb("base", [1, ROWS * PAIRS], I32)
        self.meta = [sb(f"meta{h}", [P, 4 * TPR], F32) for h in range(2)]
        self.hot = [sb(f"hot{h}", [P, TPR, WIN], F32) for h in range(2)]
        self.ps = [psum(f"ps_sum{i}", [P, WIN], F32) for i in range(slots)]
        self.base_loaded, self.cleared = sem(f"{name}_base_loaded"), sem(f"{name}_cleared")
        self.meta_loaded, self.hots, self.summed = ([sem(f"{name}_{x}{h}") for h in range(2)]
                                                    for x in ("meta_loaded", "hots", "summed"))
        self.added = [sem(f"{name}_added{i}") for i in range(slots)]

    def wait_read(self, eng, it, h):
        eng.wait_ge(self.summed[h], it * PAIRS + UP)

    def load_bases(self, sp):
        sp.dma_start(self.base[:, :], self.bases_dram).then_inc(self.base_loaded, 16)

    def load_meta(self, sp, it, h, edge_meta):
        sp.wait_ge(self.hots[h], it + UP)
        sp.dma_start(self.meta[h][:, :], edge_meta[it * 2 + h]).then_inc(self.meta_loaded[h], 16)

    def start_dve(self, dve):
        dve.wait_ge(self.base_loaded, 16 + UP)
        self.nc.vector.memset(self.acc[:, :], 0.0).then_inc(self.cleared, 1)
        dve.wait_ge(self.cleared, 1 + UP)

    def registers(self, q):
        return self.nc.values_load_multi_w_load_instructions(
            self.base[0:1, bass.ds(q * PAIRS, PAIRS)], engines=(self.nc.vector.engine,),
            min_val=0, max_val=N)[1]

    def make_hots(self, dve, it, h, weights=None):
        dve.wait_ge(self.meta_loaded[h], it * 16 + 16 + UP)
        self.wait_read(dve, it, h)
        for t in range(TPR):
            at = self.meta[h][:, 2 * TPR + t:2 * TPR + t + 1]
            w = None if weights is None else weights[:, t:t + 1]
            last = self.nc.vector.tensor_scalar(self.hot[h][:, t, :], self.k.iota[:, :], at, w, ALU.is_equal,
                                                *(() if w is None else (ALU.mult,)))
        last.then_inc(self.hots[h], 1)

    def add_pair(self, dve, it, h, pair, at):
        w, q, n = self.width, it * 2 + h, self.slots
        dve.wait_ge(self.summed[h], it * PAIRS + (pair + 1) + UP)
        before = pair - 1
        dve.wait_ge(self.added[before % n], (q * (PAIRS // n) + (before // n + 1 if pair else 0)) + UP)
        to = self.acc[0:w, bass.ds(at, WIN)]
        self.nc.vector.tensor_tensor(to, self.ps[pair % n][0:w, :], to, ALU.add).then_inc(self.added[pair % n], 1)

    def sum_pair(self, pe, it, h, pair, row_of_tile):
        q, n = it * 2 + h, self.slots
        pe.wait_ge(self.added[pair % n], q * (PAIRS // n) + pair // n + UP)
        for j in range(2):
            t = 2 * pair + j
            last = self.nc.tensor.matmul(self.ps[pair % n][0:self.width, :], row_of_tile(t), self.hot[h][:, t, :],
                                         start=j == 0, stop=j == 1)
        last.then_inc(self.summed[h], 1)


def gather_and_sum(nc, sb, psum, sem, k, edge_meta, bases, table, factors=None):
    name = "l2" if factors is not None else "l0"
    sums = SumPass(nc, sb, psum, sem, k, name, bases, D)
    rows = [sb(f"rows{h}", [P, TPR, D], F32) for h in range(2)]
    factor = [sb(f"factor{h}", [P, TPR, D], F32) for h in range(2)] if factors is not None else None
    factor_loaded, multiplied = ([sem(f"{name}_{x}{h}") for h in range(2)] for x in ("factor_loaded", "multiplied"))
    gathered, g0 = k.pool_dma.take(ROWS // 2 * 16 * TPR)
    with k.block() as block:
        @block.sync
        def _(sp):
            sums.load_bases(sp)
            with sp.Fori(0, ROWS // 2) as it:
                for h in range(2):
                    sp.wait_ge(gathered[h], it * (16 * TPR) + g0[h])
                    sp.sem_inc(k.held, 1)
                    sums.load_meta(sp, it, h, edge_meta)
                    if factors is not None:
                        sp.wait_ge(multiplied[h], it * 2 + UP)
                        sp.dma_start(factor[h][:, :, :], factors[it * 2 + h]).then_inc(factor_loaded[h], 16)

        @block.gpsimd
        def _(pool):
            with pool.Fori(0, ROWS // 2) as it:
                for h in range(2):
                    pool.wait_ge(sums.meta_loaded[h], it * 16 + 16 + UP)
                    sums.wait_read(pool, it, h)
                    pool.sem_inc(k.turns, 1)
                    index = sums.meta[h][:, :].bitcast(U32)
                    for t in range(TPR):
                        pool.indirect_dma_start(out=rows[h][:, t, :], out_offset=None, in_=table,
                                                in_offset=bass.IndirectOffsetOnAxis(ap=index[:, t:t + 1], axis=0)
                                                ).then_inc(gathered[h], 16)

        @block.vector
        def _(dve):
            sums.start_dve(dve)
            with dve.Fori(0, ROWS // 2) as it:
                for h in range(2):
                    q = it * 2 + h
                    sums.make_hots(dve, it, h, None if factors is not None else sums.meta[h][:, TPR:2 * TPR])
                    at = sums.registers(q)
                    if factors is not None:
                        dve.wait_ge(factor_loaded[h], it * 16 + 16 + UP)
                        dve.wait_ge(gathered[h], it * (16 * TPR) + (g0[h] + 16 * TPR))
                        for a in (0, TPR // 2):
                            part = rows[h][:, a:a + TPR // 2, :]
                            nc.vector.tensor_tensor(part, part, factor[h][:, a:a + TPR // 2, :], ALU.mult).then_inc(multiplied[h], 1)
                    for pair in range(PAIRS):
                        sums.add_pair(dve, it, h, pair, at[pair])

        @block.tensor
        def _(pe):
            with pe.Fori(0, ROWS // 2) as it:
                for h in range(2):
                    pe.wait_ge(sums.hots[h], it + 1 + UP)
                    pe.wait_ge(gathered[h], it * (16 * TPR) + (g0[h] + 16 * TPR))
                    for pair in range(PAIRS):
                        if factors is not None and pair % (PAIRS // 2) == 0:
                            pe.wait_ge(multiplied[h], it * 2 + (1 + 2 * pair // PAIRS) + UP)
                        sums.sum_pair(pe, it, h, pair, lambda t: rows[h][:, t, :])


GROUP = 7
NG = NB // GROUP
assert NG * GROUP == NB


class Signals:

    def __init__(self, sem, names):
        self.sems = {name: sem(name) for name in names.split()}

    def of(self, name):
        return self.sems[name]

    def raise_(self, ins, name, by=1):
        ins.then_inc(self.of(name), by)

    def wait(self, eng, name, it, by=1):
        eng.wait_ge(self.of(name), it * by + by + UP)

    def wait_before(self, eng, name, it, by=1):
        eng.wait_ge(self.of(name), it * by + UP)


def over_blocks(ap, n=GROUP):
    p, f = ap.shape
    return ap.rearrange("p (o f) -> p o f", o=1).to_broadcast([p, n, f])


def per_block(ap, f):
    p, n = ap.shape
    return ap.rearrange("p (n o) -> p n o", o=1).to_broadcast([p, n, f])


def update_nodes(nc, sb, psum, sem, k, *, mode, weights, biases, K, x_in=None, x_out=None, sums=None,
                 row_of=None, extra=None, tables=(), norm=None, cnt=None, own=None, loop=None):
    sig = Signals(sem, "x_loaded extra_loaded x_made x_stored index_made l0 l1 u0 u1 u2 u3 u4 u5 exp_made n0 n1 stats_made "
                  "dev_made scale_made h_made h_turned h_t_made product0_made product1_made bank_read out_made "
                  "own_copied table0_stored table1_stored")
    per_turn = 16 * GROUP * (2 if loop else 1)
    gathered, g0 = k.pool_dma.take(NG * per_turn if sums is not None else 0, 1)
    EF = extra.shape[-1] if extra is not None else D
    F = weights[0].shape[1]
    BANK = 512 // F if F <= 512 else 1
    banks = min(-(-GROUP // BANK), 4)
    rounds = [range(a, min(a + banks * BANK, GROUP)) for a in range(0, GROUP, banks * BANK)]
    x = sb("x", [P, GROUP, D], F32)
    s = sb("s", [P, GROUP, D], F32)
    h = sb("h", [P, GROUP, D], F32)
    t0 = sb("t0", [P, GROUP, D], F32)
    h_t = sb("h_t", [P, GROUP * P], F32)
    out = sb("out", [P, GROUP, F], F32)
    ex = sb("ex", [P, GROUP, D], F32)
    index = sb("index", [P, 2, GROUP], U32)
    loop_alpha = sb("loop_alpha", [P, GROUP, loop[0] if loop else 1], F32)
    stats = sb("stats", [P, GROUP, 6], F32)
    mv = sb("mv", [P, GROUP, 2], F32)
    rstd, dev, shift, count = (sb(n, [P, GROUP], F32) for n in ("rstd", "dev", "shift", "count"))
    eps = sb("eps", [P, 1], F32)
    w = sb("w", [P, F], F32)
    b_in = sb("b_in", [P, D], F32)
    b_out = sb("b_out", [P, F], F32)
    bn = sb("bn", [P, 6, D], F32)
    ps_t = psum("ps_t", [P, 2, 512], F32)
    ps_o = psum("ps_o", [P, banks, 512], F32)
    ready, made = sem("nodes_ready"), sem("nodes_made")
    has_x, has_sums = x_in is not None, sums is not None
    n_loads = 0

    def wide(v, f):
        return v.rearrange("(o f) -> o f", o=1).to_broadcast([P, f])
    with k.block() as block:
        @block.sync
        def _(sp):
            nonlocal n_loads
            loads = [(w[0:K, :], weights[0])]
            if biases[0] is not None:
                f = biases[0].shape[0]
                loads.append((b_in[:, 0:f], wide(biases[0], f)))
            at = 0
            for b, f in biases[1]:
                if b is not None:
                    loads.append((b_out[:, at:at + f], wide(b, f)))
                at += f
            for i, v in enumerate(norm or ()):
                loads.append((bn[:, i, :], wide(v, D)))
            if biases[1]:
                sp.wait_ge(made, 1 + UP)
            for to, of in loads:
                sp.dma_start(to, of).then_inc(ready, 16)
            n_loads = len(loads)
            with sp.Fori(0, NG) as it:
                sig.wait_before(sp, "h_made", it)
                sp.sem_inc(k.held, 1)
                if has_x:
                    if x_out is not None:
                        sig.wait_before(sp, "x_stored", it, 16)
                    sig.raise_(sp.dma_start(x[:, :, :], x_in[it]), "x_loaded", 16)
                if extra is not None:
                    sig.raise_(sp.dma_start(ex[:, :, 0:EF], extra[it]), "extra_loaded", 16)
                if x_out is not None:
                    sig.wait(sp, "x_made", it)
                    sig.raise_(sp.dma_start(x_out[it], x[:, :, :]), "x_stored", 16)
                sig.wait(sp, "out_made", it)
                for i, (table, a, f) in enumerate(tables):
                    ins = sp.dma_start(table[it], out[:, :, a:a + f])
                    sig.raise_(ins, f"table{i}_stored", 16)
            for i in range(len(tables)):
                sig.wait(sp, f"table{i}_stored", NG - 1, 16)
            if x_out is not None:
                sig.wait(sp, "x_stored", NG - 1, 16)

        @block.gpsimd
        def _(pool):
            if has_sums:
                with pool.Fori(0, NG) as it:
                    sig.wait(pool, "index_made", it)
                    sig.wait_before(pool, "h_made", it)
                    pool.sem_inc(k.turns, 1)
                    for j in range(GROUP):
                        pool.indirect_dma_start(
                            out=s[:, j, :], out_offset=None, in_=sums,
                            in_offset=bass.IndirectOffsetOnAxis(ap=index[:, 0, j:j + 1], axis=0)).then_inc(gathered[0], 16)
                        if loop:
                            pool.indirect_dma_start(
                                out=loop_alpha[:, j, :], out_offset=None, in_=loop[1],
                                in_offset=bass.IndirectOffsetOnAxis(ap=index[:, 1, j:j + 1], axis=0)).then_inc(gathered[0], 16)

        @block.vector
        def _(dve):
            nc.vector.memset(eps[:, :], 1e-5)
            if norm:
                nc.vector.memset(bn[:, 4, :], 1e-3)
            nc.vector.memset(b_out[:, :], 0.0).then_inc(made, 1)
            dve.wait_ge(made, 1 + UP)
            dve.wait_ge(ready, n_loads * 16 + UP)
            if norm:
                c = Chain(dve, made, 1)
                c.step(nc.vector.tensor_tensor(bn[:, 4, :], bn[:, 4, :], bn[:, 3, :], ALU.add))
                dve.wait_ge(made, 3 + UP)
                c.n += 1
                c.step(nc.vector.reciprocal(bn[:, 5, :], bn[:, 5, :]))
                c.step(nc.vector.tensor_tensor(bn[:, 4, :], bn[:, 5, :], bn[:, 0, :], ALU.mult))
                c.step(nc.vector.tensor_tensor(bn[:, 5, :], bn[:, 4, :], bn[:, 2, :], ALU.mult))
                c.step(nc.vector.tensor_tensor(bn[:, 5, :], bn[:, 1, :], bn[:, 5, :], ALU.subtract))
            with dve.Fori(0, NG) as it:
                if has_sums:
                    dve.wait_ge(gathered[0], it * per_turn + g0[0])
                    if loop:
                        nc.vector.tensor_copy(index[:, 1, :], loop[2][:, bass.ds(it * GROUP, GROUP)])
                    sig.raise_(nc.vector.tensor_copy(index[:, 0, :], row_of[:, bass.ds(it * GROUP, GROUP)]), "index_made")
                    dve.wait_ge(gathered[0], it * per_turn + (g0[0] + per_turn))
                if has_x:
                    sig.wait(dve, "x_loaded", it, 16)
                if loop:
                    sig.wait(dve, "extra_loaded", it, 16)
                    by_head = ex[:, :, 0:EF].rearrange("p n (h c) -> p n h c", h=loop[0])
                    sig.raise_(nc.vector.tensor_tensor(by_head, by_head, loop_alpha[:, :, :].rearrange(
                        "p n (h o) -> p n h o", o=1).to_broadcast([P, GROUP, loop[0], EF // loop[0]]), ALU.mult), "l0")
                    sig.wait(dve, "l0", it)
                    sig.raise_(nc.vector.tensor_tensor(s[:, :, 0:EF], s[:, :, 0:EF], ex[:, :, 0:EF], ALU.add), "l1")
                    sig.wait(dve, "l1", it)
                if mode == "residual":
                    sig.raise_(nc.vector.tensor_tensor(s[:, :, :], s[:, :, :], over_blocks(b_in[:, :]), ALU.add), "u0")
                    sig.wait(dve, "u0", it)
                    sig.raise_(nc.vector.tensor_tensor(x[:, :, :], x[:, :, :], s[:, :, :], ALU.add), "x_made")
                    sig.wait(dve, "x_made", it)
                if mode == "norm":
                    sig.wait(dve, "extra_loaded", it, 16)
                    sig.raise_(nc.vector.tensor_scalar(count[:, :], cnt[:, bass.ds(it * GROUP, GROUP)], 1.0, None, ALU.max), "u0")
                    sig.wait(dve, "u0", it)
                    sig.raise_(nc.vector.reciprocal(count[:, :], count[:, :]), "u1")
                    sig.wait(dve, "u1", it)
                    sig.raise_(nc.vector.tensor_tensor(s[:, :, :], s[:, :, :], per_block(count[:, :], D), ALU.mult), "u2")
                    sig.wait(dve, "u2", it)
                    sig.raise_(nc.vector.tensor_tensor(s[:, :, :], s[:, :, :], ex[:, :, :], ALU.add), "u3")
                    sig.wait(dve, "u3", it)
                    sig.raise_(nc.vector.tensor_tensor(s[:, :, :], s[:, :, :], over_blocks(bn[:, 4, :]), ALU.mult), "u4")
                    sig.wait(dve, "u4", it)
                    sig.raise_(nc.vector.tensor_tensor(s[:, :, :], s[:, :, :], over_blocks(bn[:, 5, :]), ALU.add), "u5")
                    sig.wait(dve, "u5", it)
                    sig.raise_(nc.vector.scalar_tensor_tensor(x[:, :, :], s[:, :, :], 0.0, x[:, :, :], ALU.max, ALU.add), "x_made")
                    sig.wait(dve, "x_made", it)
                if mode == "elu":
                    sig.wait_before(dve, "h_turned", it)
                    sig.raise_(nc.vector.tensor_tensor(s[:, :, 0:K], s[:, :, 0:K], over_blocks(b_in[:, 0:K]), ALU.add), "u0")
                    sig.wait(dve, "u0", it)
                    sig.raise_(nc.vector.tensor_scalar(t0[:, :, 0:K], s[:, :, 0:K], 0.0, None, ALU.min), "u1")
                    sig.wait(dve, "exp_made", it)
                    sig.raise_(nc.vector.tensor_scalar(s[:, :, 0:K], s[:, :, 0:K], 0.0, None, ALU.max), "u2")
                    sig.wait(dve, "u2", it)
                    sig.raise_(nc.vector.scalar_tensor_tensor(h[:, :, 0:K], t0[:, :, 0:K], -1.0, s[:, :, 0:K], ALU.add, ALU.add), "h_made")
                    sig.wait(dve, "h_made", it)
                else:
                    sig.wait_before(dve, "h_made", it)
                    for j in range(GROUP):
                        last = nc.vector.bn_stats(stats[:, j, :], x[:, j, :])
                    sig.raise_(last, "n0")
                    sig.wait(dve, "n0", it)
                    dve.sem_inc(k.held, 1)
                    for j in range(GROUP):
                        last = nc.vector.bn_aggr(mv[:, j, :], stats[:, j, :])
                    sig.raise_(last, "stats_made")
                    sig.wait(dve, "dev_made", it)
                    sig.raise_(nc.vector.reciprocal(rstd[:, :], dev[:, :]), "n1")
                    sig.wait(dve, "n1", it)
                    sig.raise_(nc.vector.scalar_tensor_tensor(shift[:, :], mv[:, :, 0], -1.0, rstd[:, :], ALU.mult, ALU.mult), "scale_made")
                for i in range(len(tables)):
                    sig.wait_before(dve, f"table{i}_stored", it, 16)
                for r, blocks in enumerate(rounds):
                    sig.wait(dve, f"product{r}_made", it)
                    for b, a in enumerate(range(blocks[0], blocks[-1] + 1, BANK)):
                        n = min(BANK, blocks[-1] + 1 - a)
                        last = nc.vector.tensor_tensor(out[:, a:a + n, :], ps_o[:, b, 0:n * F].rearrange("p (n f) -> p n f", n=n),
                                                       over_blocks(b_out[:, :], n), ALU.add)
                    sig.raise_(last, "out_made" if r == len(rounds) - 1 else "bank_read")
                if own is not None:
                    sig.wait(dve, "out_made", it)
                    sig.raise_(nc.vector.tensor_copy(own[:, bass.ds(it * GROUP, GROUP), :],
                                                     out[:, :, F - own.shape[2]:F]), "own_copied")
                    sig.wait(dve, "own_copied", it)

        @block.scalar
        def _(act):
            if norm:
                act.wait_ge(made, 2 + UP)
                nc.scalar.activation(bn[:, 5, :], bn[:, 4, :], ACT.Sqrt).then_inc(made, 1)
            else:
                act.wait_ge(made, 1 + UP)
            with act.Fori(0, NG) as it:
                if mode == "elu":
                    sig.wait(act, "u1", it)
                    sig.raise_(nc.scalar.activation(t0[:, :, 0:K], t0[:, :, 0:K], ACT.Exp), "exp_made")
                else:
                    sig.wait(act, "stats_made", it)
                    sig.raise_(nc.scalar.activation(dev[:, :], mv[:, :, 1], ACT.Sqrt, bias=eps[:, :]), "dev_made")
                    sig.wait(act, "scale_made", it)
                    sig.wait_before(act, "h_turned", it)
                    for j in range(GROUP):
                        last = nc.scalar.activation(h[:, j, :], x[:, j, :], ACT.Relu, scale=rstd[:, j:j + 1], bias=shift[:, j:j + 1])
                    sig.raise_(last, "h_made")
                sig.wait(act, "h_turned", it)
                sig.wait_before(act, f"product{len(rounds) - 1}_made", it)
                nc.scalar.copy(h_t[0:K, 0:512], ps_t[0:K, 0, :])
                sig.raise_(nc.scalar.copy(h_t[0:K, 512:GROUP * P], ps_t[0:K, 1, 0:GROUP * P - 512]), "h_t_made")

        @block.tensor
        def _(pe):
            pe.wait_ge(ready, n_loads * 16 + UP)
            with pe.Fori(0, NG) as it:
                sig.wait(pe, "h_made", it)
                sig.wait_before(pe, "h_t_made", it)
                for j in range(GROUP):
                    last = nc.tensor.transpose(ps_t[0:K, j // 4, (j % 4) * P:(j % 4 + 1) * P], h[:, j, 0:K], k.ident[:, :])
                sig.raise_(last, "h_turned")
                sig.wait(pe, "h_t_made", it)
                sig.wait_before(pe, "out_made", it)
                for r, blocks in enumerate(rounds):
                    if r:
                        sig.wait(pe, "bank_read", it)
                    for j in blocks:
                        i = j - blocks[0]
                        last = nc.tensor.matmul(ps_o[:, i // BANK, (i % BANK) * F:(i % BANK + 1) * F],
                                                h_t[0:K, j * P:(j + 1) * P], w[0:K, :], start=True, stop=True,
                                                skip_group_check=True)
                    sig.raise_(last, f"product{r}_made")


def fold_attention(nc, sb, psum, sem, k, layer, w, a_src, a_dst, K, folded):
    heads, c = a_src.shape
    F = heads * c
    w_sb, a_sb = sb("w", [P, F + 2 * heads], F32), sb("a", [P, 2 * heads], F32)
    w_t = sb("w_t", [P, P], F32)
    ps = psum("ps", [P, 2, P], F32)
    s = {x: sem(f"fold{layer}_{x}") for x in ("made", "loaded", "turned", "copied", "product", "done", "stored")}
    with k.block() as block:
        @block.sync
        def _(sp):
            sp.dma_start(w_sb[0:K, 0:F], w).then_inc(s["loaded"], 16)
            sp.wait_ge(s["made"], 1 + UP)
            for i, a in enumerate((a_src, a_dst)):
                for h in range(heads):
                    sp.dma_start(a_sb[h * c:(h + 1) * c, i * heads + h:i * heads + h + 1],
                                 a[h:h + 1, :].rearrange("o c -> c o")).then_inc(s["loaded"], 16)
            sp.wait_ge(s["done"], 1 + UP)
            sp.dma_start(folded, w_sb[0:K, :]).then_inc(s["stored"], 16)
            sp.wait_ge(s["stored"], 16 + UP)

        @block.vector
        def _(dve):
            nc.vector.memset(a_sb[:, :], 0.0).then_inc(s["made"], 1)
            dve.wait_ge(s["turned"], 1 + UP)
            nc.vector.tensor_copy(w_t[0:F, 0:K], ps[0:F, 0, 0:K]).then_inc(s["copied"], 1)
            dve.wait_ge(s["product"], 1 + UP)
            nc.vector.tensor_copy(w_sb[0:K, F:F + 2 * heads], ps[0:K, 1, 0:2 * heads]).then_inc(s["done"], 1)

        @block.tensor
        def _(pe):
            pe.wait_ge(s["loaded"], (1 + 2 * heads) * 16 + UP)
            nc.tensor.transpose(ps[0:F, 0, 0:K], w_sb[0:K, 0:F], k.ident[0:K, 0:K]).then_inc(s["turned"], 1)
            pe.wait_ge(s["copied"], 1 + UP)
            nc.tensor.matmul(ps[0:K, 1, 0:2 * heads], w_t[0:F, 0:K], a_sb[0:F, :], start=True, stop=True).then_inc(s["product"], 1)


def finish_nodes(nc, sb, psum, sem, k, *, x_in, own, sums, row_of, has, w1b, w2, b2, x_out):
    sig = Signals(sem, "x_loaded extra_loaded x_stored index_made u0 h_made h_turned h_turned_copied product_made u1 u2 "
                  "r_turned r_turned_copied product2_made u3 out_made")
    gathered, g0 = k.pool_dma.take(NG * 16 * GROUP, 1)
    x, s, r = (sb(n, [P, GROUP, D], F32) for n in ("x", "s", "r"))
    o = sb("own", [P, GROUP, 2 * D], F32)
    flag = sb("flag", [P, GROUP], F32)
    index = sb("index", [P, GROUP], U32)
    turned = sb("turned", [P, GROUP * P], F32)
    w = sb("w", [P, 2, D], F32)
    b = sb("b", [P, D], F32)
    ps_t, ps_o = psum("ps_t", [P, 2, 512], F32), psum("ps_o", [P, 2, 512], F32)
    ready = sem("nodes_ready")
    with k.block() as block:
        @block.sync
        def _(sp):
            sp.dma_start(w[:, 0, :], w1b).then_inc(ready, 16)
            sp.dma_start(w[:, 1, :], w2).then_inc(ready, 16)
            sp.dma_start(b[:, :], b2.rearrange("(o f) -> o f", o=1).to_broadcast([P, D])).then_inc(ready, 16)
            with sp.Fori(0, NG) as it:
                sig.wait_before(sp, "x_stored", it, 16)
                sig.raise_(sp.dma_start(x[:, :, :], x_in[it]), "x_loaded", 16)
                sig.raise_(sp.dma_start(o[:, :, :], own[it]), "extra_loaded", 16)
                sig.wait(sp, "out_made", it)
                sig.raise_(sp.dma_start(x_out[it], x[:, :, :]), "x_stored", 16)
            sig.wait(sp, "x_stored", NG - 1, 16)

        @block.gpsimd
        def _(pool):
            with pool.Fori(0, NG) as it:
                sig.wait(pool, "index_made", it)
                pool.sem_inc(k.turns, 1)
                for j in range(GROUP):
                    pool.indirect_dma_start(
                        out=s[:, j, :], out_offset=None, in_=sums,
                        in_offset=bass.IndirectOffsetOnAxis(ap=index[:, j:j + 1], axis=0)).then_inc(gathered[0], 16)

        @block.vector
        def _(dve):
            dve.wait_ge(ready, 48 + UP)
            with dve.Fori(0, NG) as it:
                sig.wait_before(dve, "out_made", it)
                nc.vector.tensor_copy(flag[:, :], has[:, bass.ds(it * GROUP, GROUP)])
                sig.raise_(nc.vector.tensor_copy(index[:, :], row_of[:, bass.ds(it * GROUP, GROUP)]), "index_made")
                sig.wait(dve, "index_made", it)
                dve.wait_ge(gathered[0], it * (16 * GROUP) + (g0[0] + 16 * GROUP))
                sig.wait(dve, "extra_loaded", it, 16)
                sig.raise_(nc.vector.tensor_tensor(s[:, :, :], s[:, :, :], o[:, :, 0:D], ALU.add), "u0")
                sig.wait(dve, "u0", it)
                sig.raise_(nc.vector.tensor_tensor(s[:, :, :], s[:, :, :], per_block(flag[:, :], D), ALU.mult), "h_made")
                sig.wait(dve, "product_made", it)
                for i, (a, n) in enumerate(((0, 4), (4, GROUP - 4))):
                    last = nc.vector.tensor_tensor(r[:, a:a + n, :], ps_o[:, i, 0:n * D].rearrange("p (n f) -> p n f", n=n),
                                                   o[:, a:a + n, D:2 * D], ALU.add)
                sig.raise_(last, "u1")
                sig.wait(dve, "u1", it)
                sig.raise_(nc.vector.tensor_scalar(r[:, :, :], r[:, :, :], 0.0, None, ALU.max), "u2")
                sig.wait(dve, "x_loaded", it, 16)
                sig.raise_(nc.vector.tensor_tensor(x[:, :, :], x[:, :, :], over_blocks(b[:, :]), ALU.add), "u3")
                sig.wait(dve, "u3", it)
                sig.wait(dve, "product2_made", it)
                for i, (a, n) in enumerate(((0, 4), (4, GROUP - 4))):
                    last = nc.vector.tensor_tensor(x[:, a:a + n, :], ps_o[:, i, 0:n * D].rearrange("p (n f) -> p n f", n=n),
                                                   x[:, a:a + n, :], ALU.add)
                sig.raise_(last, "out_made")

        @block.scalar
        def _(act):
            with act.Fori(0, NG) as it:
                for x in ("h_turned", "r_turned"):
                    sig.wait(act, x, it)
                    nc.scalar.copy(turned[:, 0:512], ps_t[:, 0, :])
                    sig.raise_(nc.scalar.copy(turned[:, 512:GROUP * P], ps_t[:, 1, 0:GROUP * P - 512]), x + "_copied")

        @block.tensor
        def _(pe):
            pe.wait_ge(ready, 48 + UP)
            with pe.Fori(0, NG) as it:
                sig.wait_before(pe, "out_made", it)
                for i, (src, made, name_t, product) in enumerate(((s, "h_made", "h_turned", "product_made"),
                                                                  (r, "u2", "r_turned", "product2_made"))):
                    sig.wait(pe, made, it)
                    for j in range(GROUP):
                        last = nc.tensor.transpose(ps_t[:, j // 4, (j % 4) * P:(j % 4 + 1) * P], src[:, j, :], k.ident[:, :])
                    sig.raise_(last, name_t)
                    sig.wait(pe, name_t + "_copied", it)
                    for j in range(GROUP):
                        last = nc.tensor.matmul(ps_o[:, j // 4, (j % 4) * P:(j % 4 + 1) * P], turned[:, j * P:(j + 1) * P],
                                                w[:, i, :], start=True, stop=True, skip_group_check=True)
                    sig.raise_(last, product)
class GatedFilters:

    HALF = TPR // 2
    QUADS = HALF // 4

    def __init__(self, nc, sb, psum, sem, attr, gated, start, w_gate, b_gate, w_filt, b_filt):
        self.nc = nc
        size = ROWS // 2 * COLS
        self.attr_dram, self.gated_dram = (x[start:start + size, :].rearrange("(g p h t) f -> g h p t f", g=ROWS // 2, p=P, h=2)
                                           for x in (attr, gated))
        self.params = (w_gate, b_gate, w_filt, b_filt)
        self.attr = [sb(f"attr{h}", [P, self.HALF, D], F32) for h in range(2)]
        self.out = [sb(f"gated{h}", [P, self.HALF, D], F32) for h in range(2)]
        self.attr_t, self.before_gate, self.gate, self.filt = (
            [sb(f"{x}{i}", [P, 4 * D], F32) for i in range(2)] for x in ("attr_t", "before_gate", "gate", "filt"))
        self.w = sb("w_gated", [P, 2, D], F32)
        self.b = sb("b_gated", [P, 2, D], F32)
        self.ps_t, self.ps_g, self.ps_f = ([psum(f"{x}{i}", [P, 4 * D], F32) for i in range(2)] for x in ("ps_attr", "ps_gate", "ps_filt"))
        self.params_loaded = sem("gated_params_loaded")
        self.loaded, self.stored = ([sem(f"gated_{x}{h}") for h in range(2)] for x in ("loaded", "stored"))
        self.turned, self.copied, self.product, self.biased, self.sigmoid, self.filtered, self.made = (
            [sem(f"gated_{x}{i}") for i in range(2)] for x in ("turned", "copied", "product", "biased", "sigmoid", "filtered", "made"))

    def load_params(self, sp):
        w_gate, b_gate, w_filt, b_filt = self.params
        for i, (w, b) in enumerate(((w_gate, b_gate), (w_filt, b_filt))):
            sp.dma_start(self.w[:, i, :], w).then_inc(self.params_loaded, 16)
            sp.dma_start(self.b[:, i, :], b.rearrange("(o f) -> o f", o=1).to_broadcast([P, D])).then_inc(self.params_loaded, 16)

    def nth(self, it, h):
        return it * 2 + h

    def sp(self, sp, it, h):
        for i in range(2):
            sp.wait_ge(self.turned[i], self.nth(it, 0) + UP)
        sp.dma_start(self.attr[h][:, :, :], self.attr_dram[it, h]).then_inc(self.loaded[h], 16)

    def pe(self, pe, it, h):
        nc, n = self.nc, self.nth(it, h)
        pe.wait_ge(self.loaded[h], it * 16 + 16 + UP)
        for i in range(2):
            pe.wait_ge(self.copied[i], n + UP)
            for j in range(4):
                last = nc.tensor.transpose(self.ps_t[i][:, j * P:(j + 1) * P], self.attr[h][:, 4 * i + j, :], self.ident)
            last.then_inc(self.turned[i], 1)
        for i in range(2):
            pe.wait_ge(self.copied[i], n + 1 + UP)
            pe.wait_ge(self.filtered[i], n + UP)
            for ps, w in ((self.ps_g, 0), (self.ps_f, 1)):
                for j in range(4):
                    last = nc.tensor.matmul(ps[i][:, j * P:(j + 1) * P], self.attr_t[i][:, j * P:(j + 1) * P], self.w[:, w, :],
                                            start=True, stop=True, skip_group_check=True)
            last.then_inc(self.product[i], 1)

    def act(self, act, it, h):
        nc, n = self.nc, self.nth(it, h)
        for i in range(2):
            act.wait_ge(self.turned[i], n + 1 + UP)
            act.wait_ge(self.product[i], n + UP)
            nc.scalar.copy(self.attr_t[i][:, :], self.ps_t[i][:, :]).then_inc(self.copied[i], 1)
        for i in range(2):
            act.wait_ge(self.biased[i], n + 1 + UP)
            act.wait_ge(self.made[i], n + UP)
            nc.scalar.activation(self.gate[i][:, :], self.before_gate[i][:, :], ACT.Sigmoid).then_inc(self.sigmoid[i], 1)

    def dve(self, dve, it, h):
        nc, n = self.nc, self.nth(it, h)

        def tiled(a):
            return a[:, :].rearrange("p (j f) -> p j f", f=D)
        for i in range(2):
            dve.wait_ge(self.product[i], n + 1 + UP)
            dve.wait_ge(self.sigmoid[i], n + UP)
            nc.vector.tensor_tensor(tiled(self.before_gate[i]), tiled(self.ps_g[i]), over_blocks(self.b[:, 0, :], 4),
                                    ALU.add).then_inc(self.biased[i], 1)
            dve.wait_ge(self.made[i], n + UP)
            nc.vector.tensor_tensor(tiled(self.filt[i]), tiled(self.ps_f[i]), over_blocks(self.b[:, 1, :], 4),
                                    ALU.add).then_inc(self.filtered[i], 1)
        dve.wait_ge(self.stored[h], it * 16 + UP)
        for i in range(2):
            dve.wait_ge(self.filtered[i], n + 1 + UP)
            dve.wait_ge(self.sigmoid[i], n + 1 + UP)
            nc.vector.tensor_tensor(self.out[h][:, 4 * i:4 * i + 4, :], tiled(self.filt[i]), tiled(self.gate[i]),
                                    ALU.mult).then_inc(self.made[i], 1)

    def store(self, eng, it, h):
        for i in range(2):
            eng.wait_ge(self.made[i], self.nth(it, h) + 1 + UP)
        eng.dma_start(self.gated_dram[it, h], self.out[h][:, :, :]).then_inc(self.stored[h], 16)

    def finish(self, eng):
        for h in range(2):
            eng.wait_ge(self.stored[h], ROWS // 2 * 16 + UP)


class KeptRows:

    HALF = TPR // 2

    def __init__(self, nc, sb, sem, k, table, index, kept, start):
        self.k, self.table = k, table
        self.index_dram, self.kept_dram, self.start = index, kept, start
        self.index = [sb(f"kept_index{h}", [P, self.HALF], U32) for h in range(2)]
        self.rows = [sb(f"kept_rows{h}", [P, self.HALF, D], F32) for h in range(2)]
        self.loaded, self.stored = ([sem(f"kept_{x}{h}") for h in range(2)] for x in ("loaded", "stored"))
        self.gathered, self.g0 = k.pool_dma.take(ROWS // 2 * 16 * self.HALF)

    def sp(self, sp, it, h):
        sp.wait_ge(self.gathered[h], it * (16 * self.HALF) + self.g0[h])
        sp.sem_inc(self.k.held, 1)
        at = 3 * TPR + h * self.HALF
        sp.dma_start(self.index[h][:, :], self.index_dram[it + self.start, :, at:at + self.HALF].bitcast(U32)).then_inc(self.loaded[h], 16)

    def pool(self, pool, it, h):
        pool.wait_ge(self.loaded[h], it * 16 + 16 + UP)
        pool.wait_ge(self.stored[h], it * 16 + UP)
        pool.sem_inc(self.k.turns, 1)
        for t in range(self.HALF):
            pool.indirect_dma_start(out=self.rows[h][:, t, :], out_offset=None, in_=self.table,
                                    in_offset=bass.IndirectOffsetOnAxis(ap=self.index[h][:, t:t + 1], axis=0)
                                    ).then_inc(self.gathered[h], 16)

    def act(self, act, it, h):
        act.wait_ge(self.gathered[h], it * (16 * self.HALF) + (self.g0[h] + 16 * self.HALF))
        act.dma_start(self.kept_dram[it + self.start, :, h * self.HALF * D:(h + 1) * self.HALF * D], self.rows[h][:, :, :]).then_inc(self.stored[h], 16)

    def finish(self, act):
        for h in range(2):
            act.wait_ge(self.stored[h], ROWS // 2 * 16 + UP)


def gather_rows(nc, sb, psum, sem, k, F, H, edge_meta, table, rows_out, scores_out, filters=None):
    WROW = F + H
    meta = [sb(f"meta{h}", [P, TPR], U32) for h in range(2)]
    rows = [sb(f"rows{h}", [P, TPR, WROW], F32) for h in range(2)]
    score = [sb(f"score{h}", [TPR * H, P], F32) for h in range(2)]
    ps = [psum(f"ps{h}", [TPR * H, P], F32) for h in range(2)]
    gathered, g0 = k.pool_dma.take(ROWS // 2 * 16 * TPR)
    column = [sb(f"column{h}", [P, TPR * H], F32) for h in range(2)]
    extra = GatedFilters(nc, sb, psum, sem, *filters) if filters else None
    if extra:
        extra.ident = k.ident[:, :]
    loaded, picked, turned, copied, stored, kept = ([sem(f"gat_rows_{x}{h}") for h in range(2)] for x in
                                                    ("loaded", "picked", "turned", "copied", "stored", "kept"))
    with k.block() as block:
        @block.sync
        def _(sp):
            if extra:
                extra.load_params(sp)
            with sp.Fori(0, ROWS // 2) as it:
                for h in range(2):
                    if extra:
                        extra.sp(sp, it, h)
                    sp.wait_ge(gathered[h], it * (16 * TPR) + g0[h])
                    sp.dma_start(meta[h][:, :], edge_meta[it * 2 + h, :, 0:TPR].bitcast(U32)).then_inc(loaded[h], 16)

        @block.gpsimd
        def _(pool):
            with pool.Fori(0, ROWS // 2) as it:
                for h in range(2):
                    pool.wait_ge(loaded[h], it * 16 + 16 + UP)
                    pool.wait_ge(stored[h], it * 16 + UP)
                    pool.wait_ge(turned[h], it + UP)
                    pool.sem_inc(k.turns, 1)
                    for t in range(TPR):
                        pool.indirect_dma_start(out=rows[h][:, t, :], out_offset=None, in_=table,
                                                in_offset=bass.IndirectOffsetOnAxis(ap=meta[h][:, t:t + 1], axis=0)
                                                ).then_inc(gathered[h], 16)

        @block.tensor
        def _(pe):
            if extra:
                pe.wait_ge(extra.params_loaded, 64 + UP)
            with pe.Fori(0, ROWS // 2) as it:
                for h in range(2):
                    if extra:
                        extra.pe(pe, it, h)
                    pe.wait_ge(picked[h], it + 1 + UP)
                    pe.wait_ge(copied[h], it + UP)
                    pe.sem_inc(k.held, 1)
                    nc.tensor.transpose(ps[h][:, :], column[h][:, :], k.ident[:, :]).then_inc(turned[h], 1)

        @block.vector
        def _(dve):
            if extra:
                dve.wait_ge(extra.params_loaded, 64 + UP)
            with dve.Fori(0, ROWS // 2) as it:
                for h in range(2):
                    if extra:
                        extra.dve(dve, it, h)
                    dve.wait_ge(turned[h], it + 1 + UP)
                    dve.wait_ge(kept[h], it * 16 + UP)
                    nc.vector.tensor_copy(score[h][:, :], ps[h][:, :]).then_inc(copied[h], 1)

        @block.scalar
        def _(act):
            with act.Fori(0, ROWS // 2) as it:
                for h in range(2):
                    if extra:
                        extra.act(act, it, h)
                        extra.store(act, it, h)
                    act.wait_ge(gathered[h], it * (16 * TPR) + (g0[h] + 16 * TPR))
                    act.dma_start(rows_out[it * 2 + h], rows[h][:, :, :]).then_inc(stored[h], 16)
                    act.wait_ge(turned[h], it + UP)
                    nc.scalar.copy(column[h][:, :].rearrange("p (t h) -> p t h", h=H), rows[h][:, :, F:WROW]).then_inc(picked[h], 1)
                    act.wait_ge(copied[h], it + 1 + UP)
                    act.dma_start(scores_out[it * 2 + h], score[h][:, :]).then_inc(kept[h], 16)
            for h in range(2):
                act.wait_ge(stored[h], ROWS // 2 * 16 + UP)
                act.wait_ge(kept[h], ROWS // 2 * 16 + UP)
            if extra:
                extra.finish(act)


def place_scores(nc, sb, psum, sem, k, own, spot, placed):
    scattered, g0 = k.pool_dma.take(NB * 16, 1)
    with k.block() as block:
        @block.gpsimd
        def _(pool):
            for b in range(NB):
                pool.indirect_dma_start(out=placed, out_offset=bass.IndirectOffsetOnAxis(ap=spot[:, b:b + 1], axis=0),
                                        in_=own[:, b, :], in_offset=None).then_inc(scattered[0], 16)
            pool.wait_ge(scattered[0], g0[0] + NB * 16)


def softmax_by_segment(nc, sb, psum, sem, k, H, flags, scores, placed, alphas, loop_alphas):
    keep = [sb(f"keep{i}", [ROWS, COLS], F32) for i in range(2)]
    drop = [sb(f"drop{i}", [ROWS, COLS], F32) for i in range(2)]
    room = sb("room", [P, COLS * H], F32)
    sc = room[0:ROWS, :].rearrange("g (t h i) -> g t h i", t=TPR, h=H)
    packed = room[:, 0:ROWS * H * TPR].rearrange("p (g c) -> p g c", g=ROWS)
    v = sb("v", [ROWS, COLS, 2 * H], F32)
    alone = sb("alone", [ROWS, COLS, H], F32)
    one, two, p, m = (sb(x, [ROWS, COLS], F32) for x in ("one", "two", "p", "m"))
    totals = sb("totals", [ROWS, 4], F32)
    last, carry = sb("last", [ROWS, 1], F32), sb("carry", [ROWS, 1], F32)
    line = sb("line", [1, ROWS], F32)
    total_line = sb("total_line", [1, 4, ROWS], F32)
    run = sb("run", [1, ROWS + 2], F32)
    ps_line, ps_col = psum("ps_line", [1, ROWS], F32), psum("ps_col", [ROWS, 1], F32)
    ps = [psum(f"ps_turn{i}", [P, 512], F32) for i in range(2)]
    names = ("loaded", "steps", "asked", "answered", "shifted", "exp_made", "alpha_made", "loops_made", "turned", "evacuated", "stored")
    s = {x: sem(f"softmax_{x}") for x in names}
    BACK = (0, 0, 1, 0, 1)
    requests = 4 + 2 * len(BACK) * H
    with k.block() as block:
        @block.sync
        def _(sp):
            sp.dma_start(keep[0][:, :], flags[0]).then_inc(s["loaded"], 16)
            sp.dma_start(keep[1][:, :], flags[1]).then_inc(s["loaded"], 16)
            sp.dma_start(sc[:, :, :, :], scores.rearrange("g (t h) i -> g t h i", h=H)).then_inc(s["loaded"], 16)
            sp.dma_start(v[:, :, :], placed[0:EP, :].rearrange("(g c) h -> g c h", c=COLS)).then_inc(s["loaded"], 16)
            sp.dma_start(loop_alphas[EP:EP + P, :], k.ones[:, 0:H]).then_inc(s["stored"], 16)
            sp.wait_ge(s["loops_made"], H + UP)
            sp.dma_start(loop_alphas[0:EP, :].rearrange("(g c) h -> g c h", c=COLS), alone[:, :, :]).then_inc(s["stored"], 16)
            sp.wait_ge(s["evacuated"], H * TPR // 4 + UP)
            sp.dma_start(alphas.rearrange("g p c -> p g c"), packed[:, :, :]).then_inc(s["stored"], 16)
            sp.wait_ge(s["stored"], 48 + UP)

        @block.vector
        def _(dve):
            c = Chain(dve, s["steps"])
            asked = Chain(dve, s["answered"])
            dve.wait_ge(s["loaded"], 64 + UP)

            def ask(ins):
                ins.then_inc(s["asked"], 1)
                asked.n += 1
                dve.wait_ge(s["answered"], asked.base + asked.n + UP)

            for i in range(2):
                c.step(nc.vector.tensor_scalar(drop[i][:, :], keep[i][:, :], -BIG, None, ALU.mult))
                c.step(nc.vector.tensor_scalar(keep[i][:, :], keep[i][:, :], -1.0, 1.0, ALU.mult, ALU.add))
                for j, x in enumerate((keep[i], drop[i])):
                    n = 2 * i + j
                    ask(nc.vector.tensor_reduce(totals[:, n:n + 1], x[:, :], mybir.AxisListType.X, ALU.min))
                    c.step(nc.vector.tensor_copy(total_line[:, n, :], ps_line[:, :]))

            def running(out, data, back, largest):
                mask = (drop if largest else keep)[back]
                ops = (ALU.add, ALU.max) if largest else (ALU.mult, ALU.add)
                start = -BIG if largest else 0.0
                fl = (lambda a: a[:, ::-1]) if back else (lambda a: a)
                c.step(nc.vector.tensor_tensor_scan(fl(out), fl(mask[:, :]), fl(data), start, *ops))
                edge = 0 if back else COLS - 1
                c.step(nc.vector.memset(run[:, :], start))
                ask(nc.vector.tensor_copy(last[:, :], out[:, edge:edge + 1]))
                c.step(nc.vector.tensor_copy(line[:, :], ps_line[:, :]))
                ask(nc.vector.tensor_tensor_scan(fl(run[:, 1:ROWS + 1]), fl(total_line[:, 2 * back + largest, :]),
                                                 fl(line[:, :]), start, *ops))
                c.step(nc.vector.tensor_copy(carry[:, :], ps_col[:, :]))
                c.step(nc.vector.tensor_tensor_scan(fl(out), fl(mask[:, :]), fl(data), carry[:, 0:1], *ops))

            def tiled(a):
                return a[:, :].rearrange("g (t i) -> g t i", i=P)

            for h in range(H):
                own = alone[:, :, h]
                running(one[:, :], v[:, :, H + h], 0, 0)
                c.step(nc.vector.tensor_tensor(tiled(two), sc[:, :, h, :], tiled(one), ALU.add))
                c.step(nc.vector.scalar_tensor_tensor(p[:, :], two[:, :], 0.2, two[:, :], ALU.mult, ALU.max))
                c.step(nc.vector.tensor_tensor(two[:, :], v[:, :, h], v[:, :, H + h], ALU.add))
                c.step(nc.vector.scalar_tensor_tensor(m[:, :], two[:, :], 0.2, two[:, :], ALU.mult, ALU.max))
                c.step(nc.vector.scalar_tensor_tensor(own, keep[0][:, :], -BIG, m[:, :], ALU.mult, ALU.add))
                c.step(nc.vector.tensor_tensor(v[:, :, h], p[:, :], own, ALU.max))
                running(one[:, :], v[:, :, h], 0, 1)
                running(two[:, :], v[:, :, h], 1, 1)
                c.step(nc.vector.tensor_tensor(m[:, :], one[:, :], two[:, :], ALU.max))
                nc.vector.tensor_tensor(own, own, m[:, :], ALU.subtract)
                nc.vector.tensor_tensor(p[:, :], p[:, :], m[:, :], ALU.subtract).then_inc(s["shifted"], 1)
                dve.wait_ge(s["exp_made"], h + 1 + UP)
                c.step(nc.vector.tensor_tensor(v[:, :, h], p[:, :], own, ALU.add))
                running(one[:, :], v[:, :, h], 0, 0)
                running(two[:, :], v[:, :, h], 1, 0)
                c.step(nc.vector.tensor_tensor(m[:, :], one[:, :], two[:, :], ALU.add))
                c.step(nc.vector.tensor_tensor(m[:, :], m[:, :], v[:, :, h], ALU.subtract))
                c.step(nc.vector.tensor_scalar(m[:, :], m[:, :], 1e-16, None, ALU.add))
                c.step(nc.vector.reciprocal(m[:, :], m[:, :]))
                nc.vector.tensor_tensor(own, own, m[:, :], ALU.mult).then_inc(s["loops_made"], 1)
                nc.vector.tensor_tensor(v[:, :, h], p[:, :], m[:, :], ALU.mult).then_inc(s["alpha_made"], 1)
            c.step(nc.vector.memset(run[:, :], 0.0))
            to_tile_columns(nc, None, dve, "dve", [(v[:, :, h], F32) for h in range(H)], ps, packed, k.ident,
                            s["turned"], s["evacuated"])

        @block.scalar
        def _(act):
            for h in range(H):
                act.wait_ge(s["shifted"], h + 1 + UP)
                nc.scalar.activation(alone[:, :, h], alone[:, :, h], ACT.Exp)
                nc.scalar.activation(p[:, :], p[:, :], ACT.Exp).then_inc(s["exp_made"], 1)

        @block.tensor
        def _(pe):
            n = 0

            def answer(out, lhs_t, rhs):
                nonlocal n
                pe.wait_ge(s["asked"], n + 1 + UP)
                nc.tensor.matmul(out, lhs_t, rhs, start=True, stop=True).then_inc(s["answered"], 1)
                n += 1
            for i in range(4):
                answer(ps_line[:, :], totals[:, i:i + 1], k.ident[0:ROWS, 0:ROWS])
            for h in range(H):
                for back in BACK:
                    answer(ps_line[:, :], last[:, :], k.ident[0:ROWS, 0:ROWS])
                    at = 2 if back else 0
                    answer(ps_col[:, :], run[:, at:at + ROWS], k.ones[0:1, 0:1])
            assert n == requests
            pe.wait_ge(s["alpha_made"], H + UP)
            to_tile_columns(nc, pe, None, "pe", [(v[:, :, h], F32) for h in range(H)], ps, packed, k.ident,
                            s["turned"], s["evacuated"])


def sum_weighted_rows(nc, sb, psum, sem, k, F, H, edge_meta, bases, rows_in, alphas, keeping=None):
    WROW = F + H
    sums = SumPass(nc, sb, psum, sem, k, "gat", bases, F)
    rows = [sb(f"rows{h}", [P, TPR, WROW], F32) for h in range(2)]
    alpha = [sb(f"alpha{h}", [P, H * TPR], F32) for h in range(2)]
    extra = KeptRows(nc, sb, sem, k, *keeping) if keeping else None
    scaled = [sb(f"scaled{h}", [P, TPR, F], F32) for h in range(2)] if H > 1 else None
    rows_loaded, alpha_loaded, rows_scaled = ([sem(f"gat_{x}{h}") for h in range(2)] for x in
                                              ("rows_loaded", "alpha_loaded", "rows_scaled"))
    with k.block() as block:
        @block.sync
        def _(sp):
            sums.load_bases(sp)
            with sp.Fori(0, ROWS // 2) as it:
                for h in range(2):
                    sums.load_meta(sp, it, h, edge_meta)
                    if H > 1:
                        sp.wait_ge(rows_scaled[h], it + UP)
                    else:
                        sums.wait_read(sp, it, h)
                    sp.dma_start(rows[h][:, :, :], rows_in[it * 2 + h]).then_inc(rows_loaded[h], 16)
                    sp.dma_start(alpha[h][:, :], alphas[it * 2 + h]).then_inc(alpha_loaded[h], 16)
                    if extra:
                        extra.sp(sp, it, h)

        @block.vector
        def _(dve):
            sums.start_dve(dve)
            with dve.Fori(0, ROWS // 2) as it:
                for h in range(2):
                    q = it * 2 + h
                    if H == 1:
                        dve.wait_ge(alpha_loaded[h], it * 16 + 16 + UP)
                    sums.make_hots(dve, it, h, alpha[h] if H == 1 else None)
                    at = sums.registers(q)
                    for pair in range(PAIRS):
                        sums.add_pair(dve, it, h, pair, at[pair])

        if extra:
            @block.scalar
            def _(act):
                with act.Fori(0, ROWS // 2) as it:
                    for h in range(2):
                        extra.act(act, it, h)
                extra.finish(act)

        @block.gpsimd
        def _(pool):
            with pool.Fori(0, ROWS // 2) as it:
                for h in range(2):
                    if H > 1:
                        pool.wait_ge(rows_loaded[h], it * 16 + 16 + UP)
                        pool.wait_ge(alpha_loaded[h], it * 16 + 16 + UP)
                        sums.wait_read(pool, it, h)
                        nc.gpsimd.tensor_tensor(
                            scaled[h][:, :, :].rearrange("p t (h c) -> p t h c", h=H),
                            rows[h][:, :, 0:F].rearrange("p t (h c) -> p t h c", h=H),
                            alpha[h][:, :].rearrange("p (h t o) -> p t h o", h=H, o=1).to_broadcast([P, TPR, H, F // H]),
                            ALU.mult).then_inc(rows_scaled[h], 1)
                    if extra:
                        extra.pool(pool, it, h)

        @block.tensor
        def _(pe):
            with pe.Fori(0, ROWS // 2) as it:
                for h in range(2):
                    pe.wait_ge(sums.hots[h], it + 1 + UP)
                    if H > 1:
                        pe.wait_ge(rows_scaled[h], it + 1 + UP)
                        source = lambda t: scaled[h][:, t, :]
                    else:
                        pe.wait_ge(rows_loaded[h], it * 16 + 16 + UP)
                        source = lambda t: rows[h][:, t, 0:F]
                    for pair in range(PAIRS):
                        sums.sum_pair(pe, it, h, pair, source)

def largest_messages(nc, sb, psum, sem, k, edge_meta, bases, flags, table, w_edge):
    sums = SumPass(nc, sb, psum, sem, k, "l3", bases, D, slots=2)
    rows = [sb(f"rows{h}", [P, TPR, D], F32) for h in range(2)]
    first = sb("first", [ROWS, COLS], F32)
    drop = sb("drop", [ROWS, COLS], BF16)
    pick = [sb(f"pick{i}", [ROWS, P], BF16) for i in range(2)]
    wide = sb("wide", [P, D], F32)
    rows_t, best, back = ([sb(f"{x}{i}", [P, 4 * P], F32) for i in range(2)] for x in ("rows_t", "best", "back"))
    ps_d, ps_m, ps_b = ([psum(f"{x}{i}", [P, 4 * P], F32) for i in range(2)] for x in ("ps_d", "ps_m", "ps_b"))
    gathered, g0 = k.pool_dma.take(ROWS // 2 * 16 * TPR)
    mixed, picked = ([sem(f"l3_{x}{h}") for h in range(2)] for x in ("mixed", "picked"))
    turned, copied, spread, best_made, back_turned, back_copied = (
        [sem(f"l3_{x}{i}") for i in range(2)] for x in ("turned", "copied", "spread", "best_made", "back_turned", "back_copied"))
    ready, drop_made = sem("l3_ready"), sem("l3_drop_made")
    CH = TPR // 4

    def nth(q, c):
        return q * (CH // 2) + c // 2
    with k.block() as block:
        @block.sync
        def _(sp):
            sums.load_bases(sp)
            sp.dma_start(first[:, :], flags[0]).then_inc(ready, 16)
            sp.dma_start(wide[:, :], w_edge.to_broadcast([P, D])).then_inc(ready, 16)
            with sp.Fori(0, ROWS // 2) as it:
                for h in range(2):
                    sp.wait_ge(gathered[h], it * (16 * TPR) + g0[h])
                    sp.sem_inc(k.held, 1)
                    sp.wait_ge(mixed[h], it * CH + UP)
                    sp.sem_inc(k.held, 1)
                    sums.load_meta(sp, it, h, edge_meta)

        @block.gpsimd
        def _(pool):
            with pool.Fori(0, ROWS // 2) as it:
                for h in range(2):
                    pool.wait_ge(sums.meta_loaded[h], it * 16 + 16 + UP)
                    sums.wait_read(pool, it, h)
                    pool.sem_inc(k.turns, 1)
                    index = sums.meta[h][:, :].bitcast(U32)
                    for t in range(TPR):
                        pool.indirect_dma_start(out=rows[h][:, t, :], out_offset=None, in_=table,
                                                in_offset=bass.IndirectOffsetOnAxis(ap=index[:, t:t + 1], axis=0)
                                                ).then_inc(gathered[h], 16)

        @block.tensor
        def _(pe):
            pe.wait_ge(drop_made, 2 + UP)
            with pe.Fori(0, ROWS // 2) as it:
                for h in range(2):
                    q = it * 2 + h
                    pe.wait_ge(sums.hots[h], it + 1 + UP)
                    pe.wait_ge(picked[h], it + 1 + UP)
                    for step in range(CH + 2):
                        c = step
                        if c < CH:
                            i = c % 2
                            pe.wait_ge(best_made[i], nth(q, c) + UP)
                            nc.tensor.matmul(ps_d[i][:, :], pick[h][:, :], drop[:, c * 4 * P:(c + 1) * 4 * P],
                                             start=True, stop=True).then_inc(spread[i], 1)
                            pe.wait_ge(mixed[h], it * CH + (c + 1) + UP)
                            pe.wait_ge(copied[i], nth(q, c) + UP)
                            for j in range(4):
                                last = nc.tensor.transpose(ps_m[i][:, j * P:(j + 1) * P], rows[h][:, 4 * c + j, :], k.ident[:, :])
                            last.then_inc(turned[i], 1)
                        c = step - 1
                        if 0 <= c < CH:
                            i = c % 2
                            pe.wait_ge(best_made[i], nth(q, c) + 1 + UP)
                            pe.wait_ge(back_copied[i], nth(q, c) + UP)
                            for j in range(4):
                                last = nc.tensor.transpose(ps_b[i][:, j * P:(j + 1) * P], best[i][:, j * P:(j + 1) * P], k.ident[:, :])
                            last.then_inc(back_turned[i], 1)
                        c = step - 2
                        if c >= 0:
                            i = c % 2
                            pe.wait_ge(back_copied[i], nth(q, c) + 1 + UP)
                            for pair in (2 * c, 2 * c + 1):
                                sums.sum_pair(pe, it, h, pair, lambda t: back[i][:, (t % 4) * P:(t % 4 + 1) * P])

        @block.scalar
        def _(act):
            with act.Fori(0, ROWS // 2) as it:
                for h in range(2):
                    q = it * 2 + h
                    act.wait_ge(spread[1], q * (CH // 2) + UP)
                    nc.scalar.copy(pick[h][:, :], k.ident[0:ROWS, bass.ds(q, 1)].to_broadcast([ROWS, P])).then_inc(picked[h], 1)
                    for step in range(CH + 1):
                        c = step
                        if c < CH:
                            i = c % 2
                            act.wait_ge(turned[i], nth(q, c) + 1 + UP)
                            act.wait_ge(best_made[i], nth(q, c) + UP)
                            nc.scalar.copy(rows_t[i][:, :], ps_m[i][:, :]).then_inc(copied[i], 1)
                        c = step - 1
                        if c >= 0:
                            i = c % 2
                            act.wait_ge(back_turned[i], nth(q, c) + 1 + UP)
                            if c >= 2:
                                act.wait_ge(sums.summed[h], it * PAIRS + 2 * (c - 1) + UP)
                            elif h == 1:
                                act.wait_ge(sums.summed[0], it * PAIRS + (PAIRS - 2 * (1 - c)) + UP)
                            else:
                                act.wait_ge(sums.summed[1], it * PAIRS + UP)
                            nc.scalar.copy(back[i][:, :], ps_b[i][:, :]).then_inc(back_copied[i], 1)

        @block.vector
        def _(dve):
            sums.start_dve(dve)
            dve.wait_ge(ready, 32 + UP)
            nc.vector.memset(best[1][:, :], -BIG).then_inc(drop_made, 1)
            nc.vector.tensor_scalar(drop[:, :], first[:, :], -BIG, None, ALU.mult).then_inc(drop_made, 1)
            dve.wait_ge(drop_made, 2 + UP)
            with dve.Fori(0, ROWS // 2) as it:
                for h in range(2):
                    q = it * 2 + h
                    sums.make_hots(dve, it, h, sums.meta[h][:, 3 * TPR:4 * TPR])
                    at = sums.registers(q)
                    dve.wait_ge(gathered[h], it * (16 * TPR) + (g0[h] + 16 * TPR))
                    for t in range(TPR):
                        ins = nc.vector.scalar_tensor_tensor(rows[h][:, t, :], wide[:, :], sums.meta[h][:, TPR + t:TPR + t + 1],
                                                             rows[h][:, t, :], ALU.mult, ALU.add)
                        if t % 4 == 3:
                            ins.then_inc(mixed[h], 1)
                    for c in range(CH + 1):
                        if c < CH:
                            i = c % 2
                            dve.wait_ge(spread[i], nth(q, c) + 1 + UP)
                            dve.wait_ge(copied[i], nth(q, c) + 1 + UP)
                            dve.wait_ge(back_turned[i], nth(q, c) + UP)
                            dve.wait_ge(best_made[1 - i], nth(q, c) + i + UP)
                            nc.vector.tensor_tensor_scan(best[i][:, :], ps_d[i][:, :], rows_t[i][:, :],
                                                         best[1 - i][:, 4 * P - 1:4 * P], ALU.add, ALU.max).then_inc(best_made[i], 1)
                        if c >= 1:
                            for pair in (2 * c - 2, 2 * c - 1):
                                sums.add_pair(dve, it, h, pair, at[pair])
def copy_padded(nc, sb, psum, sem, k, src, dst, rows, total):
    done, zeroed = sem("copy_done"), sem("copy_zeroed")
    fill = total > rows
    z = sb("zeros", [total - rows, src.shape[1]], F32) if fill else None
    with k.block() as block:
        @block.sync
        def _(sp):
            sp.dma_start(dst[0:rows, :], src[0:rows, :]).then_inc(done, 16)
            if fill:
                sp.wait_ge(zeroed, 1 + UP)
                sp.dma_start(dst[rows:total, :], z[:, :]).then_inc(done, 16)
            sp.wait_ge(done, (32 if fill else 16) + UP)
        if fill:
            @block.vector
            def _(dve):
                nc.vector.memset(z[:, :], 0.0).then_inc(zeroed, 1)


def clear_rows(nc, sb, psum, sem, k, tensors):
    done, zeroed = sem("clear_done"), sem("clear_zeroed")
    width = (EP + P) // P * 2 * HEADS
    z = sb("zeros", [P, width], F32)
    with k.block() as block:
        @block.vector
        def _(dve):
            nc.vector.memset(z[:, :], 0.0).then_inc(zeroed, 1)

        @block.sync
        def _(sp):
            sp.wait_ge(zeroed, 1 + UP)
            for x in tensors:
                h = x.shape[1]
                sp.dma_start(x.rearrange("(p c) h -> p (c h)", p=P), z[:, 0:(EP + P) // P * h]).then_inc(done, 16)
            sp.wait_ge(done, 16 * len(tensors) + UP)


class PoolDmas:

    def __init__(self, make):
        self.make, self.counts, self.sems = make, [1 << 16] * 2, None

    def take(self, each, slots=2):
        if max(self.counts) + each >= 1 << 16:
            self.sems, self.counts = self.make(), [16, 16]
        before = list(self.counts)
        for i in range(slots):
            self.counts[i] += each
        return self.sems, before


class Store:
    pass


def gnn_kernel(nc, x, src, dst, edge_attr_128, edge_weight, L0_gnn_weight, L0_gnn_bias, L1_gnn_W1, L1_gnn_as1, L1_gnn_ad1,
               L1_gnn_b1, L1_gnn_W2, L1_gnn_as2, L1_gnn_ad2, L1_gnn_b2, L1_gnn_W3, L1_gnn_as3, L1_gnn_ad3, L1_gnn_b3,
               L2_gnn_W_node, L2_gnn_b_node, L2_gnn_W_gate, L2_gnn_b_gate, L2_gnn_W_filt, L2_gnn_b_filt, L2_gnn_bn_gamma,
               L2_gnn_bn_beta, L2_gnn_bn_mean, L2_gnn_bn_var, L3_gnn_Wm, L3_gnn_bm, L3_gnn_W1, L3_gnn_b1, L3_gnn_W2,
               L3_gnn_b2, out):
    def dram(name, shape, dt=F32):
        return nc.dram_tensor(name, shape, dt, kind="Internal").ap()

    def by_group(t):
        return t.rearrange("(g b p) f -> g p b f", b=GROUP, p=P)

    xs = [dram(f"x{i}", (NP, D)) for i in range(5)]
    own = dram("own", (NP, 2 * D))
    sort_meta = dram("sort_meta", (ROWS, P, 8 * TPR))
    key_rows = {key: dram(f"key_rows_{key}", (ROWS, 2, COLS), BF16) for key in ("src", "dst")}
    ordered = {key: dram(f"ordered_{key}", (EP, 4)) for key in ("src", "dst")}
    meta = {key: dram(f"meta_{key}", (ROWS, P, 4 * TPR)) for key in ("src", "dst")}
    bases = {key: dram(f"bases_{key}", (1, ROWS * PAIRS), I32) for key in ("src", "dst")}
    flags = {key: dram(f"flags_{key}", (2, ROWS, COLS)) for key in ("src", "dst")}
    table_l0, table_l2, table_l3 = (dram(f"table_{i}", (NP, D)) for i in ("l0", "l2", "l3"))
    gated, gated_kept = dram("gated", (E, D)), dram("gated_kept", (ROWS, P, TPR * D))
    sums = dram("sums", (ORD, D))
    rows_kept = [dram(f"rows_kept{i}", (ROWS, P, TPR * w)) for i, w in ((0, HEADS * HID + HEADS), (1, D + 1))]
    gat = ((L1_gnn_W1, L1_gnn_as1, L1_gnn_ad1, L1_gnn_b1, D), (L1_gnn_W2, L1_gnn_as2, L1_gnn_ad2, L1_gnn_b2, HEADS * HID),
           (L1_gnn_W3, L1_gnn_as3, L1_gnn_ad3, L1_gnn_b3, HEADS * HID))
    heads = [a.shape[0] for _, a, _, _, _ in gat]
    width = [w.shape[1] for w, _, _, _, _ in gat]
    folded = [dram(f"folded{i}", (gat[i][4], width[i] + 2 * heads[i])) for i in range(3)]
    gat_table = [dram(f"gat_table{i}", (NP, width[i] + heads[i])) for i in range(3)]
    placed = [dram(f"placed{i}", (EP + P, 2 * h)) for i, h in ((0, HEADS), (1, 1))]
    loop_alphas = [dram(f"loop_alphas{i}", (EP + P, h)) for i, h in ((0, HEADS), (1, 1))]
    scores = [dram(f"scores{i}", (ROWS, TPR * h, P)) for i, h in ((0, HEADS), (1, 1))]
    alphas = [dram(f"alphas{i}", (ROWS, P, h * TPR)) for i, h in ((0, HEADS), (1, 1))]

    with ExitStack() as ctx:
        phases = [0]
        used = []

        def sem(name):
            used.append(nc.alloc_semaphore(name=f"{name}_{phases[0]}"))
            new.append(used[-1])
            return used[-1]

        def keep(name, shape, dt=F32):
            return ctx.enter_context(nc.sbuf_tensor(name, shape, dt))

        k = Store()
        k.iota, k.spare, k.eid = keep("iota", [P, WIN]), keep("spare", [P, 1]), keep("edge_number", [ROWS, COLS])
        k.number, k.joiner = keep("number", [P, 1]), keep("joiner", [2, 1])
        k.ones, k.ident, k.before, k.after = (keep(n, [P, P]) for n in ("ones", "ident", "before", "after"))
        cnt, start = ({key: keep(f"{n}_{key}", [P, NB]) for key in ("src", "dst")} for n in ("cnt", "start"))
        has_dst = keep("has_dst", [P, NB])
        own_score = [keep(f"own_score{h}", [P, NB, 2 * h]) for h in (HEADS, 1)]
        row_of, spot = ({key: keep(f"{n}_{key}", [P, NB], U32) for key in ("src", "dst")} for n in ("row_of", "spot"))
        new, new_dma = [], []

        def raised_block():
            for s in new:
                nc.gpsimd.sem_inc(s, UP)
            for s in new_dma:
                nc.gpsimd.dma_start(k.primed[:, :], k.number[:, :]).then_inc(s, 16)
                nc.gpsimd.wait_ge(s, 16)
            new.clear()
            new_dma.clear()
            nc.all_engine_barrier()
            return nc.Block()
        k.block = raised_block

        def lasting(name):
            new_dma.append(nc.alloc_semaphore(name=name))
            return new_dma[-1]
        k.primed = keep("primed", [P, 1])
        k.held = nc.alloc_semaphore(name="waits_held")
        k.turns = nc.alloc_semaphore(name="pool_turns")
        k.pool_dma = PoolDmas(lambda: [lasting(f"pool_dma{h}_{phases[0]}") for h in range(2)])

        def run(phase, *args, **kw):
            phases[0] += 1
            tag = f"p{phases[0]}_"
            with ExitStack() as st:
                phase(nc, lambda n, s, d: st.enter_context(nc.sbuf_tensor(tag + n, s, d)),
                      lambda n, s, d: st.enter_context(nc.psum_tensor(tag + n, s, d)), sem, k, *args, **kw)
            nc.clear_and_free_semaphores(used)
            nc.all_engine_barrier()
            used.clear()

        run(make_constants)
        run(copy_padded, x, xs[0], N, NP)
        run(clear_rows, placed)
        run(stage_edges, src, dst, edge_weight, sort_meta, list(key_rows.values()))
        for key in ("src", "dst"):
            run(count_keys, key, sort_meta, cnt[key])
            run(node_offsets, key, cnt[key], start[key], row_of[key], spot[key])
            run(sort_edges, key, sort_meta, key_rows[key], start[key], ordered[key])
            run(lay_out_segments, key, ordered[key], meta[key], bases[key], flags[key])
        for i, (w, a_src, a_dst, _, K) in enumerate(gat):
            run(fold_attention, i, w, a_src, a_dst, K, folded[i])
        epoch = [0]

        def edge_pass(phase, *args):
            with ExitStack() as held:
                k.acc = held.enter_context(nc.sbuf_tensor(f"acc{epoch[0]}", [P, ORD], F32))
                run(phase, *args)
                run(unload_sums, k.acc, sums)
            epoch[0] += 1

        xg = [by_group(t) for t in xs]
        run(update_nodes, mode="first", weights=[L0_gnn_weight], biases=(None, ()), K=D, x_in=xg[0],
            tables=[(by_group(table_l0), 0, D)])
        edge_pass(gather_and_sum, meta["src"], bases["src"], table_l0)
        for i, (_, _, _, b, K) in enumerate(gat):
            F, H = width[i], heads[i]
            j = 0 if i < 2 else 1
            tables = [(by_group(gat_table[i]), 0, F + H)]
            if i == 0:
                run(update_nodes, mode="residual", weights=[folded[0]], biases=(L0_gnn_bias, ()), K=K,
                    x_in=xg[0], x_out=xg[1], sums=sums, row_of=row_of["src"], tables=tables, own=own_score[j])
            else:
                run(update_nodes, mode="elu", weights=[folded[i]], biases=(gat[i - 1][3], ()), K=K,
                    sums=sums, row_of=row_of["dst"], tables=tables, own=own_score[j],
                    extra=by_group(gat_table[i - 1][:, 0:width[i - 1]]), loop=(heads[i - 1], loop_alphas[0], spot["dst"]))
            run(place_scores, own_score[j], spot["dst"], placed[j])
            filters = (edge_attr_128, gated, (0, E - ROWS // 2 * COLS)[i], L2_gnn_W_gate, L2_gnn_b_gate, L2_gnn_W_filt,
                       L2_gnn_b_filt) if i < 2 else None
            keeping = (gated, meta["src"], gated_kept, (i - 1) * ROWS // 2) if i else None
            run(gather_rows, F, H, meta["dst"], gat_table[i], rows_kept[j], scores[j], filters)
            run(softmax_by_segment, H, flags["dst"], scores[j], placed[j], alphas[j], loop_alphas[j])
            edge_pass(sum_weighted_rows, F, H, meta["dst"], bases["dst"], rows_kept[j], alphas[j], keeping)
        run(update_nodes, mode="residual", weights=[L2_gnn_W_node], biases=(gat[2][3], ((L2_gnn_b_node, D),)), K=D,
            x_in=xg[1], x_out=xg[2], sums=sums, row_of=row_of["dst"], tables=[(by_group(table_l2), 0, D)],
            extra=by_group(gat_table[2][:, 0:D]), loop=(1, loop_alphas[1], spot["dst"]))
        edge_pass(gather_and_sum, meta["src"], bases["src"], table_l2, gated_kept)
        w3 = dram("w3", (D, 3 * D))
        run(join_weights, w3, (L3_gnn_Wm[D:2 * D, :], L3_gnn_Wm[0:D, :], L3_gnn_W1[0:D, :]))
        run(update_nodes, mode="norm", weights=[w3], biases=(None, ((None, D), (L3_gnn_bm, D), (L3_gnn_b1, D))),
            K=D, x_in=xg[2], x_out=xg[3], sums=sums, row_of=row_of["src"], extra=by_group(table_l2),
            tables=[(by_group(table_l3), 0, D), (by_group(own), D, 2 * D)],
            norm=(L2_gnn_bn_gamma, L2_gnn_bn_beta, L2_gnn_bn_mean, L2_gnn_bn_var), cnt=cnt["src"])
        edge_pass(largest_messages, meta["dst"], bases["dst"], flags["dst"], table_l3, L3_gnn_Wm[2 * D:2 * D + 1, :])
        run(note_present, cnt["dst"], has_dst)
        run(finish_nodes, x_in=xg[3], own=by_group(own), sums=sums, row_of=row_of["dst"], has=has_dst,
            w1b=L3_gnn_W1[D:2 * D, :], w2=L3_gnn_W2, b2=L3_gnn_b2, x_out=xg[4])
        run(copy_padded, xs[4], out, N, N)


def join_weights(nc, sb, psum, sem, k, joined, parts):
    done = sem("weights_joined")
    with k.block() as block:
        @block.sync
        def _(sp):
            for i, w in enumerate(parts):
                sp.dma_start(joined[:, i * D:(i + 1) * D], w).then_inc(done, 16)
            sp.wait_ge(done, 16 * len(parts) + UP)


def note_present(nc, sb, psum, sem, k, cnt, has):
    made = sem("present_made")
    with k.block() as block:
        @block.vector
        def _(dve):
            nc.vector.tensor_scalar(has[:, :], cnt[:, :], 0.0, None, ALU.is_gt).then_inc(made, 1)
            dve.wait_ge(made, 1 + UP)


_INS = ['x', 'src', 'dst', 'edge_attr_128', 'edge_weight', 'L0_gnn_weight', 'L0_gnn_bias', 'L1_gnn_W1', 'L1_gnn_as1',
        'L1_gnn_ad1', 'L1_gnn_b1', 'L1_gnn_W2', 'L1_gnn_as2', 'L1_gnn_ad2', 'L1_gnn_b2', 'L1_gnn_W3', 'L1_gnn_as3',
        'L1_gnn_ad3', 'L1_gnn_b3', 'L2_gnn_W_node', 'L2_gnn_b_node', 'L2_gnn_W_gate', 'L2_gnn_b_gate', 'L2_gnn_W_filt',
        'L2_gnn_b_filt', 'L2_gnn_bn_gamma', 'L2_gnn_bn_beta', 'L2_gnn_bn_mean', 'L2_gnn_bn_var', 'L3_gnn_Wm',
        'L3_gnn_bm', 'L3_gnn_W1', 'L3_gnn_b1', 'L3_gnn_W2', 'L3_gnn_b2']


def kernel(**inputs):
    import numpy as _np
    import concourse.bacc as _bacc
    from concourse import mybir as _mybir
    from concourse.bass_utils import run_bass_kernel_spmd as _run

    nc = _bacc.Bacc("TRN2", target_bir_lowering=False, num_devices=1)
    arrays, args = {}, []
    for name in _INS:
        a = _np.ascontiguousarray(inputs[name])
        arrays[f"in_{name}"] = a
        args.append(nc.dram_tensor(f"in_{name}", a.shape, _mybir.dt.from_np(a.dtype), kind="ExternalInput").ap())
    args.append(nc.dram_tensor("out_0", (N, D), F32, kind="ExternalOutput").ap())
    gnn_kernel(nc, *args)
    r = _run(nc, [arrays], core_ids=[0])
    return r.results[0]["out_0"]
```

```python
import concourse.bass as bass
from concourse import mybir
from contextlib import ExitStack

F32 = mybir.dt.float32
BF16 = mybir.dt.bfloat16
I32 = mybir.dt.int32
U32 = mybir.dt.uint32
ALU = mybir.AluOpType
ACT = mybir.ActivationFunctionType

P = 128
N = 12500
E = 212500
D = 128
NB = -(-N // P)
NP = NB * P
COLS = 2048
ROWS = -(-E // COLS)
EP = ROWS * COLS
TPR = COLS // P
PAIRS = TPR // 2
WIN = 2 * P
FULL = E // COLS
LAST = E - FULL * COLS
PAD_NODE = NP - 1
ORD = 12800
ZERO_ROW = ORD - 1
HEADS = 3
HID = 32
BIG = 1.0e38
UP = 4
assert ROWS <= P and N < PAD_NODE and N + WIN < ZERO_ROW and ORD % 512 == 0


class Chain:

    def __init__(self, eng, sem, base=0):
        self.eng, self.sem, self.base, self.n = eng, sem, base, 0

    def step(self, ins):
        self.n += 1
        ins.then_inc(self.sem, 1)
        self.eng.wait_ge(self.sem, self.base + self.n + UP)


def make_constants(nc, sb, psum, sem, k):
    made = sem("constants_made")
    with k.block() as block:
        @block.gpsimd
        def _(pool):
            c = Chain(pool, made)
            nc.gpsimd.iota(k.iota[:, :], [[1, WIN]], base=0, channel_multiplier=0,
                           allow_small_or_imprecise_dtypes=True)
            nc.gpsimd.iota(k.spare[:, :], [[1, 1]], base=EP, channel_multiplier=1,
                           allow_small_or_imprecise_dtypes=True)
            nc.gpsimd.iota(k.eid[:, :], [[1, COLS]], base=0, channel_multiplier=COLS,
                           allow_small_or_imprecise_dtypes=True)
            nc.gpsimd.iota(k.number[:, :], [[1, 1]], base=0, channel_multiplier=1,
                           allow_small_or_imprecise_dtypes=True)
            nc.gpsimd.iota(k.joiner[:, :], [[1, 1]], base=1, channel_multiplier=P - 1,
                           allow_small_or_imprecise_dtypes=True)
            c.step(nc.gpsimd.memset(k.ones[:, :], 1.0))
            c.step(nc.gpsimd.memset(k.ident[:, :], 0.0))
            nc.gpsimd.affine_select(out=k.ident[:, :], in_=k.ident[:, :], compare_op=ALU.not_equal, fill=1.0,
                                    base=0, pattern=[[-1, P]], channel_multiplier=1)
            nc.gpsimd.affine_select(out=k.before[:, :], in_=k.ones[:, :], compare_op=ALU.is_gt, fill=0.0,
                                    base=0, pattern=[[1, P]], channel_multiplier=-1)
            c.step(nc.gpsimd.affine_select(out=k.after[:, :], in_=k.ones[:, :], compare_op=ALU.is_gt, fill=0.0,
                                           base=0, pattern=[[-1, P]], channel_multiplier=1))


def to_tile_columns(nc, pe, dve, side, fields, ps, packed, ident, turned, evacuated):
    for f, (src, dtype) in enumerate(fields):
        for b in range(TPR // 4):
            n = f * (TPR // 4) + b
            if side == "pe":
                if n >= 2:
                    pe.wait_ge(evacuated, n - 1 + UP)
                for j in range(4):
                    t = 4 * b + j
                    last = nc.tensor.transpose(ps[n % 2][:, j * ROWS:(j + 1) * ROWS],
                                               src[:, t * P:(t + 1) * P], ident[0:ROWS, 0:ROWS])
                last.then_inc(turned, 1)
            else:
                dve.wait_ge(turned, n + 1 + UP)
                c0 = f * TPR + 4 * b
                out = packed[:, :, c0:c0 + 4]
                if dtype is not F32:
                    out = packed[:, :, :].bitcast(dtype)[:, :, c0:c0 + 4]
                nc.vector.tensor_copy(out.rearrange("p g j -> p j g"),
                                      ps[n % 2][:, 0:4 * ROWS].rearrange("p (j g) -> p j g", j=4)
                                      ).then_inc(evacuated, 1)


def stage_edges(nc, sb, psum, sem, k, src, dst, weight, sort_meta, key_rows):
    loaded, filled, turned, evacuated, stored, cut = (
        sem(f"edges_{x}") for x in ("loaded", "filled", "turned", "evacuated", "stored", "cut"))
    src_i, dst_i = sb("src_i", [ROWS, COLS], I32), sb("dst_i", [ROWS, COLS], I32)
    part = sb("part", [ROWS, COLS], I32)
    src_f, dst_f, w_f = (sb(x, [ROWS, COLS], F32) for x in ("src_f", "dst_f", "w_f"))
    halves = [sb(f"half{i}", [ROWS, COLS], F32) for i in range(4)]
    short = [sb(f"short{i}", [ROWS, COLS], BF16) for i in range(4)]
    packed = sb("packed", [P, ROWS, 8 * TPR], F32)
    ps = [psum(f"ps_turn{i}", [P, 512], F32) for i in range(2)]
    fields = [(x, F32) for x in (*halves, src_f, dst_f, w_f, k.eid)]
    with k.block() as block:
        @block.sync
        def _(sp):
            sp.wait_ge(filled, 1 + UP)
            for to, of in ((src_i, src), (dst_i, dst), (w_f, weight)):
                sp.dma_start(to[0:FULL, :], of[0:FULL * COLS].rearrange("(g c) -> g c", c=COLS)).then_inc(loaded, 16)
                sp.dma_start(to[FULL:ROWS, 0:LAST], of[FULL * COLS:E].rearrange("(g c) -> g c", g=1)).then_inc(loaded, 16)
            sp.wait_ge(cut, 12 + UP)
            for i, rows in enumerate(key_rows):
                for j in range(2):
                    sp.dma_start(rows[:, j, :], short[2 * i + j][:, :]).then_inc(stored, 16)
            sp.wait_ge(evacuated, 8 * TPR // 4 + UP)
            sp.dma_start(sort_meta.rearrange("g p c -> p g c"), packed[:, :, :]).then_inc(stored, 16)
            sp.wait_ge(stored, 5 * 16 + UP)

        @block.vector
        def _(dve):
            nc.vector.memset(src_i[:, :], PAD_NODE)
            nc.vector.memset(dst_i[:, :], PAD_NODE)
            nc.vector.memset(w_f[:, :], 0.0).then_inc(filled, 1)
            dve.wait_ge(loaded, 6 * 16 + UP)
            c = Chain(dve, cut)
            nc.vector.tensor_copy(src_f[:, :], src_i[:, :])
            nc.vector.tensor_copy(dst_f[:, :], dst_i[:, :])
            for i, key in enumerate((src_i, dst_i)):
                for j, (op, by) in enumerate(((ALU.bitwise_and, P - 1), (ALU.logical_shift_right, 7))):
                    c.step(nc.vector.tensor_scalar(part[:, :], key[:, :], by, None, op))
                    c.step(nc.vector.tensor_copy(halves[2 * i + j][:, :], part[:, :]))
            for i in range(4):
                c.step(nc.vector.tensor_copy(short[i][:, :], halves[i][:, :]))
            to_tile_columns(nc, None, dve, "dve", fields, ps, packed, k.ident, turned, evacuated)

        @block.tensor
        def _(pe):
            pe.wait_ge(cut, 8 + UP)
            to_tile_columns(nc, pe, None, "pe", fields, ps, packed, k.ident, turned, evacuated)


def count_keys(nc, sb, psum, sem, k, key, sort_meta, cnt):
    meta = [sb(f"meta{h}", [P, 2 * TPR], F32) for h in range(2)]
    hot = [sb(f"hot{h}", [P, TPR, 2, P], BF16) for h in range(2)]
    total = psum("ps_count", [P, NB], F32)
    iota = sb("iota16", [P, P], BF16)
    loaded = [sem(f"count_{key}_loaded{h}") for h in range(2)]
    hots = [sem(f"count_{key}_hots{h}") for h in range(2)]
    used = [sem(f"count_{key}_used{h}") for h in range(2)]
    ready, copied = sem(f"count_{key}_iota"), sem(f"count_{key}_copied")
    c0 = 0 if key == "src" else 2 * TPR
    with k.block() as block:
        @block.sync
        def _(sp):
            with sp.Fori(0, ROWS // 2) as it:
                for h in range(2):
                    sp.wait_ge(hots[h], it + UP)
                    sp.dma_start(meta[h][:, :], sort_meta[it * 2 + h, :, c0:c0 + 2 * TPR]).then_inc(loaded[h], 16)

        @block.vector
        def _(dve):
            nc.vector.tensor_copy(iota[:, :], k.iota[:, 0:P]).then_inc(ready, 1)
            dve.wait_ge(ready, 1 + UP)
            with dve.Fori(0, ROWS // 2) as it:
                for h in range(2):
                    dve.wait_ge(loaded[h], it * 16 + 16 + UP)
                    dve.wait_ge(used[h], it + UP)
                    for t in range(TPR):
                        for half, n in ((0, P), (1, NB)):
                            last = nc.vector.tensor_scalar(hot[h][:, t, half, 0:n], iota[:, 0:n],
                                                           meta[h][:, half * TPR + t:half * TPR + t + 1], None, ALU.is_equal)
                    last.then_inc(hots[h], 1)
            for h in range(2):
                dve.wait_ge(used[h], ROWS // 2 + UP)
            nc.vector.tensor_copy(cnt[:, :], total[:, :]).then_inc(copied, 1)

        @block.tensor
        def _(pe):
            def group(h, n, first):
                pe.wait_ge(hots[h], n + UP)
                for t in range(TPR):
                    last = nc.tensor.matmul(total[:, :], hot[h][:, t, 0, :], hot[h][:, t, 1, 0:NB],
                                            start=first and t == 0, stop=True, skip_group_check=True)
                last.then_inc(used[h], 1)
            group(0, 1, True)
            group(1, 1, False)
            with pe.Fori(1, ROWS // 2) as it:
                for h in range(2):
                    group(h, it + 1, False)


def node_offsets(nc, sb, psum, sem, k, key, cnt, start, row_of, spot):
    has, col, run, tmp = (sb(x, [P, NB], F32) for x in ("has", "col", "run", "tmp"))
    ordf = sb("ordf", [P, NB], F32)
    ps = psum("ps_sums", [P, 2, 2, P], F32)
    d, summed = sem(f"offsets_{key}_steps"), sem(f"offsets_{key}_summed")
    with k.block() as block:
        @block.tensor
        def _(pe):
            pe.wait_ge(d, 1 + UP)
            for i, x in enumerate((cnt, has)):
                nc.tensor.matmul(ps[:, i, 0, 0:NB], k.ones[:, 0:P], x[:, :], start=True, stop=True)
                last = nc.tensor.matmul(ps[:, i, 1, 0:NB], k.before[:, :], x[:, :], start=True, stop=True)
            last.then_inc(summed, 1)

        @block.vector
        def _(dve):
            c = Chain(dve, d)
            c.step(nc.vector.tensor_scalar(has[:, :], cnt[:, :], 0.0, None, ALU.is_gt))
            dve.wait_ge(summed, 1 + UP)
            for i, out in enumerate((start, ordf)):
                c.step(nc.vector.tensor_copy(col[:, :], ps[:, i, 0, 0:NB]))
                c.step(nc.vector.tensor_tensor_scan(run[:, :], k.ones[:, 0:NB], col[:, :], 0.0, ALU.mult, ALU.add))
                c.step(nc.vector.tensor_tensor(tmp[:, :], run[:, :], col[:, :], ALU.subtract))
                c.step(nc.vector.tensor_tensor(out[:, :], tmp[:, :], ps[:, i, 1, 0:NB], ALU.add))
            c.step(nc.vector.scalar_tensor_tensor(tmp[:, :], ordf[:, :], -float(ZERO_ROW), has[:, :], ALU.add, ALU.mult))
            c.step(nc.vector.tensor_scalar(row_of[:, :], tmp[:, :], float(ZERO_ROW), None, ALU.add))
            c.step(nc.vector.scalar_tensor_tensor(tmp[:, :], start[:, :], k.spare[:, :], has[:, :], ALU.subtract, ALU.mult))
            c.step(nc.vector.tensor_scalar(spot[:, :], tmp[:, :], k.spare[:, :], None, ALU.add))


def sort_edges(nc, sb, psum, sem, k, key, sort_meta, key_rows, start, ordered):
    QUAD = 4
    CH = TPR // QUAD
    c0 = 0 if key == "src" else 2 * TPR
    field = 0 if key == "src" else 1
    meta = [sb(f"meta{h}", [P, 2 * TPR], F32) for h in range(2)]
    values = [sb(f"values{h}", [P, 4 * TPR], F32) for h in range(2)]
    key_row = [sb(f"key_row{h}", [2, COLS], BF16) for h in range(2)]
    moved = [sb(f"moved{h}", [P, TPR, 4], F32) for h in range(2)]
    hot = [sb(f"hot{i}", [P, QUAD, 2, P], BF16) for i in range(2)]
    low_t = [sb(f"low_t{i}", [P, QUAD * P], F32) for i in range(2)]
    table = [sb(f"table{i}", [P, NB], F32) for i in range(2)]
    equal = [sb(f"equal{i}", [P, QUAD, 2 * P], BF16) for i in range(2)]
    picked = [sb(f"picked{i}", [P, 2, NB], F32) for i in range(2)]
    parts = [sb(f"parts{h}", [P, 2, TPR], F32) for h in range(2)]
    place = [sb(f"place{h}", [P, TPR], U32) for h in range(2)]
    iota = sb("iota16", [P, P], BF16)
    join, low = sb("join", [2, P], BF16), sb("low", [2, P], BF16)
    wide_after = sb("wide_after", [P, 2 * P], F32)
    ps_key = [psum(f"ps_key{i}", [P, QUAD * P], F32) for i in range(2)]
    ps_low = [psum(f"ps_low{i}", [P, QUAD * P], F32) for i in range(2)]
    ps_read = [psum(f"ps_read{i}", [P, 2, NB], F32) for i in range(2)]
    ps_count = psum("ps_count", [P, NB], F32)
    s = {x: sem(f"sort_{key}_{x}") for x in ("ready", "seeded", "spread", "lows", "hots", "compared", "table_read",
                                            "table_grown", "table_copied", "answered")}
    scattered, g0 = k.pool_dma.take(ROWS // 2 * 16 * TPR)
    loaded, placed = ([sem(f"sort_{key}_{x}{h}") for h in range(2)] for x in ("loaded", "placed"))
    with k.block() as block:
        @block.sync
        def _(sp):
            with sp.Fori(0, ROWS // 2) as it:
                for h in range(2):
                    sp.wait_ge(placed[h], it + UP)
                    sp.dma_start(key_row[h][:, :], key_rows[it * 2 + h]).then_inc(loaded[h], 16)
                    sp.dma_start(meta[h][:, :], sort_meta[it * 2 + h, :, c0:c0 + 2 * TPR]).then_inc(loaded[h], 16)
                    sp.dma_start(values[h][:, :], sort_meta[it * 2 + h, :, 4 * TPR:8 * TPR]).then_inc(loaded[h], 16)

        @block.vector
        def _(dve):
            nc.vector.tensor_copy(wide_after[:, 0:P], k.ones[:, :])
            nc.vector.tensor_copy(wide_after[:, P:2 * P], k.after[:, :])
            nc.vector.tensor_copy(iota[:, :], k.iota[:, 0:P])
            nc.vector.tensor_scalar(join[:, :], k.ones[0:2, :], k.joiner[:, :], None, ALU.mult)
            nc.vector.tensor_scalar(low[:, :], k.ones[0:2, :], k.ident[0:2, 0:1], None, ALU.mult).then_inc(s["ready"], 1)
            dve.wait_ge(s["ready"], 1 + UP)
            with dve.Fori(0, ROWS // 2) as it:
                for h in range(2):
                    q = it * 2 + h
                    dve.wait_ge(loaded[h], it * 48 + 48 + UP)
                    dve.wait_ge(scattered[h], it * (16 * TPR) + g0[h])

                    def compare(c):
                        i, n = c % 2, q * CH + c
                        dve.wait_ge(s["answered"], (q * (2 * CH) + 2 * (c - 1) if c else q * (2 * CH)) + UP)
                        for t in range(QUAD * c, QUAD * c + QUAD):
                            for half, n_hot in ((0, P), (1, NB)):
                                last = nc.vector.tensor_scalar(hot[i][:, t % QUAD, half, 0:n_hot], iota[:, 0:n_hot],
                                                               meta[h][:, half * TPR + t:half * TPR + t + 1], None,
                                                               ALU.is_equal)
                        last.then_inc(s["hots"], 1)
                        dve.wait_ge(s["spread"], n + 1 + UP)
                        nc.vector.tensor_scalar(low_t[i][:, :], ps_low[i][:, :], k.number[:, :], None,
                                                ALU.is_equal).then_inc(s["lows"], 1)
                        for t in range(QUAD * c, QUAD * c + QUAD):
                            first, n_keys = (t % QUAD) // 2 * 2 * P, (t % 2 + 1) * P
                            last = nc.vector.scalar_tensor_tensor(
                                equal[i][:, t % QUAD, 0:n_keys], ps_key[i][:, first:first + n_keys],
                                values[h][:, field * TPR + t:field * TPR + t + 1], wide_after[:, 2 * P - n_keys:2 * P],
                                ALU.is_equal, ALU.mult, accum_out=parts[h][:, 0, t:t + 1])
                        last.then_inc(s["compared"], 1)

                    def read_answers(pair):
                        i = pair % 2
                        dve.wait_ge(s["table_read"], q * (2 * CH) + pair + 1 + UP)
                        dve.wait_ge(s["answered"], (q * (2 * CH) + (pair - 1) if pair else q * (2 * CH)) + UP)
                        for j in range(2):
                            t = 2 * pair + j
                            last = nc.vector.scalar_tensor_tensor(picked[i][:, j, :], ps_read[i][:, j, :], 1.0,
                                                                  hot[t // QUAD % 2][:, t % QUAD, 1, 0:NB], ALU.mult, ALU.mult,
                                                                  accum_out=parts[h][:, 1, t:t + 1])
                        last.then_inc(s["answered"], 1)
                    for c in range(CH + 1):
                        if c < CH:
                            compare(c)
                        if c:
                            read_answers(2 * c - 2)
                            read_answers(2 * c - 1)
                    dve.wait_ge(s["answered"], q * (2 * CH) + 2 * CH + UP)
                    dve.wait_ge(s["compared"], q * CH + CH + UP)
                    nc.vector.tensor_copy(moved[h][:, :, :].rearrange("p t c -> p c t"),
                                          values[h][:, :].rearrange("p (c t) -> p c t", c=4))
                    nc.vector.tensor_tensor(place[h][:, :], parts[h][:, 0, :], parts[h][:, 1, :],
                                            ALU.add).then_inc(placed[h], 1)

        @block.tensor
        def _(pe):
            pe.wait_ge(s["ready"], 1 + UP)
            nc.tensor.matmul(ps_count[:, :], k.ident[:, :], start[:, :], start=True, stop=True,
                             skip_group_check=True).then_inc(s["seeded"], 1)
            with pe.Fori(0, ROWS // 2) as it:
                for h in range(2):
                    q = it * 2 + h
                    pe.wait_ge(loaded[h], it * 48 + 48 + UP)

                    def spread(c):
                        i, n = c % 2, q * CH + c
                        pe.wait_ge(s["compared"], (n - 1 if c else q * CH) + UP)
                        row = key_row[h][:, c * QUAD * P:(c + 1) * QUAD * P]
                        nc.tensor.matmul(ps_low[i][:, :], low[:, :], row, start=True, stop=True)
                        nc.tensor.matmul(ps_key[i][:, :], join[:, :], row, start=True, stop=True).then_inc(s["spread"], 1)

                    spread(0)
                    for c in range(CH):
                        i = c % 2
                        if c + 1 < CH:
                            spread(c + 1)
                        pe.wait_ge(s["lows"], q * CH + (c + 1) + UP)
                        for pair in (2 * c, 2 * c + 1):
                            n = q * (2 * CH) + pair
                            pe.wait_ge(s["table_copied"], n + 1 + UP)
                            for t in (2 * pair, 2 * pair + 1):
                                last = nc.tensor.matmul(ps_count[:, :], hot[i][:, t % QUAD, 0, :],
                                                        hot[i][:, t % QUAD, 1, 0:NB], start=False,
                                                        stop=True, skip_group_check=True)
                            last.then_inc(s["table_grown"], 1)
                            pe.wait_ge(s["answered"], (n - 1 if pair >= 1 else n) + UP)
                            for t in (2 * pair, 2 * pair + 1):
                                last = nc.tensor.matmul(ps_read[pair % 2][:, t % 2, :], low_t[i][:, t % QUAD * P:(t % QUAD + 1) * P],
                                                        table[pair % 2][:, :], start=True, stop=True, skip_group_check=True)
                            last.then_inc(s["table_read"], 1)

        @block.scalar
        def _(act):
            act.wait_ge(s["seeded"], 1 + UP)
            nc.scalar.copy(table[0][:, :], ps_count[:, :]).then_inc(s["table_copied"], 1)
            with act.Fori(0, ROWS // 2) as it:
                for h in range(2):
                    for pair in range(PAIRS):
                        n = (it * 2 + h) * PAIRS + pair
                        act.wait_ge(s["table_grown"], n + 1 + UP)
                        act.wait_ge(s["table_read"], n + UP)
                        nc.scalar.copy(table[(pair + 1) % 2][:, :], ps_count[:, :]).then_inc(s["table_copied"], 1)

        @block.gpsimd
        def _(pool):
            with pool.Fori(0, ROWS // 2) as it:
                for h in range(2):
                    pool.wait_ge(placed[h], it + 1 + UP)
                    pool.sem_inc(k.turns, 1)
                    for t in range(TPR):
                        pool.indirect_dma_start(
                            out=ordered, out_offset=bass.IndirectOffsetOnAxis(ap=place[h][:, t:t + 1], axis=0),
                            in_=moved[h][:, t, :], in_offset=None).then_inc(scattered[h], 16)
            for h in range(2):
                pool.wait_ge(scattered[h], ROWS // 2 * 16 * TPR + g0[h])


def lay_out_segments(nc, sb, psum, sem, k, key, ordered, edge_meta, bases, flags):
    own, other = (0, 1) if key == "src" else (1, 0)
    rows = sb("rows", [ROWS, COLS, 4], F32)
    near = sb("near", [ROWS, 2], F32)
    first, end, ordn, rel = (sb(x, [ROWS, COLS], F32) for x in ("first", "end", "ordn", "rel"))
    cols = [sb(f"cols{i}", [ROWS, COLS], F32) for i in range(3)]
    low = sb("low", [ROWS, 1], F32)
    base_i = sb("base_i", [ROWS, PAIRS], I32)
    packed = sb("packed", [P, ROWS, 4 * TPR], F32)
    ps = [psum(f"ps_turn{i}", [P, 512], F32) for i in range(2)]
    ps_low = psum("ps_low", [P, 1], F32)
    names = ("loaded", "near", "next", "steps", "summed", "turned", "evacuated", "stored")
    s = {x: sem(f"segments_{key}_{x}") for x in names}
    last_field = cols[2] if key == "src" else end
    last_type = U32 if key == "src" else F32
    fields = [(cols[0], U32), (cols[1], F32), (rel, F32), (last_field, last_type)]
    with k.block() as block:
        @block.sync
        def _(sp):
            sp.dma_start(rows[:, :, :], ordered.rearrange("(g c) f -> g c f", c=COLS)).then_inc(s["loaded"], 16)
            sp.wait_ge(s["loaded"], 16 + UP)
            sp.wait_ge(s["steps"], 1 + UP)
            sp.dma_start(near[1:ROWS, 0:1], rows[0:ROWS - 1, COLS - 1, own:own + 1]).then_inc(s["near"], 16)
            sp.wait_ge(s["steps"], 3 + UP)
            sp.dma_start(near[0:ROWS - 1, 1:2], first[1:ROWS, 0:1]).then_inc(s["next"], 16)
            sp.wait_ge(s["evacuated"], 4 * TPR // 4 + UP)
            sp.dma_start(edge_meta.rearrange("g p c -> p g c"), packed[:, :, :]).then_inc(s["stored"], 16)
            sp.dma_start(bases.rearrange("a (g c) -> (a g) c", c=PAIRS), base_i[:, :]).then_inc(s["stored"], 16)
            sp.dma_start(flags[0], first[:, :]).then_inc(s["stored"], 16)
            sp.dma_start(flags[1], end[:, :]).then_inc(s["stored"], 16)
            sp.wait_ge(s["stored"], 64 + UP)

        @block.vector
        def _(dve):
            c = Chain(dve, s["steps"])
            nc.vector.memset(near[:, 0:1], -1.0)
            c.step(nc.vector.memset(near[:, 1:2], 1.0))
            dve.wait_ge(s["loaded"], 16 + UP)
            c.step(nc.vector.tensor_tensor(first[:, 1:COLS], rows[:, 1:COLS, own], rows[:, 0:COLS - 1, own], ALU.not_equal))
            dve.wait_ge(s["near"], 16 + UP)
            c.step(nc.vector.tensor_tensor(first[:, 0:1], rows[:, 0:1, own], near[:, 0:1], ALU.not_equal))
            c.step(nc.vector.tensor_copy(end[:, 0:COLS - 1], first[:, 1:COLS]))
            nc.vector.tensor_copy(cols[0][:, :], rows[:, :, other])
            nc.vector.tensor_copy(cols[1][:, :], rows[:, :, 2])
            if key == "src":
                nc.vector.tensor_scalar(cols[2][:, :], rows[:, :, 3], float(E - 1), None, ALU.min)
            c.step(nc.vector.memset(rel[:, :], 1.0))
            dve.wait_ge(s["next"], 16 + UP)
            c.step(nc.vector.tensor_copy(end[:, COLS - 1:COLS], near[:, 1:2]))
            c.step(nc.vector.tensor_tensor_scan(ordn[:, :], rel[:, :], first[:, :], -1.0, ALU.mult, ALU.add))
            c.step(nc.vector.tensor_scalar(low[:, :], ordn[:, COLS - 1:COLS], 1.0, None, ALU.add))
            dve.wait_ge(s["summed"], 1 + UP)
            c.step(nc.vector.tensor_copy(near[:, 0:1], ps_low[0:ROWS, :]))
            c.step(nc.vector.tensor_scalar(ordn[:, :], ordn[:, :], near[:, 0:1], None, ALU.add))
            by_pair = ordn[:, :].rearrange("p (k c) -> p k c", c=WIN)
            nc.vector.tensor_copy(base_i[:, :], by_pair[:, :, 0])
            c.step(nc.vector.tensor_tensor(rel[:, :].rearrange("p (k c) -> p k c", c=WIN), by_pair,
                                           by_pair[:, :, 0:1].to_broadcast([ROWS, PAIRS, WIN]), ALU.subtract))
            to_tile_columns(nc, None, dve, "dve", fields, ps, packed, k.ident, s["turned"], s["evacuated"])

        @block.tensor
        def _(pe):
            pe.wait_ge(s["steps"], 8 + UP)
            nc.tensor.matmul(ps_low[0:ROWS, :], k.before[0:ROWS, 0:ROWS], low[:, :], start=True, stop=True).then_inc(s["summed"], 1)
            pe.wait_ge(s["steps"], 11 + UP)
            to_tile_columns(nc, pe, None, "pe", fields, ps, packed, k.ident, s["turned"], s["evacuated"])


def unload_sums(nc, sb, psum, sem, k, acc, sums):
    stage = [sb(f"stage{i}", [P, 4 * P], F32) for i in range(2)]
    out = [sb(f"out{i}", [P, 4 * P], F32) for i in range(2)]
    ps = [psum(f"ps_unload{i}", [P, 4 * P], F32) for i in range(2)]
    fetched, turned, copied, stored = ([sem(f"unload_{x}{i}") for i in range(2)] for x in ("fetched", "turned", "copied", "stored"))
    steps = ORD // (4 * P)
    half = -(-steps // 2)
    with k.block() as block:
        @block.scalar
        def _(act):
            with act.Fori(0, half) as it:
                for i in range(2):
                    act.wait_ge(turned[i], it + UP)
                    nc.scalar.copy(stage[i][:, :], acc[:, bass.ds((it + i * (steps - half)) * 4 * P, 4 * P)]).then_inc(fetched[i], 1)

        @block.tensor
        def _(pe):
            with pe.Fori(0, half) as it:
                for i in range(2):
                    pe.wait_ge(fetched[i], it + 1 + UP)
                    pe.wait_ge(copied[i], it + UP)
                    for j in range(4):
                        last = nc.tensor.transpose(ps[i][:, j * P:(j + 1) * P], stage[i][:, j * P:(j + 1) * P], k.ident[:, :])
                    last.then_inc(turned[i], 1)

        @block.vector
        def _(dve):
            with dve.Fori(0, half) as it:
                for i in range(2):
                    dve.wait_ge(turned[i], it + 1 + UP)
                    dve.wait_ge(stored[i], it * 16 + UP)
                    nc.vector.tensor_copy(out[i][:, :], ps[i][:, :]).then_inc(copied[i], 1)

        @block.sync
        def _(sp):
            with sp.Fori(0, half) as it:
                for i in range(2):
                    sp.wait_ge(copied[i], it + 1 + UP)
                    if i == 1:
                        sp.wait_ge(stored[0], it * 16 + 16 + UP)
                    sp.dma_start(sums[bass.ds((it + i * (steps - half)) * 4 * P, 4 * P), :].rearrange("(j p) f -> p j f", p=P),
                                 out[i][:, :].rearrange("p (j f) -> p j f", j=4)).then_inc(stored[i], 16)
            for i in range(2):
                sp.wait_ge(stored[i], half * 16 + UP)


class SumPass:

    def __init__(self, nc, sb, psum, sem, k, name, bases, width, slots=4, weights=lambda sums, h: None, weights_loaded=None):
        self.weights, self.weights_loaded = (lambda h: weights(self, h)), weights_loaded
        self.nc, self.k, self.width, self.slots = nc, k, width, slots
        self.acc = k.acc
        self.bases_dram = bases
        self.base = sb("base", [1, ROWS * PAIRS], I32)
        self.meta = [sb(f"meta{h}", [P, 4 * TPR], F32) for h in range(2)]
        self.hot = [sb(f"hot{h}", [P, TPR, WIN], F32) for h in range(2)]
        self.ps = [psum(f"ps_sum{i}", [P, WIN], F32) for i in range(slots)]
        self.base_loaded, self.cleared = sem(f"{name}_base_loaded"), sem(f"{name}_cleared")
        self.meta_loaded, self.hots, self.summed = ([sem(f"{name}_{x}{h}") for h in range(2)]
                                                    for x in ("meta_loaded", "hots", "summed"))
        self.added = [sem(f"{name}_added{i}") for i in range(slots)]

    def wait_read(self, eng, it, h):
        eng.wait_ge(self.summed[h], it * PAIRS + UP)

    def load_bases(self, sp):
        sp.dma_start(self.base[:, :], self.bases_dram).then_inc(self.base_loaded, 16)

    def load_meta(self, sp, it, h, edge_meta):
        sp.wait_ge(self.hots[h], it + UP)
        sp.dma_start(self.meta[h][:, :], edge_meta[it * 2 + h]).then_inc(self.meta_loaded[h], 16)

    def start_dve(self, dve):
        dve.wait_ge(self.base_loaded, 16 + UP)
        self.nc.vector.memset(self.acc[:, :], 0.0).then_inc(self.cleared, 1)
        dve.wait_ge(self.cleared, 1 + UP)

    def registers(self, q):
        return self.nc.values_load_multi_w_load_instructions(
            self.base[0:1, bass.ds(q * PAIRS, PAIRS)], engines=(self.nc.vector.engine,),
            min_val=0, max_val=N)[1]

    def make_hots(self, dve, it, h, pair):
        weights = self.weights(h)
        if pair == 0:
            dve.wait_ge(self.meta_loaded[h], it * 16 + 16 + UP)
            if self.weights_loaded:
                dve.wait_ge(self.weights_loaded[h], it * 16 + 16 + UP)
            self.wait_read(dve, it, h)
        for t in (2 * pair, 2 * pair + 1):
            at = self.meta[h][:, 2 * TPR + t:2 * TPR + t + 1]
            w = None if weights is None else weights[:, t:t + 1]
            last = self.nc.vector.tensor_scalar(self.hot[h][:, t, :], self.k.iota[:, :], at, w, ALU.is_equal,
                                                *(() if w is None else (ALU.mult,)))
        if pair == PAIRS - 1:
            last.then_inc(self.hots[h], 1)

    def groups(self, dve, add_group):
        for pair in range(PAIRS):
            self.make_hots(dve, 0, 0, pair)

        def turn(it, more):
            for h in range(2):
                nxt = (it, 1) if h == 0 else (it + 1, 0)
                between = (lambda pair: self.make_hots(dve, *nxt, pair)) if h == 0 or more else (lambda pair: None)
                add_group(it, h, self.registers(it * 2 + h), between)
        with dve.Fori(0, ROWS // 2 - 1) as it:
            turn(it, True)
        turn(ROWS // 2 - 1, False)

    def add_pair(self, dve, it, h, pair, at):
        w, q, n = self.width, it * 2 + h, self.slots
        dve.wait_ge(self.summed[h], it * PAIRS + (pair + 1) + UP)
        before = pair - 1
        dve.wait_ge(self.added[before % n], (q * (PAIRS // n) + (before // n + 1 if pair else 0)) + UP)
        to = self.acc[0:w, bass.ds(at, WIN)]
        self.nc.vector.tensor_tensor(to, self.ps[pair % n][0:w, :], to, ALU.add).then_inc(self.added[pair % n], 1)

    def sum_pair(self, pe, it, h, pair, row_of_tile):
        q, n = it * 2 + h, self.slots
        pe.wait_ge(self.added[pair % n], q * (PAIRS // n) + pair // n + UP)
        for j in range(2):
            t = 2 * pair + j
            last = self.nc.tensor.matmul(self.ps[pair % n][0:self.width, :], row_of_tile(t), self.hot[h][:, t, :],
                                         start=j == 0, stop=j == 1)
        last.then_inc(self.summed[h], 1)


def gather_and_sum(nc, sb, psum, sem, k, edge_meta, bases, table, factors=None):
    name = "l2" if factors is not None else "l0"
    sums = SumPass(nc, sb, psum, sem, k, name, bases, D,
                   weights=lambda sums, h: None if factors is not None else sums.meta[h][:, TPR:2 * TPR])
    rows = [sb(f"rows{h}", [P, TPR, D], F32) for h in range(2)]
    factor = [sb(f"factor{h}", [P, TPR, D], F32) for h in range(2)] if factors is not None else None
    factor_loaded, multiplied = ([sem(f"{name}_{x}{h}") for h in range(2)] for x in ("factor_loaded", "multiplied"))
    gathered, g0 = k.pool_dma.take(ROWS // 2 * 16 * TPR)
    with k.block() as block:
        @block.sync
        def _(sp):
            sums.load_bases(sp)
            with sp.Fori(0, ROWS // 2) as it:
                for h in range(2):
                    sp.wait_ge(gathered[h], it * (16 * TPR) + g0[h])
                    sp.sem_inc(k.held, 1)
                    sums.load_meta(sp, it, h, edge_meta)
                    if factors is not None:
                        sp.wait_ge(multiplied[h], it * 2 + UP)
                        sp.dma_start(factor[h][:, :, :], factors[it * 2 + h]).then_inc(factor_loaded[h], 16)

        @block.gpsimd
        def _(pool):
            with pool.Fori(0, ROWS // 2) as it:
                for h in range(2):
                    pool.wait_ge(sums.meta_loaded[h], it * 16 + 16 + UP)
                    sums.wait_read(pool, it, h)
                    pool.sem_inc(k.turns, 1)
                    index = sums.meta[h][:, :].bitcast(U32)
                    for t in range(TPR):
                        pool.indirect_dma_start(out=rows[h][:, t, :], out_offset=None, in_=table,
                                                in_offset=bass.IndirectOffsetOnAxis(ap=index[:, t:t + 1], axis=0)
                                                ).then_inc(gathered[h], 16)

        @block.vector
        def _(dve):
            sums.start_dve(dve)

            def add_group(it, h, at, between):
                if factors is not None:
                    dve.wait_ge(factor_loaded[h], it * 16 + 16 + UP)
                    dve.wait_ge(gathered[h], it * (16 * TPR) + (g0[h] + 16 * TPR))
                    for a in (0, TPR // 2):
                        part = rows[h][:, a:a + TPR // 2, :]
                        nc.vector.tensor_tensor(part, part, factor[h][:, a:a + TPR // 2, :], ALU.mult).then_inc(multiplied[h], 1)
                for pair in range(PAIRS):
                    sums.add_pair(dve, it, h, pair, at[pair])
                    between(pair)
            sums.groups(dve, add_group)

        @block.tensor
        def _(pe):
            with pe.Fori(0, ROWS // 2) as it:
                for h in range(2):
                    pe.wait_ge(sums.hots[h], it + 1 + UP)
                    pe.wait_ge(gathered[h], it * (16 * TPR) + (g0[h] + 16 * TPR))
                    for pair in range(PAIRS):
                        if factors is not None and pair % (PAIRS // 2) == 0:
                            pe.wait_ge(multiplied[h], it * 2 + (1 + 2 * pair // PAIRS) + UP)
                        sums.sum_pair(pe, it, h, pair, lambda t: rows[h][:, t, :])


GROUP = 7
NG = NB // GROUP
assert NG * GROUP == NB


class Signals:

    def __init__(self, sem, names):
        self.sems = {name: sem(name) for name in names.split()}

    def of(self, name):
        return self.sems[name]

    def raise_(self, ins, name, by=1):
        ins.then_inc(self.of(name), by)

    def wait(self, eng, name, it, by=1):
        eng.wait_ge(self.of(name), it * by + by + UP)

    def wait_slot(self, eng, name, it):
        eng.wait_ge(self.of(name), it - 1 + UP)

    def wait_before(self, eng, name, it, by=1):
        eng.wait_ge(self.of(name), it * by + UP)


def over_blocks(ap, n=GROUP):
    p, f = ap.shape
    return ap.rearrange("p (o f) -> p o f", o=1).to_broadcast([p, n, f])


def per_block(ap, f):
    p, n = ap.shape
    return ap.rearrange("p (n o) -> p n o", o=1).to_broadcast([p, n, f])


def update_nodes(nc, sb, psum, sem, k, *, mode, weights, biases, K, x_in=None, x_out=None, sums=None,
                 row_of=None, extra=None, tables=(), norm=None, cnt=None, loop=None,
                 spot=None, placed=None):
    sig = Signals(sem, "x_loaded0 x_loaded1 extra_loaded0 extra_loaded1 x_made x_stored0 x_stored1 index_made l0 l1 u0 u1 u2 u3 u4 u5 exp_made n0 n1 stats_made "
                  "dev_made scale_made h_made h_turned h_t_made product0_made product1_made bank_read out_made "
                  "own_copied table0_stored table1_stored")
    per_turn = 16 * GROUP * (2 if loop else 1)
    per_slot = per_turn + (16 * GROUP if placed is not None else 0)
    gathered, g0 = k.pool_dma.take(NG // 2 * per_slot if sums is not None else 0)
    EF = extra.shape[-1] if extra is not None else D
    F = weights[0].shape[1]
    BANK = 512 // F if F <= 512 else 1
    banks = min(-(-GROUP // BANK), 4)
    rounds = [range(a, min(a + banks * BANK, GROUP)) for a in range(0, GROUP, banks * BANK)]
    xs, ss, exs = ([sb(f"{n}{i}", [P, GROUP, D], F32) for i in range(2)] for n in ("x", "s", "ex"))
    indices = [sb(f"index{i}", [P, 2, GROUP], U32) for i in range(2)]
    loop_alphas = [sb(f"loop_alpha{i}", [P, GROUP, loop[0] if loop else 1], F32) for i in range(2)]
    own_width = placed.shape[1] if placed is not None else 1
    owns = [sb(f"own{i}", [P, GROUP, own_width], F32) for i in range(2)]
    h = sb("h", [P, GROUP, D], F32)
    t0 = sb("t0", [P, GROUP, D], F32)
    h_t = sb("h_t", [P, GROUP * P], F32)
    out = sb("out", [P, GROUP, F], F32)
    stats = sb("stats", [P, GROUP, 6], F32)
    mv = sb("mv", [P, GROUP, 2], F32)
    rstd, dev, shift, count = (sb(n, [P, GROUP], F32) for n in ("rstd", "dev", "shift", "count"))
    eps = sb("eps", [P, 1], F32)
    w = sb("w", [P, F], F32)
    b_in = sb("b_in", [P, D], F32)
    b_out = sb("b_out", [P, F], F32)
    bn = sb("bn", [P, 6, D], F32)
    ps_t = psum("ps_t", [P, 2, 512], F32)
    ps_o = psum("ps_o", [P, banks, 512], F32)
    ready, made = sem("nodes_ready"), sem("nodes_made")
    has_x, has_sums = x_in is not None, sums is not None
    n_loads = 0

    def wide(v, f):
        return v.rearrange("(o f) -> o f", o=1).to_broadcast([P, f])
    with k.block() as block:
        @block.sync
        def _(sp):
            nonlocal n_loads
            loads = [(w[0:K, :], weights[0])]
            if biases[0] is not None:
                f = biases[0].shape[0]
                loads.append((b_in[:, 0:f], wide(biases[0], f)))
            at = 0
            for b, f in biases[1]:
                if b is not None:
                    loads.append((b_out[:, at:at + f], wide(b, f)))
                at += f
            for i, v in enumerate(norm or ()):
                loads.append((bn[:, i, :], wide(v, D)))
            if biases[1]:
                sp.wait_ge(made, 1 + UP)
            for to, of in loads:
                sp.dma_start(to, of).then_inc(ready, 16)
            n_loads = len(loads)

            def load(turn, i):
                it = turn * 2 + i
                sig.wait_slot(sp, "h_made", it)
                sp.sem_inc(k.held, 1)
                if has_x:
                    if x_out is not None:
                        sig.wait_before(sp, f"x_stored{i}", turn, 16)
                    sig.raise_(sp.dma_start(xs[i][:, :, :], x_in[it]), f"x_loaded{i}", 16)
                if extra is not None:
                    sig.raise_(sp.dma_start(exs[i][:, :, 0:EF], extra[it]), f"extra_loaded{i}", 16)

            def turns(turn, more):
                for i in range(2):
                    it = turn * 2 + i
                    if i == 0:
                        load(turn, 1)
                    elif more:
                        load(turn + 1, 0)
                    if x_out is not None:
                        sig.wait(sp, "x_made", it)
                        sig.raise_(sp.dma_start(x_out[it], xs[i][:, :, :]), f"x_stored{i}", 16)
                    sig.wait(sp, "out_made", it)
                    for j, (table, a, f) in enumerate(tables):
                        ins = sp.dma_start(table[it], out[:, :, a:a + f])
                        sig.raise_(ins, f"table{j}_stored", 16)
            load(0, 0)
            with sp.Fori(0, NG // 2 - 1) as turn:
                turns(turn, True)
            turns(NG // 2 - 1, False)
            for i in range(len(tables)):
                sig.wait(sp, f"table{i}_stored", NG - 1, 16)
            if x_out is not None:
                for i in range(2):
                    sig.wait(sp, f"x_stored{i}", NG // 2 - 1, 16)

        @block.gpsimd
        def _(pool):
            def gather(turn, i):
                it = turn * 2 + i
                pool.wait_ge(gathered[i], turn * per_slot + g0[i])
                if loop or placed is not None:
                    nc.gpsimd.tensor_copy(indices[i][:, 1, :], spot[:, bass.ds(it * GROUP, GROUP)])
                sig.raise_(nc.gpsimd.tensor_copy(indices[i][:, 0, :], row_of[:, bass.ds(it * GROUP, GROUP)]), "index_made")
                sig.wait(pool, "index_made", it)
                sig.wait_slot(pool, "h_made", it)
                pool.sem_inc(k.turns, 1)
                for j in range(GROUP):
                    pool.indirect_dma_start(
                        out=ss[i][:, j, :], out_offset=None, in_=sums,
                        in_offset=bass.IndirectOffsetOnAxis(ap=indices[i][:, 0, j:j + 1], axis=0)).then_inc(gathered[i], 16)
                    if loop:
                        pool.indirect_dma_start(
                            out=loop_alphas[i][:, j, :], out_offset=None, in_=loop[1],
                            in_offset=bass.IndirectOffsetOnAxis(ap=indices[i][:, 1, j:j + 1], axis=0)).then_inc(gathered[i], 16)

            def scatter(turn, i):
                if placed is None:
                    return
                sig.wait(pool, "own_copied", turn * 2 + i)
                pool.sem_inc(k.turns, 1)
                for j in range(GROUP):
                    pool.indirect_dma_start(
                        out=placed, out_offset=bass.IndirectOffsetOnAxis(ap=indices[i][:, 1, j:j + 1], axis=0),
                        in_=owns[i][:, j, :], in_offset=None).then_inc(gathered[i], 16)

            def turns(turn, more):
                gather(turn, 1)
                scatter(turn, 0)
                if more:
                    gather(turn + 1, 0)
                scatter(turn, 1)
            if has_sums:
                gather(0, 0)
                with pool.Fori(0, NG // 2 - 1) as turn:
                    turns(turn, True)
                turns(NG // 2 - 1, False)
                for i in range(2):
                    pool.wait_ge(gathered[i], NG // 2 * per_slot + g0[i])

        @block.vector
        def _(dve):
            nc.vector.memset(eps[:, :], 1e-5)
            if norm:
                nc.vector.memset(bn[:, 4, :], 1e-3)
            nc.vector.memset(b_out[:, :], 0.0).then_inc(made, 1)
            dve.wait_ge(made, 1 + UP)
            dve.wait_ge(ready, n_loads * 16 + UP)
            if norm:
                c = Chain(dve, made, 1)
                c.step(nc.vector.tensor_tensor(bn[:, 4, :], bn[:, 4, :], bn[:, 3, :], ALU.add))
                dve.wait_ge(made, 3 + UP)
                c.n += 1
                c.step(nc.vector.reciprocal(bn[:, 5, :], bn[:, 5, :]))
                c.step(nc.vector.tensor_tensor(bn[:, 4, :], bn[:, 5, :], bn[:, 0, :], ALU.mult))
                c.step(nc.vector.tensor_tensor(bn[:, 5, :], bn[:, 4, :], bn[:, 2, :], ALU.mult))
                c.step(nc.vector.tensor_tensor(bn[:, 5, :], bn[:, 1, :], bn[:, 5, :], ALU.subtract))
            with dve.Fori(0, NG // 2) as turn:
                for i in range(2):
                    it = turn * 2 + i
                    x, s, ex, loop_alpha, own = xs[i], ss[i], exs[i], loop_alphas[i], owns[i]
                    if has_sums:
                        dve.wait_ge(gathered[i], turn * per_slot + (g0[i] + per_turn))
                    if has_x:
                        sig.wait(dve, f"x_loaded{i}", turn, 16)
                    if loop:
                        sig.wait(dve, f"extra_loaded{i}", turn, 16)
                        by_head = ex[:, :, 0:EF].rearrange("p n (h c) -> p n h c", h=loop[0])
                        sig.raise_(nc.vector.tensor_tensor(by_head, by_head, loop_alpha[:, :, :].rearrange(
                            "p n (h o) -> p n h o", o=1).to_broadcast([P, GROUP, loop[0], EF // loop[0]]), ALU.mult), "l0")
                        sig.wait(dve, "l0", it)
                        sig.raise_(nc.vector.tensor_tensor(s[:, :, 0:EF], s[:, :, 0:EF], ex[:, :, 0:EF], ALU.add), "l1")
                        sig.wait(dve, "l1", it)
                    if mode == "residual":
                        sig.raise_(nc.vector.tensor_tensor(s[:, :, :], s[:, :, :], over_blocks(b_in[:, :]), ALU.add), "u0")
                        sig.wait(dve, "u0", it)
                        sig.raise_(nc.vector.tensor_tensor(x[:, :, :], x[:, :, :], s[:, :, :], ALU.add), "x_made")
                        sig.wait(dve, "x_made", it)
                    if mode == "norm":
                        sig.wait(dve, f"extra_loaded{i}", turn, 16)
                        sig.raise_(nc.vector.tensor_scalar(count[:, :], cnt[:, bass.ds(it * GROUP, GROUP)], 1.0, None, ALU.max), "u0")
                        sig.wait(dve, "u0", it)
                        sig.raise_(nc.vector.reciprocal(count[:, :], count[:, :]), "u1")
                        sig.wait(dve, "u1", it)
                        sig.raise_(nc.vector.tensor_tensor(s[:, :, :], s[:, :, :], per_block(count[:, :], D), ALU.mult), "u2")
                        sig.wait(dve, "u2", it)
                        sig.raise_(nc.vector.tensor_tensor(s[:, :, :], s[:, :, :], ex[:, :, :], ALU.add), "u3")
                        sig.wait(dve, "u3", it)
                        sig.raise_(nc.vector.tensor_tensor(s[:, :, :], s[:, :, :], over_blocks(bn[:, 4, :]), ALU.mult), "u4")
                        sig.wait(dve, "u4", it)
                        sig.raise_(nc.vector.tensor_tensor(s[:, :, :], s[:, :, :], over_blocks(bn[:, 5, :]), ALU.add), "u5")
                        sig.wait(dve, "u5", it)
                        sig.raise_(nc.vector.scalar_tensor_tensor(x[:, :, :], s[:, :, :], 0.0, x[:, :, :], ALU.max, ALU.add), "x_made")
                        sig.wait(dve, "x_made", it)
                    if mode == "elu":
                        sig.wait_before(dve, "h_turned", it)
                        sig.raise_(nc.vector.tensor_tensor(s[:, :, 0:K], s[:, :, 0:K], over_blocks(b_in[:, 0:K]), ALU.add), "u0")
                        sig.wait(dve, "u0", it)
                        sig.raise_(nc.vector.tensor_scalar(t0[:, :, 0:K], s[:, :, 0:K], 0.0, None, ALU.min), "u1")
                        sig.wait(dve, "exp_made", it)
                        sig.raise_(nc.vector.tensor_scalar(s[:, :, 0:K], s[:, :, 0:K], 0.0, None, ALU.max), "u2")
                        sig.wait(dve, "u2", it)
                        sig.raise_(nc.vector.scalar_tensor_tensor(h[:, :, 0:K], t0[:, :, 0:K], -1.0, s[:, :, 0:K], ALU.add, ALU.add), "h_made")
                        sig.wait(dve, "h_made", it)
                    else:
                        sig.wait_before(dve, "h_made", it)
                        for j in range(GROUP):
                            last = nc.vector.bn_stats(stats[:, j, :], x[:, j, :])
                        sig.raise_(last, "n0")
                        sig.wait(dve, "n0", it)
                        dve.sem_inc(k.held, 1)
                        for j in range(GROUP):
                            last = nc.vector.bn_aggr(mv[:, j, :], stats[:, j, :])
                        sig.raise_(last, "stats_made")
                        sig.wait(dve, "dev_made", it)
                        sig.raise_(nc.vector.reciprocal(rstd[:, :], dev[:, :]), "n1")
                        sig.wait(dve, "n1", it)
                        sig.raise_(nc.vector.scalar_tensor_tensor(shift[:, :], mv[:, :, 0], -1.0, rstd[:, :], ALU.mult, ALU.mult), "scale_made")
                    for j in range(len(tables)):
                        sig.wait_before(dve, f"table{j}_stored", it, 16)
                    for r, blocks in enumerate(rounds):
                        sig.wait(dve, f"product{r}_made", it)
                        for b, a in enumerate(range(blocks[0], blocks[-1] + 1, BANK)):
                            n = min(BANK, blocks[-1] + 1 - a)
                            last = nc.vector.tensor_tensor(out[:, a:a + n, :], ps_o[:, b, 0:n * F].rearrange("p (n f) -> p n f", n=n),
                                                           over_blocks(b_out[:, :], n), ALU.add)
                        sig.raise_(last, "out_made" if r == len(rounds) - 1 else "bank_read")
                    if placed is not None:
                        sig.wait(dve, "out_made", it)
                        sig.raise_(nc.vector.tensor_copy(own[:, :, :], out[:, :, F - own_width:F]), "own_copied")
                        sig.wait(dve, "own_copied", it)

        @block.scalar
        def _(act):
            if norm:
                act.wait_ge(made, 2 + UP)
                nc.scalar.activation(bn[:, 5, :], bn[:, 4, :], ACT.Sqrt).then_inc(made, 1)
            else:
                act.wait_ge(made, 1 + UP)
            with act.Fori(0, NG // 2) as turn:
                for i in range(2):
                    it, x = turn * 2 + i, xs[i]
                    if mode == "elu":
                        sig.wait(act, "u1", it)
                        sig.raise_(nc.scalar.activation(t0[:, :, 0:K], t0[:, :, 0:K], ACT.Exp), "exp_made")
                    else:
                        sig.wait(act, "stats_made", it)
                        sig.raise_(nc.scalar.activation(dev[:, :], mv[:, :, 1], ACT.Sqrt, bias=eps[:, :]), "dev_made")
                        sig.wait(act, "scale_made", it)
                        sig.wait_before(act, "h_turned", it)
                        for j in range(GROUP):
                            last = nc.scalar.activation(h[:, j, :], x[:, j, :], ACT.Relu, scale=rstd[:, j:j + 1], bias=shift[:, j:j + 1])
                        sig.raise_(last, "h_made")
                    sig.wait(act, "h_turned", it)
                    sig.wait_before(act, f"product{len(rounds) - 1}_made", it)
                    nc.scalar.copy(h_t[0:K, 0:512], ps_t[0:K, 0, :])
                    sig.raise_(nc.scalar.copy(h_t[0:K, 512:GROUP * P], ps_t[0:K, 1, 0:GROUP * P - 512]), "h_t_made")

        @block.tensor
        def _(pe):
            pe.wait_ge(ready, n_loads * 16 + UP)
            with pe.Fori(0, NG) as it:
                sig.wait(pe, "h_made", it)
                sig.wait_before(pe, "h_t_made", it)
                for j in range(GROUP):
                    last = nc.tensor.transpose(ps_t[0:K, j // 4, (j % 4) * P:(j % 4 + 1) * P], h[:, j, 0:K], k.ident[:, :])
                sig.raise_(last, "h_turned")
                sig.wait(pe, "h_t_made", it)
                sig.wait_before(pe, "out_made", it)
                for r, blocks in enumerate(rounds):
                    if r:
                        sig.wait(pe, "bank_read", it)
                    for j in blocks:
                        i = j - blocks[0]
                        last = nc.tensor.matmul(ps_o[:, i // BANK, (i % BANK) * F:(i % BANK + 1) * F],
                                                h_t[0:K, j * P:(j + 1) * P], w[0:K, :], start=True, stop=True,
                                                skip_group_check=True)
                    sig.raise_(last, f"product{r}_made")


def fold_attention(nc, sb, psum, sem, k, layer, w, a_src, a_dst, K, folded):
    heads, c = a_src.shape
    F = heads * c
    w_sb, a_sb = sb("w", [P, F + 2 * heads], F32), sb("a", [P, 2 * heads], F32)
    w_t = sb("w_t", [P, P], F32)
    ps = psum("ps", [P, 2, P], F32)
    s = {x: sem(f"fold{layer}_{x}") for x in ("made", "loaded", "turned", "copied", "product", "done", "stored")}
    with k.block() as block:
        @block.sync
        def _(sp):
            sp.dma_start(w_sb[0:K, 0:F], w).then_inc(s["loaded"], 16)
            sp.wait_ge(s["made"], 1 + UP)
            for i, a in enumerate((a_src, a_dst)):
                for h in range(heads):
                    sp.dma_start(a_sb[h * c:(h + 1) * c, i * heads + h:i * heads + h + 1],
                                 a[h:h + 1, :].rearrange("o c -> c o")).then_inc(s["loaded"], 16)
            sp.wait_ge(s["done"], 1 + UP)
            sp.dma_start(folded, w_sb[0:K, :]).then_inc(s["stored"], 16)
            sp.wait_ge(s["stored"], 16 + UP)

        @block.vector
        def _(dve):
            nc.vector.memset(a_sb[:, :], 0.0).then_inc(s["made"], 1)
            dve.wait_ge(s["turned"], 1 + UP)
            nc.vector.tensor_copy(w_t[0:F, 0:K], ps[0:F, 0, 0:K]).then_inc(s["copied"], 1)
            dve.wait_ge(s["product"], 1 + UP)
            nc.vector.tensor_copy(w_sb[0:K, F:F + 2 * heads], ps[0:K, 1, 0:2 * heads]).then_inc(s["done"], 1)

        @block.tensor
        def _(pe):
            pe.wait_ge(s["loaded"], (1 + 2 * heads) * 16 + UP)
            nc.tensor.transpose(ps[0:F, 0, 0:K], w_sb[0:K, 0:F], k.ident[0:K, 0:K]).then_inc(s["turned"], 1)
            pe.wait_ge(s["copied"], 1 + UP)
            nc.tensor.matmul(ps[0:K, 1, 0:2 * heads], w_t[0:F, 0:K], a_sb[0:F, :], start=True, stop=True).then_inc(s["product"], 1)


def finish_nodes(nc, sb, psum, sem, k, *, x_in, own, sums, row_of, has, w1b, w2, b2, x_out):
    sig = Signals(sem, "x_loaded0 x_loaded1 extra_loaded0 extra_loaded1 x_stored0 x_stored1 index_made flag_made u0 h_made h_turned h_turned_copied product_made u1 u2 "
                  "r_turned r_turned_copied product2_made u3 out_made")
    gathered, g0 = k.pool_dma.take(NG // 2 * 16 * GROUP)
    xs, ss = ([sb(f"{n}{i}", [P, GROUP, D], F32) for i in range(2)] for n in ("x", "s"))
    owns = [sb(f"own{i}", [P, GROUP, 2 * D], F32) for i in range(2)]
    indices = [sb(f"index{i}", [P, GROUP], U32) for i in range(2)]
    r = sb("r", [P, GROUP, D], F32)
    flag = sb("flag", [P, GROUP], F32)
    turned = sb("turned", [P, GROUP * P], F32)
    w = sb("w", [P, 2, D], F32)
    b = sb("b", [P, D], F32)
    ps_t, ps_o = psum("ps_t", [P, 2, 512], F32), psum("ps_o", [P, 2, 512], F32)
    ready = sem("nodes_ready")
    with k.block() as block:
        @block.sync
        def _(sp):
            sp.dma_start(w[:, 0, :], w1b).then_inc(ready, 16)
            sp.dma_start(w[:, 1, :], w2).then_inc(ready, 16)
            sp.dma_start(b[:, :], b2.rearrange("(o f) -> o f", o=1).to_broadcast([P, D])).then_inc(ready, 16)

            def load(turn, i):
                it = turn * 2 + i
                sig.wait_slot(sp, "u1", it)
                sp.sem_inc(k.held, 1)
                sig.wait_before(sp, f"x_stored{i}", turn, 16)
                sig.raise_(sp.dma_start(xs[i][:, :, :], x_in[it]), f"x_loaded{i}", 16)
                sig.raise_(sp.dma_start(owns[i][:, :, :], own[it]), f"extra_loaded{i}", 16)

            def turns(turn, more):
                for i in range(2):
                    if i == 0:
                        load(turn, 1)
                    elif more:
                        load(turn + 1, 0)
                    sig.wait(sp, "out_made", turn * 2 + i)
                    sig.raise_(sp.dma_start(x_out[turn * 2 + i], xs[i][:, :, :]), f"x_stored{i}", 16)
            load(0, 0)
            with sp.Fori(0, NG // 2 - 1) as turn:
                turns(turn, True)
            turns(NG // 2 - 1, False)
            for i in range(2):
                sig.wait(sp, f"x_stored{i}", NG // 2 - 1, 16)

        @block.gpsimd
        def _(pool):
            with pool.Fori(0, NG // 2) as turn:
                for i in range(2):
                    it = turn * 2 + i
                    pool.wait_ge(gathered[i], turn * (16 * GROUP) + g0[i])
                    sig.raise_(nc.gpsimd.tensor_copy(indices[i][:, :], row_of[:, bass.ds(it * GROUP, GROUP)]), "index_made")
                    sig.wait(pool, "index_made", it)
                    sig.wait_slot(pool, "h_turned", it)
                    pool.sem_inc(k.turns, 1)
                    for j in range(GROUP):
                        pool.indirect_dma_start(
                            out=ss[i][:, j, :], out_offset=None, in_=sums,
                            in_offset=bass.IndirectOffsetOnAxis(ap=indices[i][:, j:j + 1], axis=0)).then_inc(gathered[i], 16)

        @block.vector
        def _(dve):
            dve.wait_ge(ready, 48 + UP)
            with dve.Fori(0, NG // 2) as turn:
                for i in range(2):
                    it = turn * 2 + i
                    x, s, o = xs[i], ss[i], owns[i]
                    sig.wait_before(dve, "out_made", it)
                    sig.raise_(nc.vector.tensor_copy(flag[:, :], has[:, bass.ds(it * GROUP, GROUP)]), "flag_made")
                    sig.wait(dve, "flag_made", it)
                    dve.wait_ge(gathered[i], turn * (16 * GROUP) + (g0[i] + 16 * GROUP))
                    sig.wait(dve, f"extra_loaded{i}", turn, 16)
                    sig.raise_(nc.vector.tensor_tensor(s[:, :, :], s[:, :, :], o[:, :, 0:D], ALU.add), "u0")
                    sig.wait(dve, "u0", it)
                    sig.raise_(nc.vector.tensor_tensor(s[:, :, :], s[:, :, :], per_block(flag[:, :], D), ALU.mult), "h_made")
                    sig.wait(dve, "product_made", it)
                    for bank, (a, n) in enumerate(((0, 4), (4, GROUP - 4))):
                        last = nc.vector.tensor_tensor(r[:, a:a + n, :], ps_o[:, bank, 0:n * D].rearrange("p (n f) -> p n f", n=n),
                                                       o[:, a:a + n, D:2 * D], ALU.add)
                    sig.raise_(last, "u1")
                    sig.wait(dve, "u1", it)
                    sig.raise_(nc.vector.tensor_scalar(r[:, :, :], r[:, :, :], 0.0, None, ALU.max), "u2")
                    sig.wait(dve, f"x_loaded{i}", turn, 16)
                    sig.raise_(nc.vector.tensor_tensor(x[:, :, :], x[:, :, :], over_blocks(b[:, :]), ALU.add), "u3")
                    sig.wait(dve, "u3", it)
                    sig.wait(dve, "product2_made", it)
                    for bank, (a, n) in enumerate(((0, 4), (4, GROUP - 4))):
                        last = nc.vector.tensor_tensor(x[:, a:a + n, :], ps_o[:, bank, 0:n * D].rearrange("p (n f) -> p n f", n=n),
                                                       x[:, a:a + n, :], ALU.add)
                    sig.raise_(last, "out_made")

        @block.scalar
        def _(act):
            with act.Fori(0, NG) as it:
                for x in ("h_turned", "r_turned"):
                    sig.wait(act, x, it)
                    nc.scalar.copy(turned[:, 0:512], ps_t[:, 0, :])
                    sig.raise_(nc.scalar.copy(turned[:, 512:GROUP * P], ps_t[:, 1, 0:GROUP * P - 512]), x + "_copied")

        @block.tensor
        def _(pe):
            pe.wait_ge(ready, 48 + UP)
            with pe.Fori(0, NG // 2) as turn:
                for i in range(2):
                    it, s = turn * 2 + i, ss[i]
                    sig.wait_before(pe, "out_made", it)
                    for n, (src, made, name_t, product) in enumerate(((s, "h_made", "h_turned", "product_made"),
                                                                      (r, "u2", "r_turned", "product2_made"))):
                        sig.wait(pe, made, it)
                        for j in range(GROUP):
                            last = nc.tensor.transpose(ps_t[:, j // 4, (j % 4) * P:(j % 4 + 1) * P], src[:, j, :], k.ident[:, :])
                        sig.raise_(last, name_t)
                        sig.wait(pe, name_t + "_copied", it)
                        for j in range(GROUP):
                            last = nc.tensor.matmul(ps_o[:, j // 4, (j % 4) * P:(j % 4 + 1) * P], turned[:, j * P:(j + 1) * P],
                                                    w[:, n, :], start=True, stop=True, skip_group_check=True)
                        sig.raise_(last, product)
class GatedFilters:

    HALF = TPR // 2
    QUADS = HALF // 4

    def __init__(self, nc, sb, psum, sem, attr, gated, start, w_gate, b_gate, w_filt, b_filt):
        self.nc = nc
        size = ROWS // 2 * COLS
        self.attr_dram, self.gated_dram = (x[start:start + size, :].rearrange("(g p h t) f -> g h p t f", g=ROWS // 2, p=P, h=2)
                                           for x in (attr, gated))
        self.params = (w_gate, b_gate, w_filt, b_filt)
        self.attr = [sb(f"attr{h}", [P, self.HALF, D], F32) for h in range(2)]
        self.out = [sb(f"gated{h}", [P, self.HALF, D], F32) for h in range(2)]
        self.attr_t, self.before_gate, self.gate, self.filt = (
            [sb(f"{x}{i}", [P, 4 * D], F32) for i in range(2)] for x in ("attr_t", "before_gate", "gate", "filt"))
        self.w = sb("w_gated", [P, 2, D], F32)
        self.b = sb("b_gated", [P, 2, D], F32)
        self.ps_t, self.ps_g, self.ps_f = ([psum(f"{x}{i}", [P, 4 * D], F32) for i in range(2)] for x in ("ps_attr", "ps_gate", "ps_filt"))
        self.params_loaded = sem("gated_params_loaded")
        self.loaded, self.stored = ([sem(f"gated_{x}{h}") for h in range(2)] for x in ("loaded", "stored"))
        self.turned, self.copied, self.product, self.biased, self.sigmoid, self.filtered, self.made = (
            [sem(f"gated_{x}{i}") for i in range(2)] for x in ("turned", "copied", "product", "biased", "sigmoid", "filtered", "made"))

    def load_params(self, sp):
        w_gate, b_gate, w_filt, b_filt = self.params
        for i, (w, b) in enumerate(((w_gate, b_gate), (w_filt, b_filt))):
            sp.dma_start(self.w[:, i, :], w).then_inc(self.params_loaded, 16)
            sp.dma_start(self.b[:, i, :], b.rearrange("(o f) -> o f", o=1).to_broadcast([P, D])).then_inc(self.params_loaded, 16)

    def nth(self, it, h):
        return it * 2 + h

    def sp(self, sp, it, h):
        for i in range(2):
            sp.wait_ge(self.turned[i], self.nth(it, 0) + UP)
        sp.dma_start(self.attr[h][:, :, :], self.attr_dram[it, h]).then_inc(self.loaded[h], 16)

    def pe(self, pe, it, h):
        nc, n = self.nc, self.nth(it, h)
        pe.wait_ge(self.loaded[h], it * 16 + 16 + UP)
        for i in range(2):
            pe.wait_ge(self.copied[i], n + UP)
            for j in range(4):
                last = nc.tensor.transpose(self.ps_t[i][:, j * P:(j + 1) * P], self.attr[h][:, 4 * i + j, :], self.ident)
            last.then_inc(self.turned[i], 1)
        for i in range(2):
            pe.wait_ge(self.copied[i], n + 1 + UP)
            pe.wait_ge(self.filtered[i], n + UP)
            for ps, w in ((self.ps_g, 0), (self.ps_f, 1)):
                for j in range(4):
                    last = nc.tensor.matmul(ps[i][:, j * P:(j + 1) * P], self.attr_t[i][:, j * P:(j + 1) * P], self.w[:, w, :],
                                            start=True, stop=True, skip_group_check=True)
            last.then_inc(self.product[i], 1)

    def act(self, act, it, h):
        nc, n = self.nc, self.nth(it, h)
        for i in range(2):
            act.wait_ge(self.turned[i], n + 1 + UP)
            act.wait_ge(self.product[i], n + UP)
            nc.scalar.copy(self.attr_t[i][:, :], self.ps_t[i][:, :]).then_inc(self.copied[i], 1)
        for i in range(2):
            act.wait_ge(self.biased[i], n + 1 + UP)
            act.wait_ge(self.made[i], n + UP)
            nc.scalar.activation(self.gate[i][:, :], self.before_gate[i][:, :], ACT.Sigmoid).then_inc(self.sigmoid[i], 1)

    def dve(self, dve, it, h):
        nc, n = self.nc, self.nth(it, h)

        def tiled(a):
            return a[:, :].rearrange("p (j f) -> p j f", f=D)
        for i in range(2):
            dve.wait_ge(self.product[i], n + 1 + UP)
            dve.wait_ge(self.sigmoid[i], n + UP)
            nc.vector.tensor_tensor(tiled(self.before_gate[i]), tiled(self.ps_g[i]), over_blocks(self.b[:, 0, :], 4),
                                    ALU.add).then_inc(self.biased[i], 1)
            dve.wait_ge(self.made[i], n + UP)
            nc.vector.tensor_tensor(tiled(self.filt[i]), tiled(self.ps_f[i]), over_blocks(self.b[:, 1, :], 4),
                                    ALU.add).then_inc(self.filtered[i], 1)
        dve.wait_ge(self.stored[h], it * 16 + UP)
        for i in range(2):
            dve.wait_ge(self.filtered[i], n + 1 + UP)
            dve.wait_ge(self.sigmoid[i], n + 1 + UP)
            nc.vector.tensor_tensor(self.out[h][:, 4 * i:4 * i + 4, :], tiled(self.filt[i]), tiled(self.gate[i]),
                                    ALU.mult).then_inc(self.made[i], 1)

    def store(self, eng, it, h):
        for i in range(2):
            eng.wait_ge(self.made[i], self.nth(it, h) + 1 + UP)
        eng.dma_start(self.gated_dram[it, h], self.out[h][:, :, :]).then_inc(self.stored[h], 16)

    def finish(self, eng):
        for h in range(2):
            eng.wait_ge(self.stored[h], ROWS // 2 * 16 + UP)


class KeptRows:

    HALF = TPR // 2

    def __init__(self, nc, sb, sem, k, table, index, kept, start):
        self.k, self.table = k, table
        self.index_dram, self.kept_dram, self.start = index, kept, start
        self.index = [sb(f"kept_index{h}", [P, self.HALF], U32) for h in range(2)]
        self.rows = [sb(f"kept_rows{h}", [P, self.HALF, D], F32) for h in range(2)]
        self.loaded, self.stored = ([sem(f"kept_{x}{h}") for h in range(2)] for x in ("loaded", "stored"))
        self.gathered, self.g0 = k.pool_dma.take(ROWS // 2 * 16 * self.HALF)

    def sp(self, sp, it, h):
        sp.wait_ge(self.gathered[h], it * (16 * self.HALF) + self.g0[h])
        sp.sem_inc(self.k.held, 1)
        at = 3 * TPR + h * self.HALF
        sp.dma_start(self.index[h][:, :], self.index_dram[it + self.start, :, at:at + self.HALF].bitcast(U32)).then_inc(self.loaded[h], 16)

    def pool(self, pool, it, h):
        pool.wait_ge(self.loaded[h], it * 16 + 16 + UP)
        pool.wait_ge(self.stored[h], it * 16 + UP)
        pool.sem_inc(self.k.turns, 1)
        for t in range(self.HALF):
            pool.indirect_dma_start(out=self.rows[h][:, t, :], out_offset=None, in_=self.table,
                                    in_offset=bass.IndirectOffsetOnAxis(ap=self.index[h][:, t:t + 1], axis=0)
                                    ).then_inc(self.gathered[h], 16)

    def act(self, act, it, h):
        act.wait_ge(self.gathered[h], it * (16 * self.HALF) + (self.g0[h] + 16 * self.HALF))
        act.dma_start(self.kept_dram[it + self.start, :, h * self.HALF * D:(h + 1) * self.HALF * D], self.rows[h][:, :, :]).then_inc(self.stored[h], 16)

    def finish(self, act):
        for h in range(2):
            act.wait_ge(self.stored[h], ROWS // 2 * 16 + UP)


def gather_rows(nc, sb, psum, sem, k, F, H, edge_meta, table, rows_out, scores_out, filters=None):
    WROW = F + H
    meta = [sb(f"meta{h}", [P, TPR], U32) for h in range(2)]
    rows = [sb(f"rows{h}", [P, TPR, WROW], F32) for h in range(2)]
    score = [sb(f"score{h}", [TPR * H, P], F32) for h in range(2)]
    ps = [psum(f"ps{h}", [TPR * H, P], F32) for h in range(2)]
    gathered, g0 = k.pool_dma.take(ROWS // 2 * 16 * TPR)
    column = [sb(f"column{h}", [P, TPR * H], F32) for h in range(2)]
    extra = GatedFilters(nc, sb, psum, sem, *filters) if filters else None
    if extra:
        extra.ident = k.ident[:, :]
    loaded, picked, turned, copied, stored, kept = ([sem(f"gat_rows_{x}{h}") for h in range(2)] for x in
                                                    ("loaded", "picked", "turned", "copied", "stored", "kept"))
    with k.block() as block:
        @block.sync
        def _(sp):
            if extra:
                extra.load_params(sp)
            with sp.Fori(0, ROWS // 2) as it:
                for h in range(2):
                    if extra:
                        extra.sp(sp, it, h)
                    sp.wait_ge(gathered[h], it * (16 * TPR) + g0[h])
                    sp.dma_start(meta[h][:, :], edge_meta[it * 2 + h, :, 0:TPR].bitcast(U32)).then_inc(loaded[h], 16)

        @block.gpsimd
        def _(pool):
            with pool.Fori(0, ROWS // 2) as it:
                for h in range(2):
                    pool.wait_ge(loaded[h], it * 16 + 16 + UP)
                    pool.wait_ge(stored[h], it * 16 + UP)
                    pool.wait_ge(turned[h], it + UP)
                    pool.sem_inc(k.turns, 1)
                    for t in range(TPR):
                        pool.indirect_dma_start(out=rows[h][:, t, :], out_offset=None, in_=table,
                                                in_offset=bass.IndirectOffsetOnAxis(ap=meta[h][:, t:t + 1], axis=0)
                                                ).then_inc(gathered[h], 16)

        @block.tensor
        def _(pe):
            if extra:
                pe.wait_ge(extra.params_loaded, 64 + UP)
            with pe.Fori(0, ROWS // 2) as it:
                for h in range(2):
                    if extra:
                        extra.pe(pe, it, h)
                    pe.wait_ge(picked[h], it + 1 + UP)
                    pe.wait_ge(copied[h], it + UP)
                    pe.sem_inc(k.held, 1)
                    nc.tensor.transpose(ps[h][:, :], column[h][:, :], k.ident[:, :]).then_inc(turned[h], 1)

        @block.vector
        def _(dve):
            if extra:
                dve.wait_ge(extra.params_loaded, 64 + UP)
            with dve.Fori(0, ROWS // 2) as it:
                for h in range(2):
                    if extra:
                        extra.dve(dve, it, h)
                    dve.wait_ge(turned[h], it + 1 + UP)
                    dve.wait_ge(kept[h], it * 16 + UP)
                    nc.vector.tensor_copy(score[h][:, :], ps[h][:, :]).then_inc(copied[h], 1)

        @block.scalar
        def _(act):
            with act.Fori(0, ROWS // 2) as it:
                for h in range(2):
                    if extra:
                        extra.act(act, it, h)
                        extra.store(act, it, h)
                    act.wait_ge(gathered[h], it * (16 * TPR) + (g0[h] + 16 * TPR))
                    act.dma_start(rows_out[it * 2 + h], rows[h][:, :, :]).then_inc(stored[h], 16)
                    act.wait_ge(turned[h], it + UP)
                    nc.scalar.copy(column[h][:, :].rearrange("p (t h) -> p t h", h=H), rows[h][:, :, F:WROW]).then_inc(picked[h], 1)
                    act.wait_ge(copied[h], it + 1 + UP)
                    act.dma_start(scores_out[it * 2 + h], score[h][:, :]).then_inc(kept[h], 16)
            for h in range(2):
                act.wait_ge(stored[h], ROWS // 2 * 16 + UP)
                act.wait_ge(kept[h], ROWS // 2 * 16 + UP)
            if extra:
                extra.finish(act)


def softmax_by_segment(nc, sb, psum, sem, k, H, flags, scores, placed, alphas, loop_alphas):
    keep = [sb(f"keep{i}", [ROWS, COLS], F32) for i in range(2)]
    drop = [sb(f"drop{i}", [ROWS, COLS], F32) for i in range(2)]
    room = sb("room", [P, COLS * H], F32)
    sc = room[0:ROWS, :].rearrange("g (t h i) -> g t h i", t=TPR, h=H)
    packed = room[:, 0:ROWS * H * TPR].rearrange("p (g c) -> p g c", g=ROWS)
    v = sb("v", [ROWS, COLS, 2 * H], F32)
    alone = sb("alone", [ROWS, COLS, H], F32)
    one, two, p, m = (sb(x, [ROWS, COLS], F32) for x in ("one", "two", "p", "m"))
    totals = sb("totals", [ROWS, 4], F32)
    last, carry = sb("last", [ROWS, 1], F32), sb("carry", [ROWS, 1], F32)
    line = sb("line", [1, ROWS], F32)
    total_line = sb("total_line", [1, 4, ROWS], F32)
    run = sb("run", [1, ROWS + 2], F32)
    ps_line, ps_col = psum("ps_line", [1, ROWS], F32), psum("ps_col", [ROWS, 1], F32)
    ps = [psum(f"ps_turn{i}", [P, 512], F32) for i in range(2)]
    names = ("loaded", "steps", "asked", "answered", "shifted", "exp_made", "alpha_made", "loops_made", "turned", "evacuated", "stored")
    s = {x: sem(f"softmax_{x}") for x in names}
    BACK = (0, 0, 1, 0, 1)
    requests = 4 + 2 * len(BACK) * H
    with k.block() as block:
        @block.sync
        def _(sp):
            sp.dma_start(keep[0][:, :], flags[0]).then_inc(s["loaded"], 16)
            sp.dma_start(keep[1][:, :], flags[1]).then_inc(s["loaded"], 16)
            sp.dma_start(sc[:, :, :, :], scores.rearrange("g (t h) i -> g t h i", h=H)).then_inc(s["loaded"], 16)
            sp.dma_start(v[:, :, :], placed[0:EP, :].rearrange("(g c) h -> g c h", c=COLS)).then_inc(s["loaded"], 16)
            sp.dma_start(loop_alphas[EP:EP + P, :], k.ones[:, 0:H]).then_inc(s["stored"], 16)
            sp.wait_ge(s["loops_made"], H + UP)
            sp.dma_start(loop_alphas[0:EP, :].rearrange("(g c) h -> g c h", c=COLS), alone[:, :, :]).then_inc(s["stored"], 16)
            sp.wait_ge(s["evacuated"], H * TPR // 4 + UP)
            sp.dma_start(alphas.rearrange("g p c -> p g c"), packed[:, :, :]).then_inc(s["stored"], 16)
            sp.wait_ge(s["stored"], 48 + UP)

        @block.vector
        def _(dve):
            c = Chain(dve, s["steps"])
            asked = Chain(dve, s["answered"])
            dve.wait_ge(s["loaded"], 64 + UP)

            def ask(ins):
                ins.then_inc(s["asked"], 1)
                asked.n += 1
                dve.wait_ge(s["answered"], asked.base + asked.n + UP)

            for i in range(2):
                c.step(nc.vector.tensor_scalar(drop[i][:, :], keep[i][:, :], -BIG, None, ALU.mult))
                c.step(nc.vector.tensor_scalar(keep[i][:, :], keep[i][:, :], -1.0, 1.0, ALU.mult, ALU.add))
                for j, x in enumerate((keep[i], drop[i])):
                    n = 2 * i + j
                    ask(nc.vector.tensor_reduce(totals[:, n:n + 1], x[:, :], mybir.AxisListType.X, ALU.min))
                    c.step(nc.vector.tensor_copy(total_line[:, n, :], ps_line[:, :]))

            def running(out, data, back, largest):
                mask = (drop if largest else keep)[back]
                ops = (ALU.add, ALU.max) if largest else (ALU.mult, ALU.add)
                start = -BIG if largest else 0.0
                fl = (lambda a: a[:, ::-1]) if back else (lambda a: a)
                c.step(nc.vector.tensor_tensor_scan(fl(out), fl(mask[:, :]), fl(data), start, *ops))
                edge = 0 if back else COLS - 1
                c.step(nc.vector.memset(run[:, :], start))
                ask(nc.vector.tensor_copy(last[:, :], out[:, edge:edge + 1]))
                c.step(nc.vector.tensor_copy(line[:, :], ps_line[:, :]))
                ask(nc.vector.tensor_tensor_scan(fl(run[:, 1:ROWS + 1]), fl(total_line[:, 2 * back + largest, :]),
                                                 fl(line[:, :]), start, *ops))
                c.step(nc.vector.tensor_copy(carry[:, :], ps_col[:, :]))
                c.step(nc.vector.tensor_tensor_scan(fl(out), fl(mask[:, :]), fl(data), carry[:, 0:1], *ops))

            def tiled(a):
                return a[:, :].rearrange("g (t i) -> g t i", i=P)

            for h in range(H):
                own = alone[:, :, h]
                running(one[:, :], v[:, :, H + h], 0, 0)
                c.step(nc.vector.tensor_tensor(tiled(two), sc[:, :, h, :], tiled(one), ALU.add))
                c.step(nc.vector.scalar_tensor_tensor(p[:, :], two[:, :], 0.2, two[:, :], ALU.mult, ALU.max))
                c.step(nc.vector.tensor_tensor(two[:, :], v[:, :, h], v[:, :, H + h], ALU.add))
                c.step(nc.vector.scalar_tensor_tensor(m[:, :], two[:, :], 0.2, two[:, :], ALU.mult, ALU.max))
                c.step(nc.vector.scalar_tensor_tensor(own, keep[0][:, :], -BIG, m[:, :], ALU.mult, ALU.add))
                c.step(nc.vector.tensor_tensor(v[:, :, h], p[:, :], own, ALU.max))
                running(one[:, :], v[:, :, h], 0, 1)
                running(two[:, :], v[:, :, h], 1, 1)
                c.step(nc.vector.tensor_tensor(m[:, :], one[:, :], two[:, :], ALU.max))
                nc.vector.tensor_tensor(own, own, m[:, :], ALU.subtract)
                nc.vector.tensor_tensor(p[:, :], p[:, :], m[:, :], ALU.subtract).then_inc(s["shifted"], 1)
                dve.wait_ge(s["exp_made"], h + 1 + UP)
                c.step(nc.vector.tensor_tensor(v[:, :, h], p[:, :], own, ALU.add))
                running(one[:, :], v[:, :, h], 0, 0)
                running(two[:, :], v[:, :, h], 1, 0)
                c.step(nc.vector.tensor_tensor(m[:, :], one[:, :], two[:, :], ALU.add))
                c.step(nc.vector.tensor_tensor(m[:, :], m[:, :], v[:, :, h], ALU.subtract))
                c.step(nc.vector.tensor_scalar(m[:, :], m[:, :], 1e-16, None, ALU.add))
                c.step(nc.vector.reciprocal(m[:, :], m[:, :]))
                nc.vector.tensor_tensor(own, own, m[:, :], ALU.mult).then_inc(s["loops_made"], 1)
                nc.vector.tensor_tensor(v[:, :, h], p[:, :], m[:, :], ALU.mult).then_inc(s["alpha_made"], 1)
            c.step(nc.vector.memset(run[:, :], 0.0))
            to_tile_columns(nc, None, dve, "dve", [(v[:, :, h], F32) for h in range(H)], ps, packed, k.ident,
                            s["turned"], s["evacuated"])

        @block.scalar
        def _(act):
            for h in range(H):
                act.wait_ge(s["shifted"], h + 1 + UP)
                nc.scalar.activation(alone[:, :, h], alone[:, :, h], ACT.Exp)
                nc.scalar.activation(p[:, :], p[:, :], ACT.Exp).then_inc(s["exp_made"], 1)

        @block.tensor
        def _(pe):
            n = 0

            def answer(out, lhs_t, rhs):
                nonlocal n
                pe.wait_ge(s["asked"], n + 1 + UP)
                nc.tensor.matmul(out, lhs_t, rhs, start=True, stop=True).then_inc(s["answered"], 1)
                n += 1
            for i in range(4):
                answer(ps_line[:, :], totals[:, i:i + 1], k.ident[0:ROWS, 0:ROWS])
            for h in range(H):
                for back in BACK:
                    answer(ps_line[:, :], last[:, :], k.ident[0:ROWS, 0:ROWS])
                    at = 2 if back else 0
                    answer(ps_col[:, :], run[:, at:at + ROWS], k.ones[0:1, 0:1])
            assert n == requests
            pe.wait_ge(s["alpha_made"], H + UP)
            to_tile_columns(nc, pe, None, "pe", [(v[:, :, h], F32) for h in range(H)], ps, packed, k.ident,
                            s["turned"], s["evacuated"])


def sum_weighted_rows(nc, sb, psum, sem, k, F, H, edge_meta, bases, rows_in, alphas, keeping=None):
    WROW = F + H
    rows_loaded, alpha_loaded, rows_scaled = ([sem(f"gat_{x}{h}") for h in range(2)] for x in
                                              ("rows_loaded", "alpha_loaded", "rows_scaled"))
    rows = [sb(f"rows{h}", [P, TPR, WROW], F32) for h in range(2)]
    alpha = [sb(f"alpha{h}", [P, H * TPR], F32) for h in range(2)]
    sums = SumPass(nc, sb, psum, sem, k, "gat", bases, F, weights=lambda sums, h: alpha[h] if H == 1 else None,
                   weights_loaded=alpha_loaded if H == 1 else None)
    extra = KeptRows(nc, sb, sem, k, *keeping) if keeping else None
    scaled = [sb(f"scaled{h}", [P, TPR, F], F32) for h in range(2)] if H > 1 else None
    with k.block() as block:
        @block.sync
        def _(sp):
            sums.load_bases(sp)
            with sp.Fori(0, ROWS // 2) as it:
                for h in range(2):
                    sums.load_meta(sp, it, h, edge_meta)
                    if H > 1:
                        sp.wait_ge(rows_scaled[h], it + UP)
                    else:
                        sums.wait_read(sp, it, h)
                    sp.dma_start(rows[h][:, :, :], rows_in[it * 2 + h]).then_inc(rows_loaded[h], 16)
                    sp.dma_start(alpha[h][:, :], alphas[it * 2 + h]).then_inc(alpha_loaded[h], 16)
                    if extra:
                        extra.sp(sp, it, h)

        @block.vector
        def _(dve):
            sums.start_dve(dve)

            def add_group(it, h, at, between):
                for pair in range(PAIRS):
                    sums.add_pair(dve, it, h, pair, at[pair])
                    between(pair)
            sums.groups(dve, add_group)

        if extra:
            @block.scalar
            def _(act):
                with act.Fori(0, ROWS // 2) as it:
                    for h in range(2):
                        extra.act(act, it, h)
                extra.finish(act)

        @block.gpsimd
        def _(pool):
            with pool.Fori(0, ROWS // 2) as it:
                for h in range(2):
                    if H > 1:
                        pool.wait_ge(rows_loaded[h], it * 16 + 16 + UP)
                        pool.wait_ge(alpha_loaded[h], it * 16 + 16 + UP)
                        sums.wait_read(pool, it, h)
                        nc.gpsimd.tensor_tensor(
                            scaled[h][:, :, :].rearrange("p t (h c) -> p t h c", h=H),
                            rows[h][:, :, 0:F].rearrange("p t (h c) -> p t h c", h=H),
                            alpha[h][:, :].rearrange("p (h t o) -> p t h o", h=H, o=1).to_broadcast([P, TPR, H, F // H]),
                            ALU.mult).then_inc(rows_scaled[h], 1)
                    if extra:
                        extra.pool(pool, it, h)

        @block.tensor
        def _(pe):
            with pe.Fori(0, ROWS // 2) as it:
                for h in range(2):
                    pe.wait_ge(sums.hots[h], it + 1 + UP)
                    if H > 1:
                        pe.wait_ge(rows_scaled[h], it + 1 + UP)
                        source = lambda t: scaled[h][:, t, :]
                    else:
                        pe.wait_ge(rows_loaded[h], it * 16 + 16 + UP)
                        source = lambda t: rows[h][:, t, 0:F]
                    for pair in range(PAIRS):
                        sums.sum_pair(pe, it, h, pair, source)

def largest_messages(nc, sb, psum, sem, k, edge_meta, flags, table, w_edge, best_rows):
    meta = [sb(f"meta{h}", [P, 2 * TPR], F32) for h in range(2)]
    rows = [sb(f"rows{h}", [P, TPR, D], F32) for h in range(2)]
    back = [sb(f"back{h}", [P, TPR * D], F32) for h in range(2)]
    first = sb("first", [ROWS, COLS], F32)
    drop = sb("drop", [ROWS, COLS], BF16)
    pick = [sb(f"pick{i}", [ROWS, P], BF16) for i in range(2)]
    wide = sb("wide", [P, D], F32)
    rows_t, best = ([sb(f"{x}{i}", [P, 4 * P], F32) for i in range(2)] for x in ("rows_t", "best"))
    ps_d, ps_m, ps_b = ([psum(f"{x}{i}", [P, 4 * P], F32) for i in range(2)] for x in ("ps_d", "ps_m", "ps_b"))
    gathered, g0 = k.pool_dma.take(ROWS // 2 * 16 * TPR)
    meta_loaded, mixed, picked, stored = ([sem(f"l3_{x}{h}") for h in range(2)] for x in ("meta_loaded", "mixed", "picked", "stored"))
    turned, copied, spread, best_made, back_turned, back_copied = (
        [sem(f"l3_{x}{i}") for i in range(2)] for x in ("turned", "copied", "spread", "best_made", "back_turned", "back_copied"))
    ready, drop_made = sem("l3_ready"), sem("l3_drop_made")
    CH = TPR // 4
    by_group = best_rows.rearrange("(g t p) f -> g p t f", t=TPR, p=P)

    def nth(q, c):
        return q * (CH // 2) + c // 2
    with k.block() as block:
        @block.sync
        def _(sp):
            sp.dma_start(first[:, :], flags[0]).then_inc(ready, 16)
            sp.dma_start(wide[:, :], w_edge.to_broadcast([P, D])).then_inc(ready, 16)
            with sp.Fori(0, ROWS // 2) as it:
                for h in range(2):
                    sp.wait_ge(gathered[h], it * (16 * TPR) + g0[h])
                    sp.sem_inc(k.held, 1)
                    sp.wait_ge(mixed[h], it * CH + UP)
                    sp.dma_start(meta[h][:, :], edge_meta[it * 2 + h, :, 0:2 * TPR]).then_inc(meta_loaded[h], 16)

        @block.gpsimd
        def _(pool):
            with pool.Fori(0, ROWS // 2) as it:
                for h in range(2):
                    pool.wait_ge(meta_loaded[h], it * 16 + 16 + UP)
                    for i in range(2):
                        pool.wait_ge(turned[i], (it * 2 + h - 1) * (CH // 2) + UP)
                    pool.sem_inc(k.turns, 1)
                    index = meta[h][:, :].bitcast(U32)
                    for t in range(TPR):
                        pool.indirect_dma_start(out=rows[h][:, t, :], out_offset=None, in_=table,
                                                in_offset=bass.IndirectOffsetOnAxis(ap=index[:, t:t + 1], axis=0)
                                                ).then_inc(gathered[h], 16)

        @block.tensor
        def _(pe):
            pe.wait_ge(drop_made, 2 + UP)
            with pe.Fori(0, ROWS // 2) as it:
                for h in range(2):
                    q = it * 2 + h
                    pe.wait_ge(picked[h], it + 1 + UP)
                    for step in range(CH + 1):
                        c = step
                        if c < CH:
                            i = c % 2
                            pe.wait_ge(best_made[i], nth(q, c) + UP)
                            nc.tensor.matmul(ps_d[i][:, :], pick[h][:, :], drop[:, c * 4 * P:(c + 1) * 4 * P],
                                             start=True, stop=True).then_inc(spread[i], 1)
                            pe.wait_ge(mixed[h], it * CH + (c + 1) + UP)
                            pe.wait_ge(copied[i], nth(q, c) + UP)
                            for j in range(4):
                                last = nc.tensor.transpose(ps_m[i][:, j * P:(j + 1) * P], rows[h][:, 4 * c + j, :], k.ident[:, :])
                            last.then_inc(turned[i], 1)
                        c = step - 1
                        if c >= 0:
                            i = c % 2
                            pe.wait_ge(best_made[i], nth(q, c) + 1 + UP)
                            pe.wait_ge(back_copied[i], nth(q, c) + UP)
                            for j in range(4):
                                last = nc.tensor.transpose(ps_b[i][:, j * P:(j + 1) * P], best[i][:, j * P:(j + 1) * P], k.ident[:, :])
                            last.then_inc(back_turned[i], 1)

        @block.scalar
        def _(act):
            with act.Fori(0, ROWS // 2) as it:
                for h in range(2):
                    q = it * 2 + h
                    act.wait_ge(spread[1], q * (CH // 2) + UP)
                    nc.scalar.copy(pick[h][:, :], k.ident[0:ROWS, bass.ds(q, 1)].to_broadcast([ROWS, P])).then_inc(picked[h], 1)
                    act.wait_ge(stored[h], it * 16 + UP)
                    for step in range(CH + 1):
                        c = step
                        if c < CH:
                            i = c % 2
                            act.wait_ge(turned[i], nth(q, c) + 1 + UP)
                            act.wait_ge(best_made[i], nth(q, c) + UP)
                            nc.scalar.copy(rows_t[i][:, :], ps_m[i][:, :]).then_inc(copied[i], 1)
                        c = step - 1
                        if c >= 0:
                            i = c % 2
                            act.wait_ge(back_turned[i], nth(q, c) + 1 + UP)
                            nc.scalar.copy(back[h][:, c * 4 * P:(c + 1) * 4 * P], ps_b[i][:, :]).then_inc(back_copied[i], 1)
                    for i in range(2):
                        act.wait_ge(back_copied[i], (q + 1) * (CH // 2) + UP)
                    act.dma_start(by_group[q], back[h][:, :].rearrange("p (t f) -> p t f", t=TPR)).then_inc(stored[h], 16)
            for h in range(2):
                act.wait_ge(stored[h], ROWS // 2 * 16 + UP)

        @block.vector
        def _(dve):
            dve.wait_ge(ready, 32 + UP)
            nc.vector.memset(best[1][:, :], -BIG).then_inc(drop_made, 1)
            nc.vector.tensor_scalar(drop[:, :], first[:, :], -BIG, None, ALU.mult).then_inc(drop_made, 1)
            dve.wait_ge(drop_made, 2 + UP)
            with dve.Fori(0, ROWS // 2) as it:
                for h in range(2):
                    q = it * 2 + h
                    dve.wait_ge(gathered[h], it * (16 * TPR) + (g0[h] + 16 * TPR))
                    for t in range(TPR):
                        ins = nc.vector.scalar_tensor_tensor(rows[h][:, t, :], wide[:, :], meta[h][:, TPR + t:TPR + t + 1],
                                                             rows[h][:, t, :], ALU.mult, ALU.add)
                        if t % 4 == 3:
                            ins.then_inc(mixed[h], 1)
                    for c in range(CH):
                        i = c % 2
                        dve.wait_ge(spread[i], nth(q, c) + 1 + UP)
                        dve.wait_ge(copied[i], nth(q, c) + 1 + UP)
                        dve.wait_ge(back_turned[i], nth(q, c) + UP)
                        dve.wait_ge(best_made[1 - i], nth(q, c) + i + UP)
                        nc.vector.tensor_tensor_scan(best[i][:, :], ps_d[i][:, :], rows_t[i][:, :],
                                                     best[1 - i][:, 4 * P - 1:4 * P], ALU.add, ALU.max).then_inc(best_made[i], 1)


def copy_padded(nc, sb, psum, sem, k, src, dst, rows, total):
    done, zeroed = sem("copy_done"), sem("copy_zeroed")
    fill = total > rows
    z = sb("zeros", [total - rows, src.shape[1]], F32) if fill else None
    with k.block() as block:
        @block.sync
        def _(sp):
            sp.dma_start(dst[0:rows, :], src[0:rows, :]).then_inc(done, 16)
            if fill:
                sp.wait_ge(zeroed, 1 + UP)
                sp.dma_start(dst[rows:total, :], z[:, :]).then_inc(done, 16)
            sp.wait_ge(done, (32 if fill else 16) + UP)
        if fill:
            @block.vector
            def _(dve):
                nc.vector.memset(z[:, :], 0.0).then_inc(zeroed, 1)


def clear_rows(nc, sb, psum, sem, k, tensors):
    done, zeroed = sem("clear_done"), sem("clear_zeroed")
    width = (EP + P) // P * 2 * HEADS
    z = sb("zeros", [P, width], F32)
    with k.block() as block:
        @block.vector
        def _(dve):
            nc.vector.memset(z[:, :], 0.0).then_inc(zeroed, 1)

        @block.sync
        def _(sp):
            sp.wait_ge(zeroed, 1 + UP)
            for x in tensors:
                h = x.shape[1]
                sp.dma_start(x.rearrange("(p c) h -> p (c h)", p=P), z[:, 0:(EP + P) // P * h]).then_inc(done, 16)
            sp.wait_ge(done, 16 * len(tensors) + UP)


class PoolDmas:

    def __init__(self, make):
        self.make, self.counts, self.sems = make, [1 << 16] * 2, None

    def take(self, each, slots=2):
        if max(self.counts) + each >= 1 << 16:
            self.sems, self.counts = self.make(), [16, 16]
        before = list(self.counts)
        for i in range(slots):
            self.counts[i] += each
        return self.sems, before


class Store:
    pass


def gnn_kernel(nc, x, src, dst, edge_attr_128, edge_weight, L0_gnn_weight, L0_gnn_bias, L1_gnn_W1, L1_gnn_as1, L1_gnn_ad1,
               L1_gnn_b1, L1_gnn_W2, L1_gnn_as2, L1_gnn_ad2, L1_gnn_b2, L1_gnn_W3, L1_gnn_as3, L1_gnn_ad3, L1_gnn_b3,
               L2_gnn_W_node, L2_gnn_b_node, L2_gnn_W_gate, L2_gnn_b_gate, L2_gnn_W_filt, L2_gnn_b_filt, L2_gnn_bn_gamma,
               L2_gnn_bn_beta, L2_gnn_bn_mean, L2_gnn_bn_var, L3_gnn_Wm, L3_gnn_bm, L3_gnn_W1, L3_gnn_b1, L3_gnn_W2,
               L3_gnn_b2, out):
    def dram(name, shape, dt=F32):
        return nc.dram_tensor(name, shape, dt, kind="Internal").ap()

    def by_group(t):
        return t.rearrange("(g b p) f -> g p b f", b=GROUP, p=P)

    xs = [dram(f"x{i}", (NP, D)) for i in range(5)]
    own = dram("own", (NP, 2 * D))
    sort_meta = dram("sort_meta", (ROWS, P, 8 * TPR))
    key_rows = {key: dram(f"key_rows_{key}", (ROWS, 2, COLS), BF16) for key in ("src", "dst")}
    ordered = {key: dram(f"ordered_{key}", (EP, 4)) for key in ("src", "dst")}
    meta = {key: dram(f"meta_{key}", (ROWS, P, 4 * TPR)) for key in ("src", "dst")}
    bases = {key: dram(f"bases_{key}", (1, ROWS * PAIRS), I32) for key in ("src", "dst")}
    flags = {key: dram(f"flags_{key}", (2, ROWS, COLS)) for key in ("src", "dst")}
    table_l0, table_l2, table_l3 = (dram(f"table_{i}", (NP, D)) for i in ("l0", "l2", "l3"))
    gated, gated_kept = dram("gated", (E, D)), dram("gated_kept", (ROWS, P, TPR * D))
    best_rows = dram("best_rows", (EP, D))
    sums = dram("sums", (ORD, D))
    rows_kept = [dram(f"rows_kept{i}", (ROWS, P, TPR * w)) for i, w in ((0, HEADS * HID + HEADS), (1, D + 1))]
    gat = ((L1_gnn_W1, L1_gnn_as1, L1_gnn_ad1, L1_gnn_b1, D), (L1_gnn_W2, L1_gnn_as2, L1_gnn_ad2, L1_gnn_b2, HEADS * HID),
           (L1_gnn_W3, L1_gnn_as3, L1_gnn_ad3, L1_gnn_b3, HEADS * HID))
    heads = [a.shape[0] for _, a, _, _, _ in gat]
    width = [w.shape[1] for w, _, _, _, _ in gat]
    folded = [dram(f"folded{i}", (gat[i][4], width[i] + 2 * heads[i])) for i in range(3)]
    gat_table = [dram(f"gat_table{i}", (NP, width[i] + heads[i])) for i in range(3)]
    placed = [dram(f"placed{i}", (EP + P, 2 * h)) for i, h in ((0, HEADS), (1, 1))]
    loop_alphas = [dram(f"loop_alphas{i}", (EP + P, h)) for i, h in ((0, HEADS), (1, 1))]
    scores = [dram(f"scores{i}", (ROWS, TPR * h, P)) for i, h in ((0, HEADS), (1, 1))]
    alphas = [dram(f"alphas{i}", (ROWS, P, h * TPR)) for i, h in ((0, HEADS), (1, 1))]

    with ExitStack() as ctx:
        phases = [0]
        used = []

        def sem(name):
            used.append(nc.alloc_semaphore(name=f"{name}_{phases[0]}"))
            new.append(used[-1])
            return used[-1]

        def keep(name, shape, dt=F32):
            return ctx.enter_context(nc.sbuf_tensor(name, shape, dt))

        k = Store()
        k.iota, k.spare, k.eid = keep("iota", [P, WIN]), keep("spare", [P, 1]), keep("edge_number", [ROWS, COLS])
        k.number, k.joiner = keep("number", [P, 1]), keep("joiner", [2, 1])
        k.ones, k.ident, k.before, k.after = (keep(n, [P, P]) for n in ("ones", "ident", "before", "after"))
        cnt, start = ({key: keep(f"{n}_{key}", [P, NB]) for key in ("src", "dst")} for n in ("cnt", "start"))
        has_dst, last_of = keep("has_dst", [P, NB]), keep("last_of", [P, NB], U32)
        row_of, spot = ({key: keep(f"{n}_{key}", [P, NB], U32) for key in ("src", "dst")} for n in ("row_of", "spot"))
        new, new_dma = [], []

        def raised_block():
            for s in new:
                nc.gpsimd.sem_inc(s, UP)
            for s in new_dma:
                nc.gpsimd.dma_start(k.primed[:, :], k.number[:, :]).then_inc(s, 16)
                nc.gpsimd.wait_ge(s, 16)
            new.clear()
            new_dma.clear()
            nc.all_engine_barrier()
            return nc.Block()
        k.block = raised_block

        def lasting(name):
            new_dma.append(nc.alloc_semaphore(name=name))
            return new_dma[-1]
        k.primed = keep("primed", [P, 1])
        k.held = nc.alloc_semaphore(name="waits_held")
        k.turns = nc.alloc_semaphore(name="pool_turns")
        k.pool_dma = PoolDmas(lambda: [lasting(f"pool_dma{h}_{phases[0]}") for h in range(2)])

        def run(phase, *args, **kw):
            phases[0] += 1
            tag = f"p{phases[0]}_"
            with ExitStack() as st:
                phase(nc, lambda n, s, d: st.enter_context(nc.sbuf_tensor(tag + n, s, d)),
                      lambda n, s, d: st.enter_context(nc.psum_tensor(tag + n, s, d)), sem, k, *args, **kw)
            nc.clear_and_free_semaphores(used)
            nc.all_engine_barrier()
            used.clear()

        run(make_constants)
        run(copy_padded, x, xs[0], N, NP)
        run(clear_rows, placed)
        run(stage_edges, src, dst, edge_weight, sort_meta, list(key_rows.values()))
        for key in ("src", "dst"):
            run(count_keys, key, sort_meta, cnt[key])
            run(node_offsets, key, cnt[key], start[key], row_of[key], spot[key])
            run(sort_edges, key, sort_meta, key_rows[key], start[key], ordered[key])
            run(lay_out_segments, key, ordered[key], meta[key], bases[key], flags[key])
        for i, (w, a_src, a_dst, _, K) in enumerate(gat):
            run(fold_attention, i, w, a_src, a_dst, K, folded[i])
        epoch = [0]

        def edge_pass(phase, *args):
            with ExitStack() as held:
                k.acc = held.enter_context(nc.sbuf_tensor(f"acc{epoch[0]}", [P, ORD], F32))
                run(phase, *args)
                run(unload_sums, k.acc, sums)
            epoch[0] += 1

        xg = [by_group(t) for t in xs]
        run(update_nodes, mode="first", weights=[L0_gnn_weight], biases=(None, ()), K=D, x_in=xg[0],
            tables=[(by_group(table_l0), 0, D)])
        edge_pass(gather_and_sum, meta["src"], bases["src"], table_l0)
        for i, (_, _, _, b, K) in enumerate(gat):
            F, H = width[i], heads[i]
            j = 0 if i < 2 else 1
            tables = [(by_group(gat_table[i]), 0, F + H)]
            if i == 0:
                run(update_nodes, mode="residual", weights=[folded[0]], biases=(L0_gnn_bias, ()), K=K,
                    x_in=xg[0], x_out=xg[1], sums=sums, row_of=row_of["src"], tables=tables, spot=spot["dst"], placed=placed[j])
            else:
                run(update_nodes, mode="elu", weights=[folded[i]], biases=(gat[i - 1][3], ()), K=K,
                    sums=sums, row_of=row_of["dst"], tables=tables, spot=spot["dst"], placed=placed[j],
                    extra=by_group(gat_table[i - 1][:, 0:width[i - 1]]), loop=(heads[i - 1], loop_alphas[0]))
            filters = (edge_attr_128, gated, (0, E - ROWS // 2 * COLS)[i], L2_gnn_W_gate, L2_gnn_b_gate, L2_gnn_W_filt,
                       L2_gnn_b_filt) if i < 2 else None
            keeping = (gated, meta["src"], gated_kept, (i - 1) * ROWS // 2) if i else None
            run(gather_rows, F, H, meta["dst"], gat_table[i], rows_kept[j], scores[j], filters)
            run(softmax_by_segment, H, flags["dst"], scores[j], placed[j], alphas[j], loop_alphas[j])
            edge_pass(sum_weighted_rows, F, H, meta["dst"], bases["dst"], rows_kept[j], alphas[j], keeping)
        run(update_nodes, mode="residual", weights=[L2_gnn_W_node], biases=(gat[2][3], ((L2_gnn_b_node, D),)), K=D,
            x_in=xg[1], x_out=xg[2], sums=sums, row_of=row_of["dst"], tables=[(by_group(table_l2), 0, D)],
            extra=by_group(gat_table[2][:, 0:D]), loop=(1, loop_alphas[1]), spot=spot["dst"])
        edge_pass(gather_and_sum, meta["src"], bases["src"], table_l2, gated_kept)
        w3 = dram("w3", (D, 3 * D))
        run(join_weights, w3, (L3_gnn_Wm[D:2 * D, :], L3_gnn_Wm[0:D, :], L3_gnn_W1[0:D, :]))
        run(update_nodes, mode="norm", weights=[w3], biases=(None, ((None, D), (L3_gnn_bm, D), (L3_gnn_b1, D))),
            K=D, x_in=xg[2], x_out=xg[3], sums=sums, row_of=row_of["src"], extra=by_group(table_l2),
            tables=[(by_group(table_l3), 0, D), (by_group(own), D, 2 * D)],
            norm=(L2_gnn_bn_gamma, L2_gnn_bn_beta, L2_gnn_bn_mean, L2_gnn_bn_var), cnt=cnt["src"])
        run(largest_messages, meta["dst"], flags["dst"], table_l3, L3_gnn_Wm[2 * D:2 * D + 1, :], best_rows)
        run(find_last_edges, cnt["dst"], start["dst"], has_dst, last_of)
        run(finish_nodes, x_in=xg[3], own=by_group(own), sums=best_rows, row_of=last_of, has=has_dst,
            w1b=L3_gnn_W1[D:2 * D, :], w2=L3_gnn_W2, b2=L3_gnn_b2, x_out=xg[4])
        run(copy_padded, xs[4], out, N, N)


def join_weights(nc, sb, psum, sem, k, joined, parts):
    done = sem("weights_joined")
    with k.block() as block:
        @block.sync
        def _(sp):
            for i, w in enumerate(parts):
                sp.dma_start(joined[:, i * D:(i + 1) * D], w).then_inc(done, 16)
            sp.wait_ge(done, 16 * len(parts) + UP)


def find_last_edges(nc, sb, psum, sem, k, cnt, start, has, last_of):
    made, at = sem("last_made"), sb("at", [P, NB], F32)
    with k.block() as block:
        @block.vector
        def _(dve):
            c = Chain(dve, made)
            nc.vector.tensor_scalar(has[:, :], cnt[:, :], 0.0, None, ALU.is_gt)
            c.step(nc.vector.scalar_tensor_tensor(at[:, :], cnt[:, :], -1.0, start[:, :], ALU.add, ALU.add))
            c.step(nc.vector.tensor_tensor(last_of[:, :], at[:, :], has[:, :], ALU.mult))


_INS = ['x', 'src', 'dst', 'edge_attr_128', 'edge_weight', 'L0_gnn_weight', 'L0_gnn_bias', 'L1_gnn_W1', 'L1_gnn_as1',
        'L1_gnn_ad1', 'L1_gnn_b1', 'L1_gnn_W2', 'L1_gnn_as2', 'L1_gnn_ad2', 'L1_gnn_b2', 'L1_gnn_W3', 'L1_gnn_as3',
        'L1_gnn_ad3', 'L1_gnn_b3', 'L2_gnn_W_node', 'L2_gnn_b_node', 'L2_gnn_W_gate', 'L2_gnn_b_gate', 'L2_gnn_W_filt',
        'L2_gnn_b_filt', 'L2_gnn_bn_gamma', 'L2_gnn_bn_beta', 'L2_gnn_bn_mean', 'L2_gnn_bn_var', 'L3_gnn_Wm',
        'L3_gnn_bm', 'L3_gnn_W1', 'L3_gnn_b1', 'L3_gnn_W2', 'L3_gnn_b2']


def kernel(**inputs):
    import numpy as _np
    import concourse.bacc as _bacc
    from concourse import mybir as _mybir
    from concourse.bass_utils import run_bass_kernel_spmd as _run

    nc = _bacc.Bacc("TRN2", target_bir_lowering=False, num_devices=1)
    arrays, args = {}, []
    for name in _INS:
        a = _np.ascontiguousarray(inputs[name])
        arrays[f"in_{name}"] = a
        args.append(nc.dram_tensor(f"in_{name}", a.shape, _mybir.dt.from_np(a.dtype), kind="ExternalInput").ap())
    args.append(nc.dram_tensor("out_0", (N, D), F32, kind="ExternalOutput").ap())
    gnn_kernel(nc, *args)
    r = _run(nc, [arrays], core_ids=[0])
    return r.results[0]["out_0"]
```
